# Optimizing a Trainium2 kernel written in Bass

```python
import numpy as np
import jax
import jax.numpy as jnp

def _softmax(x, axis=-1):
    return jax.nn.softmax(x, axis=axis)
def _gelu(x):
    return jax.nn.gelu(x, approximate=True)
def _silu(x):
    return jax.nn.silu(x)
def _sigmoid(x):
    return jax.nn.sigmoid(x)
def _layernorm(x, axis=-1, eps=1e-5):
    m = jnp.mean(x, axis=axis, keepdims=True)
    v = jnp.var(x, axis=axis, keepdims=True)
    return (x - m) / jnp.sqrt(v + eps)
def _scatter_add(tgt, idx, src, axis=0):
    return tgt.at[idx].add(src)
def _segment_sum(src, seg, n):
    return jax.ops.segment_sum(src, seg, n)

kernel_name = 'mk_adj_ffn_d1_adj_256_9159a9'

def setup_inputs(seed: int = 0):
    np.random.seed(seed)
    _w = jnp.asarray
    def _rec_inputs():
        import jax
        import jax.numpy as jnp
        _gk = jax.random.key(seed)
        x = -0.0002928 + 1 * jax.random.normal(jax.random.fold_in(_gk, 1), (8, 2048, 256), jnp.float32)
        _w = (1.0 + jnp.arange(2048, dtype=jnp.float32)) ** -0.5
        _w = _w / _w.mean()
        _pij = jnp.clip(0.00390625 * _w[:, None] * _w[None, :], 0.0, 1.0)
        _a = jax.random.uniform(jax.random.fold_in(_gk, 2), (2048, 2048)) < _pij
        adj = _a.astype(jnp.int32)
        return x, adj
    x, adj = _rec_inputs()
    def _L0_gnn_setup():
        import jax, jax.numpy as jnp
        import numpy as np
        NEG_BIG = -9000000000000000.0
        key = jax.random.key(seed)
        k1, k2, k3, k4 = jax.random.split(key, 4)
        bs, N, Fin, Fout = (8, 2048, 256, 256)
        x = jax.random.normal(k1, (bs, N, Fin), dtype=jnp.float32)
        adj = jax.random.randint(k2, (N, N), 0, 2, dtype=jnp.int32)
        W = jax.random.normal(k3, (Fin, Fout), dtype=jnp.float32) * (1.414 / np.sqrt(Fin))
        a = jax.random.normal(k4, (2 * Fout, 1), dtype=jnp.float32) * 0.1
        return {'x': x, 'adj': adj, 'W': W, 'a': a}
    _L0_gnn_all = _L0_gnn_setup()
    _L0_gnn_in = {k: v for k, v in _L0_gnn_all.items() if k in ('W', 'a', )}
    del _L0_gnn_all

    def _L0_ffn_setup():
        import jax, jax.numpy as jnp
        import numpy as np
        E, D, H, TOP_K = (6, 256, 256, 2)
        ROUTER_H = D // 2
        key = jax.random.key(seed)
        ks = jax.random.split(key, 12)
        s = 1.0 / np.sqrt(D)
        sh = 1.0 / np.sqrt(H)
        sr = 1.0 / np.sqrt(ROUTER_H)
        return {'features': jax.random.normal(ks[0], (8, 4096, D), dtype=jnp.float32), 'router_w1': jax.random.uniform(ks[1], (D, ROUTER_H), jnp.float32, -s, s), 'router_b1': jnp.zeros((ROUTER_H,), jnp.float32), 'router_w2': jax.random.uniform(ks[2], (ROUTER_H, E), jnp.float32, -sr, sr), 'router_b2': jnp.zeros((E,), jnp.float32), 'expert_w1': jax.random.uniform(ks[3], (E, D, H), jnp.float32, -s, s), 'expert_b1': jnp.zeros((E, H), jnp.float32), 'expert_w2': jax.random.uniform(ks[4], (E, H, H), jnp.float32, -sh, sh), 'expert_b2': jnp.zeros((E, H), jnp.float32), 'expert_w3': jax.random.uniform(ks[5], (E, H, D), jnp.float32, -sh, sh), 'expert_b3': jnp.zeros((E, D), jnp.float32)}
    _L0_ffn_all = _L0_ffn_setup()
    _L0_ffn_in = {k: v for k, v in _L0_ffn_all.items() if k in ('router_w1', 'router_b1', 'router_w2', 'router_b2', 'expert_w1', 'expert_b1', 'expert_w2', 'expert_b2', 'expert_w3', 'expert_b3', )}
    del _L0_ffn_all

    return {
        "x": x,
        "adj": adj,
        "L0_gnn_W": _L0_gnn_in["W"],
        "L0_gnn_a": _L0_gnn_in["a"],
        "L0_ffn_router_w1": _L0_ffn_in["router_w1"],
        "L0_ffn_router_b1": _L0_ffn_in["router_b1"],
        "L0_ffn_router_w2": _L0_ffn_in["router_w2"],
        "L0_ffn_router_b2": _L0_ffn_in["router_b2"],
        "L0_ffn_expert_w1": _L0_ffn_in["expert_w1"],
        "L0_ffn_expert_b1": _L0_ffn_in["expert_b1"],
        "L0_ffn_expert_w2": _L0_ffn_in["expert_w2"],
        "L0_ffn_expert_b2": _L0_ffn_in["expert_b2"],
        "L0_ffn_expert_w3": _L0_ffn_in["expert_w3"],
        "L0_ffn_expert_b3": _L0_ffn_in["expert_b3"],
    }

def reference(x, adj, L0_gnn_W, L0_gnn_a, L0_ffn_router_w1, L0_ffn_router_b1, L0_ffn_router_w2, L0_ffn_router_b2, L0_ffn_expert_w1, L0_ffn_expert_b1, L0_ffn_expert_w2, L0_ffn_expert_b2, L0_ffn_expert_w3, L0_ffn_expert_b3):
    import jax
    import jax.numpy as jnp
    def _L0_gnn_ref(x, adj, W, a):
        import jax, jax.numpy as jnp
        import numpy as np
        NEG_BIG = -9000000000000000.0
        alpha = 0.2
        h = jnp.matmul(x, W)
        Fout = h.shape[-1]
        a1, a2 = (a[:Fout, 0], a[Fout:, 0])
        s1 = jnp.einsum('bnf,f->bn', h, a1)
        s2 = jnp.einsum('bnf,f->bn', h, a2)
        e = jax.nn.leaky_relu(s1[:, :, None] + s2[:, None, :], negative_slope=alpha)
        attention = jnp.where(adj[None, :, :] > 0, e, NEG_BIG)
        attention = jax.nn.softmax(attention, axis=-1)
        h_prime = jnp.matmul(attention, h)
        return jax.nn.elu(h_prime)

    def _L0_ffn_ref(features, router_w1, router_b1, router_w2, router_b2, expert_w1, expert_b1, expert_w2, expert_b2, expert_w3, expert_b3):
        import jax, jax.numpy as jnp
        import numpy as np
        E, D, H, TOP_K = (6, 256, 256, 2)
        ROUTER_H = D // 2
        rh = jax.nn.relu(features @ router_w1 + router_b1)
        expert_logits = jax.nn.softmax(rh @ router_w2 + router_b2, axis=-1)
        top_w, top_i = jax.lax.top_k(expert_logits, TOP_K)
        routing_weights = jax.nn.softmax(top_w, axis=-1)
        h1 = jax.nn.relu(jnp.einsum('bsd,edh->bseh', features, expert_w1) + expert_b1)
        h2 = jax.nn.relu(jnp.einsum('bseh,ehf->bsef', h1, expert_w2) + expert_b2)
        expert_out = jnp.einsum('bsef,efo->bseo', h2, expert_w3) + expert_b3
        sel = jnp.take_along_axis(expert_out, top_i[:, :, :, None], axis=2)
        combined = jnp.sum(sel * routing_weights[..., None], axis=2)
        return combined

    x = x + _L0_gnn_ref(_layernorm(x, axis=-1), adj, L0_gnn_W, L0_gnn_a)
    x = x + _L0_ffn_ref(_layernorm(x, axis=-1), L0_ffn_router_w1, L0_ffn_router_b1, L0_ffn_router_w2, L0_ffn_router_b2, L0_ffn_expert_w1, L0_ffn_expert_b1, L0_ffn_expert_w2, L0_ffn_expert_b2, L0_ffn_expert_w3, L0_ffn_expert_b3)
    return x


_drawn_inputs = setup_inputs


def setup_inputs(seed=0):
    import zlib

    import numpy as np

    out = dict(_drawn_inputs(seed))
    spreads = {'L0_ffn_router_b1': (0.0, 0.1),
     'L0_ffn_router_b2': (0.0, 0.1),
     'L0_ffn_expert_b1': (0.0, 0.8),
     'L0_ffn_expert_b2': (0.0, 0.358),
     'L0_ffn_expert_b3': (0.0, 0.1)}
    factors = {}
    for name, (base, spread) in spreads.items():
        noise = np.random.default_rng([zlib.crc32(name.encode()), seed]).standard_normal(out[name].shape)
        drawn = base * np.exp(spread * noise) if base else spread * noise
        out[name] = jnp.asarray(drawn.astype(out[name].dtype))
    for name, factor in factors.items():
        out[name] = (out[name] * factor).astype(out[name].dtype)
    return out
```

```python
from contextlib import ExitStack

import numpy as np

import concourse.bass as bass
from concourse import mybir

ALU = mybir.AluOpType
ACT = mybir.ActivationFunctionType
AX = mybir.AxisListType
RMAX = bass.bass_isa.ReduceOp.max
F32 = mybir.dt.float32
F32R = mybir.dt.float32r
BF16 = mybir.dt.bfloat16
U8 = mybir.dt.uint8
I32 = mybir.dt.int32
U32 = mybir.dt.uint32

P = 128
BATCH, NODES, FEAT = 8, 2048, 256
TOKENS = BATCH * NODES
KF = FEAT // P
TILES = TOKENS // P
BT = NODES // P
GT = 2
GROUPS = TILES // GT
BG = BT // GT
GW = GT * P
EXPERTS, LAYERS, RH = 6, 3, 128
TOPK = 2
ROW = FEAT + 4
C_W2, C_DW, C_TOKEN, C_FIRST = range(FEAT, ROW)
CHUNK = 1024
CU = CHUNK // P
HALF = 512
HU = HALF // P
CHUNKS = TOPK * TOKENS // CHUNK + EXPERTS - 1
STRIDE = TOKENS + CHUNK
IDLE = EXPERTS * STRIDE
LIST_ROWS = IDLE + CHUNK
OUT_ROWS = TOKENS + CHUNK
CH = 4
NC = BT // CH
SLOTS = 2 * BT - CH
AHEAD = BG - 1
CENTER = 60.0
SLOPE = 0.2
EPS = 1e-5
SW = 2 * FEAT + 2


def at_least(eng, sem, value):
    if not (isinstance(value, int) and value <= 0):
        eng.wait_ge(sem, value)


def waits_apart(eng, passed, *waits):
    for sem, v in waits:
        at_least(eng, sem, v)
    eng.sem_inc(passed, 1)


def project_stage(nc, t, A):
    with ExitStack() as ctx:
        def sb(name, shape, dt):
            return ctx.enter_context(nc.sbuf_tensor(name, shape, dt))

        def sem(name):
            return ctx.enter_context(nc.semaphore(name))

        xin = sb("xin", [P, 2, GT, FEAT], F32)
        stats = sb("stats1", [P, 2, GT, 6], F32)
        meanvar = sb("meanvar1", [P, 2, GT, 2], F32)
        std = sb("std1", [P, 2, GT], F32)
        rstd = sb("rstd1", [P, 2, GT], F32)
        eps = sb("eps1", [P, 1], F32)
        xn = sb("xn1", [P, 2, GT, FEAT], F32)
        xT_hi = sb("xT_hi", [P, 2, KF, GW], F32R)
        xT_lo = sb("xT_lo", [P, 2, KF, GW], F32R)
        w = sb("w_f32", [P, KF, FEAT + 2], F32)
        w_hi = sb("w_hi", [P, KF, FEAT + 2], F32R)
        w_lo = sb("w_lo", [P, KF, FEAT + 2], F32R)
        arow = sb("arow", [P, 2, FEAT], F32)
        junk = sb("junk", [P, 2, KF, FEAT], F32)
        hsb = sb("hsb", [P, 2, GT, FEAT], F32)
        score = sb("score", [P, TILES, 2], F32)
        xsum = sb("xsum", [P, GROUPS, KF], F32)
        bsum = sb("bsum", [P, KF, BATCH], F32)
        hmean = sb("hmean", [BATCH, FEAT], F32)
        raw = sb("adj_raw", [P, 2, NODES], I32)
        adj_bf = sb("adj_bf", [P, 2, NODES], BF16)
        ones = sb("ones_bf", [P, 2], BF16)
        mx = sb("mx", [P, BATCH], F32)
        mb = sb("mb", [P, BATCH], F32)
        s1 = sb("s1", [P, TILES], F32)
        s1T = sb("s1T", [P, TILES], F32)
        rel = sb("rel", [P, TILES], F32)
        relc = sb("relc", [P, TILES], F32)
        q = sb("q", [P, TILES], F32)
        qs = sb("qs", [P, TILES], F32)
        qc = sb("qc", [P, TILES], F32)
        top = sb("top", [P, TILES], F32)

        ps_T = ctx.enter_context(nc.psum_tensor("ps_T", [P, 2, KF, GW], F32))
        ps_h = ctx.enter_context(nc.psum_tensor("ps_h", [P, 2, GT, 512], F32))
        ps_deg = ctx.enter_context(nc.psum_tensor("ps_deg", [P, BT, 2], F32))
        ps_misc = ctx.enter_context(nc.psum_tensor("ps_misc", [P, 512], F32))

        weights_in = sem("weights_in")
        x_in = [sem(f"x_in{i}") for i in range(2)]
        adj_in = [sem(f"adj_in{i}") for i in range(2)]
        consts = sem("consts")
        ident_zero = sem("ident_zero")
        ident_ready = sem("ident_ready")
        wa_ready = sem("wa_ready")
        whi_ready = sem("whi_ready")
        wlo_ready = sem("wlo_ready")
        stats_ready = sem("stats_ready")
        meanvar_ready = sem("meanvar_ready")
        stats_passed = sem("stats_passed")
        adj_passed = sem("adj_passed")
        std_ready = sem("std_ready")
        rstd_ready = sem("rstd_ready")
        xn_ready = sem("xn_ready")
        transposed = sem("transposed")
        xhi_ready = sem("xhi_ready")
        xlo_ready = sem("xlo_ready")
        h_ready = sem("h_ready")
        h_copied = sem("h_copied")
        h_saved = [sem(f"h_saved{i}") for i in range(2)]
        scores_copied = sem("scores_copied")
        adj_bytes = sem("adj_bytes")
        adj_halves = sem("adj_halves")
        deg_counted = sem("deg_counted")
        bsum_ready = sem("bsum_ready")
        hsum_ready = sem("hsum_ready")
        hmean_ready = sem("hmean_ready")
        rows_saved = sem("rows_saved")
        max_part = sem("max_part")
        max_ready = sem("max_ready")
        tail = sem("tail")
        exps_ready = sem("exps_ready")
        exp_in = sem("exp_in")
        s1_ready = sem("s1_ready")
        s1T_ready = sem("s1T_ready")
        s1T_copied = sem("s1T_copied")

        block = ctx.enter_context(nc.Block())

        def batches(eng, body):
            body(0)
            with eng.Fori(1, BATCH) as b:
                body(b)

        @block.sync
        def _(sp):
            sp.dma_start(w[:, :, 0:FEAT], A["W"].rearrange("(k p) f -> p k f", p=P)).then_inc(weights_in, 16)
            sp.dma_start(arow[:, :, :], A["a"].rearrange("(s f) one -> one s f", s=2).to_broadcast([P, 2, FEAT])
                         ).then_inc(weights_in, 16)

            def batch(b):
                for u in range(BG):
                    n = b * BG + u
                    at_least(sp, xn_ready, (n - 1) * GT)
                    sp.dma_start(xin[:, u % 2, :, :], A["x"][n]).then_inc(x_in[u % 2], 16)
                    if u % 4 == 0:
                        k = b * 2 + u // 4
                        at_least(sp, adj_halves, (k - 1) * 2)
                        sp.dma_start(raw[:, u // 4, :], A["adjT"][k]).then_inc(adj_in[u // 4], 16)
            batches(sp, batch)
            sp.wait_ge(s1T_copied, 1)
            sp.dma_start(A["s1_save"], s1T[:, :]).then_inc(rows_saved, 16)
            sp.wait_ge(hmean_ready, 1)
            sp.dma_start(A["hmean_rows"][:, 0, :], hmean[:, :]).then_inc(rows_saved, 16)
            sp.wait_ge(rows_saved, 32)

        @block.gpsimd
        def _(pool):
            pool.memset(t.ident[:, :], 0.0).then_inc(ident_zero, 1)
            pool.memset(ones[:, :], 1.0).then_inc(consts, 1)
            pool.memset(eps[:, :], EPS).then_inc(consts, 1)
            pool.wait_ge(ident_zero, 1)
            pool.affine_select(out=t.ident[:, :], in_=t.ident[:, :], compare_op=ALU.not_equal, fill=1.0,
                               base=0, pattern=[[-1, P]], channel_multiplier=1).then_inc(ident_ready, 1)

            def batch(b):
                for s in range(2):
                    k = b * 2 + s
                    waits_apart(pool, adj_passed, (adj_in[s], (b + 1) * 16), (deg_counted, k - 1))
                    pool.tensor_scalar(adj_bf[:, s, :], raw[:, s, :], 0.0, None, ALU.is_gt).then_inc(adj_halves, 1)
                    pool.wait_ge(adj_halves, 2 * k + 1)
                    pool.tensor_copy(t.adj[:, k, :], adj_bf[:, s, :]).then_inc(adj_halves, 1)
            batches(pool, batch)
            pool.wait_ge(max_part, 1)
            pool.partition_all_reduce(mb[:, :], mx[:, :], P, RMAX).then_inc(max_ready, 1)

        @block.tensor
        def _(pe):
            def transposes(n, s):
                at_least(pe, xlo_ready, n - 1)
                pe.wait_ge(xn_ready, (n + 1) * GT)
                for k in range(KF):
                    for u in range(GT):
                        last = pe.transpose(ps_T[:, s, k, u * P:(u + 1) * P], xn[:, s, u, k * P:(k + 1) * P],
                                            t.ident[:, :])
                last.then_inc(transposed, 1)

            def project(n, s):
                at_least(pe, scores_copied, n - 1)
                pe.wait_ge(xlo_ready, n + 1)
                for u in range(GT):
                    for i, (l, r) in enumerate([(xT_hi, w_hi), (xT_hi, w_lo), (xT_lo, w_hi)]):
                        for k in range(KF):
                            last = pe.matmul(ps_h[:, s, u, 0:FEAT + 2], l[:, s, k, u * P:(u + 1) * P], r[:, k, :],
                                             start=(i == 0 and k == 0), stop=(i == 2 and k == KF - 1))
                last.then_inc(h_ready, 1)

            def count(b, s):
                k = b * 2 + s
                pe.wait_ge(adj_halves, 2 * k + 1)
                for i in range(BT):
                    last = pe.matmul(ps_deg[:, i, :], adj_bf[:, s, i * P:(i + 1) * P], ones[:, :],
                                     start=(isinstance(b, int) and s == 0 and i == 0), stop=True,
                                     skip_group_check=True)
                last.then_inc(deg_counted, 1)

            def batch(b):
                for u in range(BG):
                    n = b * BG + u
                    transposes(n, u % 2)
                    if u or not isinstance(b, int):
                        project(n - 1, (u + 1) % 2)
                    if u % 4 == 3:
                        count(b, u // 4)
            pe.wait_ge(ident_ready, 1)
            pe.wait_ge(consts, 2)
            pe.wait_ge(wlo_ready, 1)
            batches(pe, batch)
            project(GROUPS - 1, 1)
            pe.wait_ge(bsum_ready, 1)
            for k in range(KF):
                last = pe.matmul(ps_misc[0:BATCH, 0:FEAT], bsum[:, k, :], w[:, k, 0:FEAT],
                                 start=(k == 0), stop=(k == KF - 1))
            last.then_inc(hsum_ready, 1)
            pe.wait_ge(s1_ready, 1)
            pe.wait_ge(hmean_ready, 1)
            pe.transpose(ps_misc[:, 0:TILES], s1[:, :], t.ident[:, :]).then_inc(s1T_ready, 1)

        @block.scalar
        def _(act):
            act.wait_ge(consts, 2)

            def rows(n, s):
                act.wait_ge(meanvar_ready, (n + 1) * GT)
                act.activation(std[:, s, :], meanvar[:, s, :, 1], ACT.Sqrt, bias=eps[:, 0:1]).then_inc(std_ready, 1)

            def split(n, s):
                act.wait_ge(transposed, n + 1)
                at_least(act, h_ready, n - 1)
                for k in range(KF):
                    last = act.activation(xT_hi[:, s, k, :], ps_T[:, s, k, :], ACT.Copy,
                                          accum_out=xsum[:, n, k:k + 1])
                last.then_inc(xhi_ready, 1)

            def save(n, s, n2):
                act.wait_ge(h_ready, n + 1)
                at_least(act, h_saved[s], n2 * 16)
                act.activation(hsb[:, s, :, :], ps_h[:, s, :, 0:FEAT], ACT.Copy).then_inc(h_copied, 1)
                act.activation(score[:, bass.ds(n * GT, GT), :], ps_h[:, s, :, FEAT:FEAT + 2], ACT.Copy
                               ).then_inc(scores_copied, 1)
                act.wait_ge(h_copied, n + 1)
                act.dma_start(A["h"][n], hsb[:, s, :, :]).then_inc(h_saved[s], 16)

            def batch(b):
                for u in range(BG):
                    n = b * BG + u
                    rows(n, u % 2)
                    if u or not isinstance(b, int):
                        split(n - 1, (u + 1) % 2)
                    if u > 1 or not isinstance(b, int):
                        save(n - 2, u % 2, b * (BG // 2) + (u - 2) // 2)
            batches(act, batch)
            split(GROUPS - 1, 1)
            save(GROUPS - 2, 0, GROUPS // 2 - 1)
            save(GROUPS - 1, 1, GROUPS // 2 - 1)
            act.wait_ge(exp_in, 1)
            act.activation(t.col_neg[:, :], rel[:, :], ACT.Exp, scale=SLOPE).then_inc(exps_ready, 1)
            act.activation(t.col_pos[:, :], relc[:, :], ACT.Exp).then_inc(exps_ready, 1)
            act.wait_ge(exp_in, 2)
            act.activation(t.row_pos[:, :], qc[:, :], ACT.Exp).then_inc(exps_ready, 1)
            act.activation(t.row_neg[:, :], qs[:, :], ACT.Exp).then_inc(exps_ready, 1)
            for s in range(2):
                act.wait_ge(h_saved[s], GROUPS // 2 * 16)

        @block.vector
        def _(dve):
            dve.wait_ge(weights_in, 32)
            for s in range(2):
                for k in range(KF):
                    last = dve.tensor_tensor_reduce(junk[:, s, k, :], w[:, k, 0:FEAT], arow[:, s, :], 1.0, 0.0, ALU.mult,
                                                    ALU.add, w[:, k, FEAT + s:FEAT + s + 1])
                    last.then_inc(wa_ready, 1)
            dve.wait_ge(wa_ready, 4)
            dve.tensor_copy(w_hi[:, :, :], w[:, :, :]).then_inc(whi_ready, 1)
            dve.wait_ge(whi_ready, 1)
            dve.tensor_tensor(w_lo[:, :, :], w[:, :, :], w_hi[:, :, :].bitcast(F32), ALU.subtract).then_inc(wlo_ready, 1)

            def moments(n, s, n2):
                dve.wait_ge(x_in[s], (n2 + 1) * 16)
                for u in range(GT):
                    dve.bn_stats(stats[:, s, u, :], xin[:, s, u, :]).then_inc(stats_ready, 1)
                waits_apart(dve, stats_passed, (stats_ready, (n + 1) * GT))
                for u in range(GT):
                    dve.bn_aggr(meanvar[:, s, u, :], stats[:, s, u, :]).then_inc(meanvar_ready, 1)

            def normalise(n, s):
                dve.wait_ge(std_ready, n + 1)
                dve.reciprocal(rstd[:, s, :], std[:, s, :]).then_inc(rstd_ready, 1)
                dve.wait_ge(rstd_ready, n + 1)
                at_least(dve, transposed, n - 1)
                for u in range(GT):
                    dve.tensor_scalar(xn[:, s, u, :], xin[:, s, u, :], meanvar[:, s, u, 0:1], rstd[:, s, u:u + 1],
                                      ALU.subtract, ALU.mult).then_inc(xn_ready, 1)

            def split(n, s):
                dve.wait_ge(xhi_ready, n + 1)
                at_least(dve, h_ready, n - 1)
                dve.tensor_tensor(xT_lo[:, s, :, :], ps_T[:, s, :, :], xT_hi[:, s, :, :].bitcast(F32), ALU.subtract
                                  ).then_inc(xlo_ready, 1)

            def batch(b):
                for u in range(BG):
                    n = b * BG + u
                    moments(n, u % 2, b * (BG // 2) + u // 2)
                    if u or not isinstance(b, int):
                        normalise(n - 1, (u + 1) % 2)
                    if u > 1 or not isinstance(b, int):
                        split(n - 2, u % 2)
            batches(dve, batch)
            normalise(GROUPS - 1, 1)
            split(GROUPS - 2, 0)
            split(GROUPS - 1, 1)
            dve.wait_ge(xhi_ready, GROUPS)
            dve.tensor_reduce(bsum[:, :, :], xsum[:, :, :].rearrange("p (b g) k -> p k b g", b=BATCH), AX.X, ALU.add
                              ).then_inc(bsum_ready, 1)
            dve.wait_ge(scores_copied, GROUPS)
            s2 = score[:, :, 1]
            dve.tensor_reduce(mx[:, :], s2.rearrange("p (b t) -> p b t", b=BATCH), AX.X, ALU.max).then_inc(max_part, 1)
            dve.tensor_copy(s1[:, :], score[:, :, 0]).then_inc(s1_ready, 1)
            dve.tensor_scalar(t.neg_s2[:, :], s2, -1.0, None, ALU.mult).then_inc(tail, 1)
            dve.wait_ge(deg_counted, BT)
            dve.tensor_scalar(t.alone[:, :], ps_deg[:, :, 0], 0.0, None, ALU.is_equal).then_inc(tail, 1)
            dve.wait_ge(hsum_ready, 1)
            dve.tensor_scalar(hmean[:, :], ps_misc[0:BATCH, 0:FEAT], 1.0 / NODES, None, ALU.mult).then_inc(hmean_ready, 1)
            dve.wait_ge(s1T_ready, 1)
            dve.tensor_copy(s1T[:, :], ps_misc[:, 0:TILES]).then_inc(s1T_copied, 1)

            def of_batch(tile):
                return tile[:, :].rearrange("p (b t) -> p b t", b=BATCH)
            peak = mb[:, :].unsqueeze(2).to_broadcast([P, BATCH, BT])
            dve.wait_ge(max_ready, 1)
            dve.tensor_tensor(of_batch(rel), s2.rearrange("p (b t) -> p b t", b=BATCH), peak, ALU.subtract).then_inc(tail, 1)
            dve.tensor_tensor(of_batch(q), score[:, :, 0].rearrange("p (b t) -> p b t", b=BATCH), peak, ALU.add).then_inc(tail, 1)
            dve.wait_ge(tail, 4)
            dve.tensor_scalar(relc[:, :], rel[:, :], CENTER, None, ALU.add).then_inc(exp_in, 1)
            dve.tensor_scalar(qs[:, :], q[:, :], SLOPE, None, ALU.mult).then_inc(tail, 1)
            dve.tensor_scalar(qc[:, :], q[:, :], -CENTER, None, ALU.add).then_inc(tail, 1)
            dve.wait_ge(tail, 6)
            dve.tensor_tensor(top[:, :], qs[:, :], qc[:, :], ALU.max).then_inc(tail, 1)
            dve.wait_ge(tail, 7)
            dve.tensor_tensor(qs[:, :], qs[:, :], top[:, :], ALU.subtract).then_inc(tail, 1)
            dve.wait_ge(tail, 8)
            dve.tensor_tensor(qc[:, :], qc[:, :], top[:, :], ALU.subtract).then_inc(exp_in, 1)
            dve.wait_ge(exps_ready, 2)
            for i, col in enumerate((t.col_pos, t.col_neg)):
                dve.tensor_copy(t.col_parts[:, :, i, 0], col[:, :]).then_inc(tail, 1)
            dve.wait_ge(tail, 10)
            for i, col in enumerate((t.col_pos, t.col_neg)):
                dve.tensor_tensor(t.col_parts[:, :, i, 1], col[:, :], t.col_parts[:, :, i, 0].bitcast(F32),
                                  ALU.subtract).then_inc(tail, 1)


def attend_stage(nc, t, A):
    with ExitStack() as ctx:
        def sb(name, shape, dt):
            return ctx.enter_context(nc.sbuf_tensor(name, shape, dt))

        def sem(name):
            return ctx.enter_context(nc.semaphore(name))

        def psum(name, shape):
            return ctx.enter_context(nc.psum_tensor(name, shape, F32))

        scaled = sb("scaled", [P, SLOTS, 2, SW], F32R)
        mask_pos = sb("mask_pos", [P, BT, GW], F32R)
        mask_neg = sb("mask_neg", [P, BT, GW], F32R)
        s1row = sb("s1row", [P, 2, GW], F32)
        hmean = sb("hmean_all", [P, 2, FEAT], F32)
        hin = sb("hin", [P, GT, FEAT], F32)
        xres = sb("xres", [P, 2, GT, FEAT], F32)
        att = sb("att", [P, GT, FEAT + 2], F32)
        expo = sb("expo", [P, GT, FEAT], F32)
        xrow = sb("xrow", [P, 2, GT, ROW], F32)
        xT = sb("xT_router", [P, KF, GW], F32)
        rh = sb("rh", [P, GW], F32)
        wr1 = sb("wr1", [P, KF, RH], F32)
        wr2 = sb("wr2", [P, EXPERTS], F32)
        br1 = sb("br1", [P, 1], F32)
        br2 = sb("br2", [P, EXPERTS], F32)
        eps = sb("eps2", [P, 1], F32)
        tri = sb("tri", [P, P], BF16)
        ones = sb("ones2", [P, P], BF16)
        iota_e = sb("iota_e", [P, EXPERTS], F32)
        den = sb("den", [P, GT], F32)
        den1 = sb("den1", [P, GT], F32)
        rden = sb("rden", [P, GT], F32)
        stats = sb("stats2", [P, GT, 6], F32)
        meanvar = sb("meanvar2", [P, GT, 2], F32)
        std = sb("std2", [P, GT], F32)
        rstd = sb("rstd2", [P, GT], F32)
        logits = sb("logits", [P, GT, 8], F32)
        best = sb("best", [P, GT, 8], F32)
        bidx = sb("bidx", [P, GT, 8], U32)
        exin = sb("exin", [P, GT, EXPERTS + 1], F32)
        exout = sb("exout", [P, GT, EXPERTS + 1], F32)
        idxf = sb("idxf", [P, GT, TOPK], F32)
        chosen = sb("chosen", [P, GT, TOPK, EXPERTS], F32)
        sel = sb("sel", [P, GT, EXPERTS], BF16)
        prob = sb("prob", [P, 4, GT], F32)
        edif = sb("edif", [P, GT], F32)
        rank = sb("rank", [P, 2, GT, 2, EXPERTS], F32)
        place = sb("place", [P, GT, TOPK, EXPERTS], F32)
        posf = sb("posf", [P, GT, TOPK], F32)
        pos = sb("pos", [P, 2, GT, TOPK], I32)

        u_pos = [psum(f"u_pos{i}", [P, 512]) for i in range(GT)]
        u_neg = [psum(f"u_neg{i}", [P, 512]) for i in range(GT)]
        ps_xT = psum("ps_xT", [P, KF, GW])
        ps_rh = psum("ps_rh", [P, 512])
        ps_lg = psum("ps_lg", [P, 512])
        ps_rk = psum("ps_rk", [P, 512])
        lg = ps_lg[:, 0:GT * 8].rearrange("p (u e) -> p u e", u=GT)
        rk = ps_rk[:, 0:2 * GT * EXPERTS].rearrange("p (s u e) -> p s u e", s=2, u=GT)

        small_in = sem("small_in")
        const_zero = sem("const_zero")
        const_ready = sem("const_ready")
        s1_in = [sem(f"s1_in{i}") for i in range(2)]
        hm_in = [sem(f"hm_in{i}") for i in range(2)]
        xr_in = [sem(f"xr_in{i}") for i in range(2)]
        h_in = sem("h_in")
        hi_ready = sem("hi_ready")
        parts_ready = sem("parts_ready")
        lo_ready = sem("lo_ready")
        mp_ready = sem("mp_ready")
        pos_passed = sem("pos_passed")
        adj_ready = sem("adj_ready")
        mm_ready = sem("mm_ready")
        masks_used = sem("masks_used")
        u_ready = sem("u_ready")
        v_ready = sem("v_ready")
        att_ready = sem("att_ready")
        den_ready = sem("den_ready")
        den1_ready = sem("den1_ready")
        rden_ready = sem("rden_ready")
        mean_added = sem("mean_added")
        expo_ready = sem("expo_ready")
        elu_pos = sem("elu_pos")
        elu_ready = sem("elu_ready")
        x1_ready = sem("x1_ready")
        x1_saved = [sem(f"x1_saved{i}") for i in range(2)]
        stats_ready = sem("stats2_ready")
        stats_passed = sem("stats2_passed")
        meanvar_ready = sem("meanvar2_ready")
        std_ready = sem("std2_ready")
        rstd_ready = sem("rstd2_ready")
        xn_ready = sem("xn2_ready")
        xT_ready = sem("xT_ready")
        xT_copied = sem("xT_copied")
        rh_ready = sem("rh_ready")
        rh_copied = sem("rh_copied")
        logits_ready = sem("logits_ready")
        route = sem("route")
        route_passed = sem("route_passed")
        exin_ready = sem("exin_ready")
        exout_ready = sem("exout_ready")
        edif_in = sem("edif_in")
        edif_ready = sem("edif_ready")
        sel_ready = sem("sel_ready")
        rank_ready = sem("rank_ready")
        pos_ready = sem("pos_ready")
        scattered = [sem(f"scattered{i}") for i in range(2)]
        counts_ready = sem("counts_ready")
        zero_ready = sem("zero_ready")
        zero_saved = sem("zero_saved")

        (R_LOGITS, R_BEST0, R_BEST1, R_IDX0, R_IDX1, R_DIF, R_IDXF, R_CHOSEN, R_SUM, R_RSUM, R_ONE, R_W1, R_W2,
         R_RANK0, R_DW, R_RANK1, R_TOK, R_FIRST, R_PLACE, R_POSF) = range(1, 21)
        STEPS = 20

        block = ctx.enter_context(nc.Block())

        def pipeline(eng, body, start=0):
            for n in range(4):
                body(n, n % 2, True)
            with eng.Fori(2, (GROUPS - BG) // 2) as i:
                for s in range(2):
                    body(i * 2 + s, s, True)
            body(GROUPS - BG, 0, True)
            body(GROUPS - BG + 1, 1, False)
            with eng.Fori((GROUPS - BG) // 2 + 1, GROUPS // 2) as i:
                for s in range(2):
                    body(i * 2 + s, s, False)
            for n in range(GROUPS, GROUPS + 3):
                body(n, n % 2, False)

        def runs(n, lag=0):
            return not isinstance(n, int) or lag <= n < GROUPS + lag

        def half(n, s):
            return (n - s) // 2 if isinstance(n, int) else (n - s) // 2

        @block.sync
        def _(sp):
            sp.dma_start(wr1[:, :, :], A["router_w1"].rearrange("(k p) f -> p k f", p=P)).then_inc(small_in, 16)
            sp.dma_start(wr2[:, :], A["router_w2"]).then_inc(small_in, 16)
            sp.dma_start(br1[:, :], A["router_b1"].rearrange("(p one) -> p one", one=1)).then_inc(small_in, 16)
            sp.dma_start(br2[:, :], A["router_b2"].rearrange("(one e) -> one e", one=1).to_broadcast([P, EXPERTS])
                         ).then_inc(small_in, 16)

            def load_h(m):
                at_least(sp, lo_ready, m * 2 * GT)
                sp.dma_start(hin[:, :, :], A["h"][m]).then_inc(h_in, 16)
            load_h(0)
            with sp.Fori(1, AHEAD) as m:
                load_h(m)

            def body(n, s, ahead):
                if runs(n):
                    at_least(sp, mp_ready, (n - 1) * BT)
                    sp.dma_start(s1row[:, s, :], A["s1_rows"][n].to_broadcast([P, GW])).then_inc(s1_in[s], 16)
                    if not isinstance(n, int) or n >= 2:
                        sp.wait_ge(mean_added, (n - 1) * GT)
                    sp.dma_start(hmean[:, s, :], A["hmean_rows"][n // BG].to_broadcast([P, FEAT])).then_inc(hm_in[s], 16)
                    if ahead:
                        load_h(n + AHEAD)
                if runs(n, 2):
                    m = n - 2
                    sp.wait_ge(x1_ready, m + 1)
                    sp.dma_start(A["x1"][m], xres[:, s, :, :]).then_inc(x1_saved[s], 16)
                if runs(n):
                    if not isinstance(n, int) or n >= 2:
                        sp.wait_ge(x1_saved[s], half(n, s) * 16)
                        sp.wait_ge(xn_ready, (n - 1) * GT)
                    sp.dma_start(xres[:, s, :, :], A["x"][n]).then_inc(xr_in[s], 16)
            pipeline(sp, body)
            for s in range(2):
                sp.wait_ge(x1_saved[s], GROUPS // 2 * 16)
            sp.wait_ge(zero_ready, 1)
            sp.dma_start(A["out_pad"], hin[:, :, :]).then_inc(zero_saved, 16)
            sp.dma_start(A["out_pad2"], hin[:, :, :]).then_inc(zero_saved, 16)
            sp.dma_start(A["out_pad3"], hin[:, :, :]).then_inc(zero_saved, 16)
            sp.dma_start(A["out_pad4"], hin[:, :, :]).then_inc(zero_saved, 16)
            sp.wait_ge(zero_saved, 64)

        @block.gpsimd
        def _(pool):
            pool.memset(eps[:, :], EPS).then_inc(const_zero, 1)
            pool.memset(ones[:, :], 1.0).then_inc(const_zero, 1)
            pool.memset(logits[:, :, :], -3.0e38).then_inc(const_zero, 1)
            pool.iota(iota_e[:, :], [[1, EXPERTS]], base=0, channel_multiplier=0,
                      allow_small_or_imprecise_dtypes=True).then_inc(const_zero, 1)
            pool.iota(rank[:, 1, 1, 1, :], [[STRIDE, EXPERTS]], base=0, channel_multiplier=0,
                      allow_small_or_imprecise_dtypes=True).then_inc(const_zero, 1)
            pool.iota(xrow[:, 1, :, C_TOKEN], [[P, GT]], base=-GW, channel_multiplier=1,
                      allow_small_or_imprecise_dtypes=True).then_inc(const_zero, 1)
            pool.wait_ge(const_zero, 6)
            pool.affine_select(out=tri[:, :], in_=ones[:, :], compare_op=ALU.is_gt, fill=0.0, base=0,
                               pattern=[[1, P]], channel_multiplier=-1).then_inc(const_ready, 1)

            def body(n, s, ahead):
                if runs(n):
                    for c in range(NC):
                        r = slice(c * CH, (c + 1) * CH)
                        pool.wait_ge(adj_ready, n * NC + c + 1)
                        pool.wait_ge(mp_ready, n * BT + (c + 1) * CH)
                        pool.tensor_tensor(mask_neg[:, r, :], mask_neg[:, r, :].bitcast(F32),
                                           mask_pos[:, r, :].bitcast(F32), ALU.subtract).then_inc(mm_ready, 1)
                if runs(n, 3):
                    m = n - 3
                    o = 1 - s
                    waits_apart(pool, pos_passed, (pos_ready, m + 1))
                    for u in range(GT):
                        for k in range(TOPK):
                            pool.indirect_dma_start(
                                A["lists"], bass.IndirectOffsetOnAxis(ap=pos[:, o, u, k:k + 1].bitcast(U32), axis=0),
                                xrow[:, o, u, :], None, bounds_check=LIST_ROWS - 1).then_inc(scattered[o], 16)
            pipeline(pool, body)
            for s in range(2):
                pool.wait_ge(scattered[s], GROUPS // 2 * 16 * GT * TOPK)

        @block.tensor
        def _(pe):
            def attend(n, c):
                pe.wait_ge(mm_ready, n * NC + c + 1)
                if c == 0:
                    pe.wait_ge(parts_ready, n // BG * BG + AHEAD)
                    pe.wait_ge(lo_ready, (n // BG * BG + AHEAD) * 2 * GT)
                if c == NC - 1:
                    pe.wait_ge(parts_ready, (n // BG + 1) * BG)
                    pe.wait_ge(lo_ready, (n // BG + 1) * BG * 2 * GT)
                for u in range(GT):
                    if c == 0:
                        at_least(pe, att_ready, (n - 1) * GT + u + 1)
                    for j in range(c * CH, (c + 1) * CH):
                        slot = (n // BG * BT + c * CH) % SLOTS + j % CH
                        for i, (mask, acc) in enumerate(((mask_pos, u_pos[u]), (mask_neg, u_neg[u]))):
                            st = mask[:, j, u * P:(u + 1) * P]
                            pe.matmul(acc[:, 0:FEAT + 2], st, scaled[:, slot, i, 0:FEAT + 2], start=(j == 0), stop=False,
                                      skip_group_check=True)
                            last = pe.matmul(acc[:, 0:FEAT], st, scaled[:, slot, i, FEAT + 2:SW], start=False,
                                             stop=(j == BT - 1), skip_group_check=True)
                    if u == 1:
                        last.then_inc(masks_used, 1)
                    if u == 0 and c == NC - 1:
                        last.then_inc(u_ready, 1)

            def body(n, s, ahead):
                if runs(n, 2):
                    m = n - 2
                    pe.wait_ge(xn_ready, (m + 1) * GT)
                    at_least(pe, xT_copied, m)
                    for k in range(KF):
                        for u in range(GT):
                            last = pe.transpose(ps_xT[:, k, u * P:(u + 1) * P], xrow[:, s, u, k * P:(k + 1) * P],
                                                t.ident[:, :])
                    last.then_inc(xT_ready, 1)
                if runs(n, 3):
                    pe.wait_ge(sel_ready, n - 3 + 1)
                    for i, w in enumerate((tri, ones)):
                        last = pe.matmul(ps_rk[:, i * GT * EXPERTS:(i + 1) * GT * EXPERTS], w[:, :],
                                         sel[:, :, :], start=(i == 0), stop=True, skip_group_check=True)
                    last.then_inc(rank_ready, 1)
                if runs(n):
                    attend(n, 0)
                if runs(n, 2):
                    pe.wait_ge(xT_copied, m + 1)
                    at_least(pe, rh_copied, m)
                    for k in range(KF):
                        last = pe.matmul(ps_rh[:, 0:GW], wr1[:, k, :], xT[:, k, :], start=(k == 0), stop=(k == KF - 1))
                    last.then_inc(rh_ready, 1)
                if runs(n):
                    attend(n, 1)
                if runs(n, 2):
                    pe.wait_ge(rh_copied, m + 1)
                    at_least(pe, route, (m - 1) * STEPS + R_LOGITS)
                    for u in range(GT):
                        last = pe.matmul(lg[:, u, 0:EXPERTS], rh[:, u * P:(u + 1) * P], wr2[:, :], start=(u == 0),
                                         stop=True, skip_group_check=True)
                    last.then_inc(logits_ready, 1)
                if runs(n):
                    attend(n, 2)
                    attend(n, 3)
            pe.wait_ge(small_in, 64)
            pe.wait_ge(const_ready, 1)
            pipeline(pe, body)

        @block.scalar
        def _(act):
            act.wait_ge(const_zero, 6)
            act.wait_ge(small_in, 64)

            def scale(m):
                act.wait_ge(h_in, (m + 1) * 16)
                for u in range(GT):
                    slot = (m * GT + u) % SLOTS
                    for i, col in enumerate((t.col_pos, t.col_neg)):
                        act.activation(scaled[:, slot, i, 0:FEAT], hin[:, u, :], ACT.Copy,
                                       scale=col[:, bass.ds(m * GT + u, 1)]).then_inc(hi_ready, 1)
                act.activation(scaled[:, bass.ds(m * GT % SLOTS, GT), :, FEAT:FEAT + 2],
                               t.col_parts[:, bass.ds(m * GT, GT), :, :].bitcast(F32), ACT.Copy).then_inc(parts_ready, 1)

            with act.Fori(0, AHEAD) as m:
                scale(m)

            def spread(n, c):
                at_least(act, masks_used, (n - 1) * NC + c + 1)
                act.activation(mask_neg[:, c * CH:(c + 1) * CH, :],
                               t.adj[:, c * CH:(c + 1) * CH, bass.ds((n % BG) * GW, GW)], ACT.Copy
                               ).then_inc(adj_ready, 1)

            def body(n, s, ahead):
                if runs(n):
                    spread(n, 0)
                    spread(n, 1)
                if runs(n, 3):
                    act.wait_ge(exin_ready, n - 3 + 1)
                    act.activation(exout[:, :, :], exin[:, :, :], ACT.Exp).then_inc(exout_ready, 1)
                if runs(n):
                    spread(n, 2)
                if runs(n, 3):
                    act.wait_ge(edif_in, n - 3 + 1)
                    act.activation(edif[:, :], prob[:, 2, :], ACT.Exp).then_inc(edif_ready, 1)
                if runs(n, 1):
                    m = n - 1
                    for u in range(GT):
                        if u == 0:
                            act.wait_ge(u_ready, m + 1)
                            at_least(act, elu_ready, m)
                        else:
                            act.wait_ge(masks_used, (m + 1) * NC)
                        act.activation(att[:, u, :], u_pos[u][:, 0:FEAT + 2], ACT.Copy,
                                       scale=t.row_pos[:, bass.ds(m * GT + u, 1)]).then_inc(v_ready, 1)
                if runs(n):
                    spread(n, 3)
                if runs(n, 2):
                    act.wait_ge(xT_ready, n - 2 + 1)
                    act.activation(xT[:, :, :], ps_xT[:, :, :], ACT.Copy).then_inc(xT_copied, 1)
                if runs(n, 1):
                    act.wait_ge(rden_ready, m + 1)
                    act.wait_ge(mean_added, (m + 1) * GT)
                    for u in range(GT):
                        act.activation(expo[:, u, :], att[:, u, 0:FEAT], ACT.Exp, scale=rden[:, u:u + 1]
                                       ).then_inc(expo_ready, 1)
                    act.wait_ge(expo_ready, (m + 1) * GT)
                    for u in range(GT):
                        act.activation(att[:, u, 0:FEAT], att[:, u, 0:FEAT], ACT.Relu, scale=rden[:, u:u + 1]
                                       ).then_inc(elu_pos, 1)
                if runs(n, 2):
                    act.wait_ge(rh_ready, n - 2 + 1)
                    act.activation(rh[:, :], ps_rh[:, 0:GW], ACT.Relu, bias=br1[:, 0:1]).then_inc(rh_copied, 1)
                if runs(n) and ahead:
                    act.wait_ge(masks_used, n * NC + 1)
                    scale(n + AHEAD)
                if runs(n, 1):
                    act.wait_ge(meanvar_ready, (m + 1) * GT)
                    act.activation(std[:, :], meanvar[:, :, 1], ACT.Sqrt, bias=eps[:, 0:1]).then_inc(std_ready, 1)
            pipeline(act, body)

        @block.vector
        def _(dve):
            def scale(m):
                dve.wait_ge(hi_ready, (m + 1) * 2 * GT)
                for u in range(GT):
                    slot = (m * GT + u) % SLOTS
                    for i, col in enumerate((t.col_pos, t.col_neg)):
                        dve.scalar_tensor_tensor(scaled[:, slot, i, FEAT + 2:SW], hin[:, u, :],
                                                 col[:, bass.ds(m * GT + u, 1)],
                                                 scaled[:, slot, i, 0:FEAT].bitcast(F32), ALU.mult, ALU.subtract
                                                 ).then_inc(lo_ready, 1)
            with dve.Fori(0, AHEAD) as m:
                scale(m)

            def masks_of(n, s):
                def mask(j):
                    if not runs(n):
                        return
                    if j == 0:
                        dve.wait_ge(s1_in[s], (half(n, s) + 1) * 16)
                    if j % CH == 0:
                        at_least(dve, masks_used, (n - 1) * NC + j // CH + 1)
                    dve.scalar_tensor_tensor(mask_pos[:, j, :], s1row[:, s, :],
                                             t.neg_s2[:, bass.ds(n // BG * BT + j, 1)],
                                             t.adj[:, j, bass.ds((n % BG) * GW, GW)], ALU.is_gt, ALU.mult
                                             ).then_inc(mp_ready, 1)
                return mask

            def take_out(m, s, u):
                dve.wait_ge(v_ready, m * GT + u + 1)
                dve.scalar_tensor_tensor(att[:, u, :], u_neg[u][:, 0:FEAT + 2], t.row_neg[:, bass.ds(m * GT + u, 1)],
                                         att[:, u, :], ALU.mult, ALU.add).then_inc(att_ready, 1)

            def finish_a(m, s, mask):
                tile = (m % BG) * GT
                dve.wait_ge(att_ready, (m + 1) * GT)
                dve.tensor_tensor(den[:, :], att[:, :, FEAT], att[:, :, FEAT + 1], ALU.add).then_inc(den_ready, 1)
                dve.wait_ge(hm_in[s], (half(m, s) + 1) * 16)
                for u in range(GT):
                    dve.scalar_tensor_tensor(att[:, u, 0:FEAT], hmean[:, s, :], t.alone[:, bass.ds(tile + u, 1)],
                                             att[:, u, 0:FEAT], ALU.mult, ALU.add).then_inc(mean_added, 1)
                dve.wait_ge(den_ready, m + 1)
                dve.tensor_tensor(den1[:, :], den[:, :], t.alone[:, bass.ds(tile, GT)], ALU.add).then_inc(den1_ready, 1)
                mask(12)
                dve.wait_ge(den1_ready, m + 1)
                dve.reciprocal(rden[:, :], den1[:, :]).then_inc(rden_ready, 1)

            def elu(m):
                dve.wait_ge(expo_ready, (m + 1) * GT)
                dve.wait_ge(elu_pos, (m + 1) * GT)
                dve.scalar_tensor_tensor(expo[:, :, :], expo[:, :, :], 1.0, att[:, :, 0:FEAT], ALU.min, ALU.add
                                         ).then_inc(elu_ready, 1)

            def residual(m, s):
                dve.wait_ge(elu_ready, m + 1)
                dve.wait_ge(xr_in[s], (half(m, s) + 1) * 16)
                dve.scalar_tensor_tensor(xres[:, s, :, :], expo[:, :, :], -1.0, xres[:, s, :, :], ALU.add, ALU.add
                                         ).then_inc(x1_ready, 1)

            def moments(m, s):
                dve.wait_ge(x1_ready, m + 1)
                for u in range(GT):
                    dve.bn_stats(stats[:, u, :], xres[:, s, u, :]).then_inc(stats_ready, 1)
                waits_apart(dve, stats_passed, (stats_ready, (m + 1) * GT))
                for u in range(GT):
                    dve.bn_aggr(meanvar[:, u, :], stats[:, u, :]).then_inc(meanvar_ready, 1)

            def normalise(m, s, mask):
                dve.wait_ge(std_ready, m + 1)
                dve.reciprocal(rstd[:, :], std[:, :]).then_inc(rstd_ready, 1)
                mask(8)
                dve.wait_ge(rstd_ready, m + 1)
                at_least(dve, scattered[s], half(m, s) * 16 * GT * TOPK)
                for u in range(GT):
                    dve.tensor_scalar(xrow[:, s, u, 0:FEAT], xres[:, s, u, :], meanvar[:, u, 0:1], rstd[:, u:u + 1],
                                      ALU.subtract, ALU.mult).then_inc(xn_ready, 1)

            def step(m, k, ins):
                ins.then_inc(route, 1)

            def need(m, k):
                dve.wait_ge(route, m * STEPS + k)

            def choose(m, s, mask):
                dve.wait_ge(logits_ready, m + 1)
                step(m, R_LOGITS, dve.tensor_tensor(
                    logits[:, :, 0:EXPERTS], lg[:, :, 0:EXPERTS],
                    br2[:, :].unsqueeze(1).to_broadcast([P, GT, EXPERTS]), ALU.add))
                mask(0)
                waits_apart(dve, route_passed, (route, m * STEPS + R_LOGITS))
                for u in range(GT):
                    step(m, R_BEST0 + u, dve.max(best[:, u, :], logits[:, u, :]))
                mask(1)
                waits_apart(dve, route_passed, (route, m * STEPS + R_BEST1))
                for u in range(GT):
                    step(m, R_IDX0 + u, dve.max_index(bidx[:, u, :], best[:, u, :], logits[:, u, :]))
                step(m, R_DIF, dve.tensor_tensor(exin[:, :, 0:EXPERTS], logits[:, :, 0:EXPERTS],
                                                 best[:, :, 0:1].to_broadcast([P, GT, EXPERTS]), ALU.subtract))
                mask(2)
                dve.wait_ge(route, m * STEPS + R_DIF)
                dve.tensor_tensor(exin[:, :, EXPERTS], best[:, :, 1], best[:, :, 0], ALU.subtract
                                  ).then_inc(exin_ready, 1)
                step(m, R_IDXF, dve.tensor_copy(idxf[:, :, :], bidx[:, :, 0:TOPK]))
                mask(3)
                need(m, R_IDXF)
                step(m, R_CHOSEN, dve.tensor_tensor(
                    chosen[:, :, :, :], idxf[:, :, :].unsqueeze(3).to_broadcast([P, GT, TOPK, EXPERTS]),
                    iota_e[:, :].unsqueeze(1).unsqueeze(1).to_broadcast([P, GT, TOPK, EXPERTS]), ALU.is_equal))
                mask(4)
                need(m, R_CHOSEN)
                dve.tensor_tensor(sel[:, :, :], chosen[:, :, 0, :], chosen[:, :, 1, :], ALU.add).then_inc(sel_ready, 1)
                mask(5)
                mask(6)

            def weigh(m, s, mask):
                dve.wait_ge(exout_ready, m + 1)
                step(m, R_SUM, dve.tensor_reduce(prob[:, 0, :], exout[:, :, 0:EXPERTS], AX.X, ALU.add))
                mask(7)
                need(m, R_SUM)
                step(m, R_RSUM, dve.reciprocal(prob[:, 1, :], prob[:, 0, :]))
                need(m, R_RSUM)
                dve.scalar_tensor_tensor(prob[:, 2, :], exout[:, :, EXPERTS], -1.0, prob[:, 1, :], ALU.add, ALU.mult
                                         ).then_inc(edif_in, 1)

            def pair_weights(m, s, mask):
                dve.wait_ge(edif_ready, m + 1)
                step(m, R_ONE, dve.tensor_scalar(prob[:, 0, :], edif[:, :], 1.0, None, ALU.add))
                mask(13)
                need(m, R_ONE)
                step(m, R_W1, dve.reciprocal(prob[:, 3, :], prob[:, 0, :]))
                mask(14)
                need(m, R_W1)
                step(m, R_W2, dve.tensor_tensor(xrow[:, s, :, C_W2], edif[:, :], prob[:, 3, :], ALU.mult))
                dve.wait_ge(rank_ready, m + 1)
                step(m, R_RANK0, dve.tensor_tensor(
                    rank[:, s, 0, :, :], rk[:, :, 0, :],
                    rank[:, 1 - s, 1, 1, :].unsqueeze(1).to_broadcast([P, 2, EXPERTS]), ALU.add))
                mask(15)
                need(m, R_RANK0)
                step(m, R_DW, dve.tensor_tensor(xrow[:, s, :, C_DW], prob[:, 3, :], xrow[:, s, :, C_W2], ALU.subtract))
                step(m, R_RANK1, dve.tensor_tensor(
                    rank[:, s, 1, :, :], rk[:, :, 1, :],
                    rank[:, s, 0, 1, :].unsqueeze(1).to_broadcast([P, 2, EXPERTS]), ALU.add))
                step(m, R_TOK, dve.tensor_scalar(xrow[:, s, :, C_TOKEN], xrow[:, 1 - s, :, C_TOKEN], float(GW), None,
                                                 ALU.add))
                step(m, R_FIRST, dve.tensor_copy(xrow[:, s, :, C_FIRST], idxf[:, :, 0]))
                need(m, R_RANK1)
                step(m, R_PLACE, dve.tensor_tensor(
                    place[:, :, :, :], chosen[:, :, :, :],
                    rank[:, s, :, 0, :].unsqueeze(2).to_broadcast([P, GT, TOPK, EXPERTS]), ALU.mult))

            def position(m, s):
                need(m, R_PLACE)
                step(m, R_POSF, dve.tensor_reduce(posf[:, :, :], place[:, :, :, :], AX.X, ALU.add))

            def place_rows(m, s):
                need(m, R_POSF)
                dve.tensor_copy(pos[:, s, :, :], posf[:, :, :]).then_inc(pos_ready, 1)

            def body(n, s, ahead):
                o = 1 - s
                mask = masks_of(n, s)
                if runs(n, 3):
                    choose(n - 3, o, mask)
                    weigh(n - 3, o, mask)
                else:
                    for j in range(0, 8):
                        mask(j)
                if runs(n, 2):
                    normalise(n - 2, s, mask)
                else:
                    mask(8)
                for j in range(9, 12):
                    mask(j)
                if runs(n, 1):
                    for u in range(GT):
                        take_out(n - 1, o, u)
                    finish_a(n - 1, o, mask)
                else:
                    mask(12)
                if runs(n, 3):
                    pair_weights(n - 3, o, mask)
                else:
                    for j in range(13, BT):
                        mask(j)
                if runs(n, 1):
                    elu(n - 1)
                if runs(n, 3):
                    position(n - 3, o)
                if runs(n, 1):
                    residual(n - 1, o)
                if runs(n, 3):
                    place_rows(n - 3, o)
                if runs(n) and ahead:
                    scale(n + AHEAD)
                if runs(n, 1):
                    moments(n - 1, o)
            dve.wait_ge(small_in, 64)
            dve.wait_ge(const_ready, 1)
            pipeline(dve, body)
            dve.memset(hin[:, :, :], 0.0).then_inc(zero_ready, 1)
            dve.wait_ge(route, GROUPS * STEPS)
            dve.tensor_copy(t.ends[:, :], rank[:, 1, 1, 1, :]).then_inc(counts_ready, 1)


def pad_stage(nc, t):
    with ExitStack() as ctx:
        pad_zero = ctx.enter_context(nc.semaphore("pad_zero"))
        pad_ready = ctx.enter_context(nc.semaphore("pad_ready"))
        block = ctx.enter_context(nc.Block())

        @block.gpsimd
        def _(pool):
            pool.memset(t.pad[:, :, :], 0.0).then_inc(pad_zero, 1)
            pool.wait_ge(pad_zero, 1)
            pool.iota(t.pad[:, :, C_TOKEN], [[1, CU]], base=TOKENS, channel_multiplier=CU,
                      allow_small_or_imprecise_dtypes=True).then_inc(pad_ready, 1)
            pool.wait_ge(pad_ready, 1)


def expert_stage(nc, t, A):
    with ExitStack() as ctx:
        def sb(name, shape, dt):
            return ctx.enter_context(nc.sbuf_tensor(name, shape, dt))

        def sem(name):
            return ctx.enter_context(nc.semaphore(name))

        def psum(name, shape):
            return ctx.enter_context(nc.psum_tensor(name, shape, F32))

        M = FEAT // P
        all_hi = sb("all_hi", [P, EXPERTS, LAYERS, KF, FEAT], F32R)
        all_lo = sb("all_lo", [P, EXPERTS, LAYERS, KF, FEAT], F32R)
        cur_hi = sb("cur_hi", [P, 2, LAYERS, KF, FEAT], F32R)
        cur_lo = sb("cur_lo", [P, 2, LAYERS, KF, FEAT], F32R)
        bias_all = sb("bias_all", [P, 2, EXPERTS, M], F32)
        bias = sb("bias", [P, 2, 2, M], F32)
        b3 = sb("b3", [P, EXPERTS, FEAT], F32)
        rows = sb("rows", [P, 2, CU, ROW], F32)
        act_hi = [sb(f"act_hi{i}", [P, KF, HALF], F32R) for i in range(4)]
        act_lo = [sb(f"act_lo{i}", [P, KF, HALF], F32R) for i in range(4)]
        relu = sb("relu", [P, 2, HALF], F32)
        y = sb("y", [P, 2, CU, FEAT], F32)
        raw = [sb(f"w_raw{i}", [P, KF, FEAT], F32) for i in range(2)]
        first = sb("first", [P, 2, CU], F32)
        weight = sb("weight", [P, 2, CU], F32)
        token = sb("token", [P, 2, CU], I32)
        iota_m = sb("iota_m", [P, TOKENS // CHUNK], F32)
        iota_c = sb("iota_c", [P, CHUNKS], F32)
        starts = sb("starts", [P, EXPERTS], F32)
        counts = sb("counts", [P, EXPERTS], F32)
        more = sb("more", [P, EXPERTS, TOKENS // CHUNK], F32)
        chunks = sb("chunks", [P, EXPERTS], F32)
        upto = sb("upto", [P, EXPERTS], F32)
        passed = sb("passed", [P, CHUNKS, EXPERTS], F32)
        passed_n = sb("passed_n", [P, CHUNKS, EXPERTS], F32)
        owner = sb("owner", [P, CHUNKS], F32)
        before = sb("before", [P, CHUNKS], F32)
        offset = sb("offset", [P, CHUNKS], F32)
        base = sb("base", [P, CHUNKS], F32)
        owner5 = sb("owner5", [P, CHUNKS], F32)
        base_i = sb("base_i", [P, CHUNKS], I32)
        owner_i = sb("owner_i", [P, CHUNKS], I32)
        ends_i = sb("ends_i", [P, EXPERTS], I32)

        ps_x = [psum(f"ps_x{k}", [P, HALF]) for k in range(KF)]
        ps_a = [[psum(f"ps_a{h}{m}", [P, HALF]) for m in range(M)] for h in range(2)]
        ps_y = [psum(f"ps_y{i}", [P, 512]) for i in range(2)]

        consts = sem("consts3")
        biases_in = sem("biases_in")
        raw_in = [sem(f"raw_in{i}") for i in range(2)]
        whi_ready = sem("whi3_ready")
        wlo_ready = sem("wlo3_ready")
        plan = sem("plan")
        plan_ready = sem("plan_ready")
        pads_saved = sem("pads_saved")
        rows_in = [sem(f"rows_in{i}") for i in range(2)]
        cur_ready = sem("cur_ready")
        bias_ready = sem("bias_ready")
        x_turned = sem("x_turned")
        xhi_ready = sem("xhi3_ready")
        xlo_ready = sem("xlo3_ready")
        z_ready = sem("z_ready")
        relu_ready = sem("relu_ready")
        ahi_ready = sem("ahi_ready")
        alo_ready = sem("alo_ready")
        first_ready = sem("first_ready")
        weight_ready = sem("weight_ready")
        token_ready = sem("token_ready")
        out_ready = sem("out_ready")
        y_scaled = sem("y_scaled")
        y_ready = sem("y_ready")
        added = sem("added")
        out_passed = sem("out_passed")
        load_passed = sem("load_passed")

        ZC = 2 * 2 * M

        block = ctx.enter_context(nc.Block())

        def turns(eng, body):
            body(0, 0)
            body(1, 1)
            with eng.Fori(1, CHUNKS // 2) as i:
                body(i * 2, 0)
                body(i * 2 + 1, 1)
            for c in range(CHUNKS // 2 * 2, CHUNKS):
                body(c, c % 2)

        def half(c, s):
            return (c - s) // 2

        @block.sync
        def _(sp):
            with nc.allow_non_contiguous_dma(reason="biases, one number for each partition"):
                sp.dma_start(bias_all[:, 0, :, :], A["b1"].rearrange("e (m p) -> p e m", p=P)).then_inc(biases_in, 16)
                sp.dma_start(bias_all[:, 1, :, :], A["b2"].rearrange("e (m p) -> p e m", p=P)).then_inc(biases_in, 16)
            sp.dma_start(b3[:, :, :], A["b3"].rearrange("(one e) f -> one e f", one=1).to_broadcast([P, EXPERTS, FEAT])
                         ).then_inc(biases_in, 16)
            for n in range(EXPERTS * LAYERS):
                e, l = n // LAYERS, n % LAYERS
                at_least(sp, wlo_ready, n - 1)
                sp.dma_start(raw[n % 2][:, :, :], A["w"][l][e].rearrange("(k p) f -> p k f", p=P)
                             ).then_inc(raw_in[n % 2], 16)
            sp.wait_ge(plan_ready, 1)
            for e in range(EXPERTS):
                end = sp.value_load(ends_i[0:1, e:e + 1], min_val=e * STRIDE, max_val=e * STRIDE + TOKENS)
                sp.dma_start(A["lists"][bass.ds(end, CHUNK), :].rearrange("(p u) f -> p u f", p=P), t.pad[:, :, :]
                             ).then_inc(pads_saved, 16)
            sp.dma_start(A["lists"][IDLE:LIST_ROWS, :].rearrange("(p u) f -> p u f", p=P), t.pad[:, :, :]
                         ).then_inc(pads_saved, 16)
            sp.wait_ge(pads_saved, 16 * (EXPERTS + 1))

            def turn(c, s):
                start = sp.value_load(base_i[0:1, bass.ds(c, 1)], min_val=0, max_val=IDLE)
                waits_apart(sp, load_passed, (token_ready, c - 1))
                waits_apart(sp, load_passed, (x_turned, (c - 1) * 2))
                sp.dma_start(rows[:, s, :, :], A["lists"][bass.ds(start, CHUNK), :].rearrange("(p u) f -> p u f", p=P)
                             ).then_inc(rows_in[s], 16)
            turns(sp, turn)

        @block.gpsimd
        def _(pool):
            pool.iota(iota_m[:, :], [[CHUNK, TOKENS // CHUNK]], base=0, channel_multiplier=0,
                      allow_small_or_imprecise_dtypes=True).then_inc(consts, 1)
            pool.iota(iota_c[:, :], [[1, CHUNKS]], base=0, channel_multiplier=0,
                      allow_small_or_imprecise_dtypes=True).then_inc(consts, 1)
            pool.iota(starts[:, :], [[STRIDE, EXPERTS]], base=0, channel_multiplier=0,
                      allow_small_or_imprecise_dtypes=True).then_inc(consts, 1)

            def turn(c, s):
                waits_apart(pool, out_passed, (token_ready, c + 1))
                for u in range(CU):
                    waits_apart(pool, out_passed, (y_ready, c * CU + u + 1), (added, c * CU * 16))
                    pool.indirect_dma_start(A["out"], bass.IndirectOffsetOnAxis(ap=token[:, s, u:u + 1].bitcast(U32), axis=0),
                                            y[:, s, u, :], None, bounds_check=OUT_ROWS - 1, compute_op=ALU.add
                                            ).then_inc(added, 16)
            turns(pool, turn)
            pool.wait_ge(added, CHUNKS * CU * 16)

        @block.tensor
        def _(pe):
            def turn_x(c, s, h):
                at_least(pe, xlo_ready, c * 2 + h)
                if h == 0:
                    pe.wait_ge(rows_in[s], (half(c, s) + 1) * 16)
                for k in range(KF):
                    for u in range(HU):
                        last = pe.transpose(ps_x[k][:, u * P:(u + 1) * P],
                                            rows[:, s, h * HU + u, k * P:(k + 1) * P], t.ident[:, :])
                last.then_inc(x_turned, 1)

            def product(out, pairs):
                n = len(pairs)
                for i, (l, r) in enumerate(pairs):
                    last = pe.matmul(out, l, r, start=(i == 0), stop=(i == n - 1))
                return last

            def layer(c, s, l, h):
                if l == 0:
                    pe.wait_ge(xlo_ready, c * 2 + h + 1)
                    if h == 0:
                        pe.wait_ge(cur_ready, (c + 1) * 2)
                else:
                    pe.wait_ge(alo_ready, c * ZC + (h + 1) * M)
                src = h + 2 * l
                for m in range(M):
                    at_least(pe, relu_ready, c * ZC + (l - 1) * 2 * M + h * M + m + 1)
                    cols = slice(m * P, (m + 1) * P)
                    product(ps_a[h][m][:, :],
                            [(w[:, s, l, k, cols], a[src][:, k, :]) for w, a in
                             ((cur_hi, act_hi), (cur_lo, act_hi), (cur_hi, act_lo)) for k in range(KF)]
                            ).then_inc(z_ready, 1)

            def last_layer(c, s, h):
                pe.wait_ge(alo_ready, c * ZC + 2 * M + (h + 1) * M)
                for u in range(HU):
                    n = h * HU + u
                    at_least(pe, y_scaled, c * CU + n - 1)
                    tok = slice(u * P, (u + 1) * P)
                    product(ps_y[n % 2][:, 0:FEAT],
                            [(a[h][:, k, tok], w[:, s, 2, k, :]) for a, w in
                             ((act_hi, cur_hi), (act_hi, cur_lo), (act_lo, cur_hi)) for k in range(KF)]
                            ).then_inc(out_ready, 1)

            def turn(c, s):
                turn_x(c, s, 0)
                turn_x(c, s, 1)
                for l in range(2):
                    for h in range(2):
                        layer(c, s, l, h)
                for h in range(2):
                    last_layer(c, s, h)
            turns(pe, turn)

        @block.scalar
        def _(act):
            act.wait_ge(biases_in, 48)

            def turn(c, s):
                for h in range(2):
                    act.wait_ge(x_turned, c * 2 + h + 1)
                    at_least(act, out_ready, (c - 1) * CU + (h + 1) * HU)
                    for k in range(KF):
                        act.activation(act_hi[h][:, k, :], ps_x[k][:, :], ACT.Copy).then_inc(xhi_ready, 1)
                act.wait_ge(bias_ready, c + 1)
                for l in range(2):
                    for h in range(2):
                        for m in range(M):
                            i = l * 2 * M + h * M + m
                            act.wait_ge(z_ready, c * ZC + i + 1)
                            at_least(act, alo_ready, c * ZC + i - 1)
                            act.activation(relu[:, m, :], ps_a[h][m][:, :], ACT.Relu, bias=bias[:, s, l, m:m + 1]
                                           ).then_inc(relu_ready, 1)
                act.wait_ge(weight_ready, c + 1)
                for n in range(CU):
                    act.wait_ge(out_ready, c * CU + n + 1)
                    if n == 0:
                        at_least(act, added, (c - 1) * CU * 16)
                    act.activation(y[:, s, n, :], ps_y[n % 2][:, 0:FEAT], ACT.Copy, scale=weight[:, s, n:n + 1]
                                   ).then_inc(y_scaled, 1)
            turns(act, turn)

        @block.vector
        def _(dve):
            def next_step(v, ins):
                ins.then_inc(plan, 1)
                dve.wait_ge(plan, v)
            dve.wait_ge(consts, 3)
            next_step(1, dve.tensor_tensor(counts[:, :], t.ends[:, :], starts[:, :], ALU.subtract))
            next_step(2, dve.tensor_tensor(
                more[:, :, :], counts[:, :].unsqueeze(2).to_broadcast([P, EXPERTS, TOKENS // CHUNK]),
                iota_m[:, :].unsqueeze(1).to_broadcast([P, EXPERTS, TOKENS // CHUNK]), ALU.is_gt))
            next_step(3, dve.tensor_reduce(chunks[:, :], more[:, :, :], AX.X, ALU.add))
            next_step(4, dve.tensor_copy(upto[:, 0:1], chunks[:, 0:1]))
            for e in range(1, EXPERTS):
                next_step(4 + e, dve.tensor_tensor(upto[:, e:e + 1], upto[:, e - 1:e], chunks[:, e:e + 1], ALU.add))
            wide = [P, CHUNKS, EXPERTS]
            next_step(10, dve.tensor_tensor(passed[:, :, :], iota_c[:, :].unsqueeze(2).to_broadcast(wide),
                                            upto[:, :].unsqueeze(1).to_broadcast(wide), ALU.is_ge))
            next_step(11, dve.tensor_tensor(passed_n[:, :, :], passed[:, :, :],
                                            chunks[:, :].unsqueeze(1).to_broadcast(wide), ALU.mult))
            next_step(12, dve.tensor_reduce(owner[:, :], passed[:, :, :], AX.X, ALU.add))
            next_step(13, dve.tensor_reduce(before[:, :], passed_n[:, :, :], AX.X, ALU.add))
            next_step(14, dve.tensor_tensor(offset[:, :], iota_c[:, :], before[:, :], ALU.subtract))
            next_step(15, dve.tensor_scalar(offset[:, :], offset[:, :], float(CHUNK), None, ALU.mult))
            next_step(16, dve.scalar_tensor_tensor(base[:, :], owner[:, :], float(STRIDE), offset[:, :], ALU.mult, ALU.add))
            next_step(17, dve.tensor_scalar(base[:, :], base[:, :], float(IDLE), None, ALU.min))
            next_step(18, dve.tensor_scalar(owner5[:, :], owner[:, :], float(EXPERTS - 1), None, ALU.min))
            next_step(19, dve.tensor_copy(base_i[:, :], base[:, :]))
            next_step(20, dve.tensor_copy(ends_i[:, :], t.ends[:, :]))
            dve.tensor_copy(owner_i[:, :], owner5[:, :]).then_inc(plan_ready, 1)

            for n in range(EXPERTS * LAYERS):
                e, l = n // LAYERS, n % LAYERS
                dve.wait_ge(raw_in[n % 2], (n // 2 + 1) * 16)
                dve.tensor_copy(all_hi[:, e, l, :, :], raw[n % 2][:, :, :]).then_inc(whi_ready, 1)
                dve.wait_ge(whi_ready, n + 1)
                dve.tensor_tensor(all_lo[:, e, l, :, :], raw[n % 2][:, :, :], all_hi[:, e, l, :, :].bitcast(F32),
                                  ALU.subtract).then_inc(wlo_ready, 1)
            dve.wait_ge(wlo_ready, EXPERTS * LAYERS)
            dve.wait_ge(biases_in, 48)
            dve.wait_ge(plan_ready, 1)

            def turn(c, s):
                e = dve.value_load(owner_i[0:1, bass.ds(c, 1)], min_val=0, max_val=EXPERTS - 1)
                at_least(dve, out_ready, (c - 1) * CU)
                dve.tensor_copy(cur_hi[:, s, :, :, :], all_hi[:, bass.ds(e, 1), :, :, :].squeeze(1).bitcast(F32)).then_inc(cur_ready, 1)
                dve.tensor_copy(cur_lo[:, s, :, :, :], all_lo[:, bass.ds(e, 1), :, :, :].squeeze(1).bitcast(F32)).then_inc(cur_ready, 1)
                at_least(dve, relu_ready, (c - 1) * ZC)
                dve.tensor_copy(bias[:, s, :, :], bias_all[:, :, bass.ds(e, 1), :].squeeze(2)).then_inc(bias_ready, 1)
                for h in range(2):
                    for k in range(KF):
                        dve.wait_ge(xhi_ready, (c * 2 + h) * KF + k + 1)
                        last = dve.tensor_tensor(act_lo[h][:, k, :], ps_x[k][:, :], act_hi[h][:, k, :].bitcast(F32),
                                                 ALU.subtract)
                    last.then_inc(xlo_ready, 1)
                dve.wait_ge(rows_in[s], (half(c, s) + 1) * 16)
                dve.tensor_scalar(first[:, s, :], rows[:, s, :, C_FIRST], owner5[:, bass.ds(c, 1)], None, ALU.is_equal
                                  ).then_inc(first_ready, 1)
                dve.wait_ge(first_ready, 2 * c + 1)
                dve.tensor_tensor(first[:, s, :], first[:, s, :], rows[:, s, :, C_DW], ALU.mult).then_inc(first_ready, 1)
                dve.wait_ge(first_ready, 2 * c + 2)
                at_least(dve, y_scaled, (c - 1) * CU)
                dve.tensor_tensor(weight[:, s, :], first[:, s, :], rows[:, s, :, C_W2], ALU.add).then_inc(weight_ready, 1)
                at_least(dve, added, (c - 1) * CU * 16)
                dve.tensor_copy(token[:, s, :], rows[:, s, :, C_TOKEN]).then_inc(token_ready, 1)
                for l in range(2):
                    for h in range(2):
                        for m in range(M):
                            i = l * 2 * M + h * M + m
                            dst = h + 2 * (1 - l)
                            dve.wait_ge(relu_ready, c * ZC + i + 1)
                            dve.tensor_copy(act_hi[dst][:, m, :], relu[:, m, :]).then_inc(ahi_ready, 1)
                            dve.wait_ge(ahi_ready, c * ZC + i + 1)
                            dve.tensor_tensor(act_lo[dst][:, m, :], relu[:, m, :], act_hi[dst][:, m, :].bitcast(F32),
                                              ALU.subtract).then_inc(alo_ready, 1)
                for n in range(CU):
                    dve.wait_ge(y_scaled, c * CU + n + 1)
                    dve.scalar_tensor_tensor(y[:, s, n, :], b3[:, bass.ds(e, 1), :].squeeze(1), weight[:, s, n:n + 1],
                                             y[:, s, n, :], ALU.mult, ALU.add).then_inc(y_ready, 1)
            turns(dve, turn)


class Kept:
    pass


def build(nc, A):
    with ExitStack() as ctx:
        def sb(name, shape, dt):
            return ctx.enter_context(nc.sbuf_tensor(name, shape, dt))
        k = Kept()
        k.ident = sb("ident", [P, P], F32)
        k.ends = sb("ends", [P, EXPERTS], F32)
        with ExitStack() as attention:
            def sa(name, shape, dt):
                return attention.enter_context(nc.sbuf_tensor(name, shape, dt))
            k.adj = sa("adj01", [P, BT, NODES], U8)
            k.col_pos = sa("col_pos", [P, TILES], F32)
            k.col_neg = sa("col_neg", [P, TILES], F32)
            k.row_pos = sa("row_pos", [P, TILES], F32)
            k.row_neg = sa("row_neg", [P, TILES], F32)
            k.neg_s2 = sa("neg_s2", [P, TILES], F32)
            k.alone = sa("alone", [P, BT], F32)
            k.col_parts = sa("col_parts", [P, TILES, 2, 2], F32R)
            project_stage(nc, k, A)
            attend_stage(nc, k, A)
        k.pad = sb("pad", [P, CU, ROW], F32)
        pad_stage(nc, k)
        expert_stage(nc, k, A)


_INS = [("x", (TOKENS, FEAT), F32), ("adjT", (NODES, NODES), I32), ("L0_gnn_W", (FEAT, FEAT), F32),
        ("L0_gnn_a", (2 * FEAT, 1), F32), ("L0_ffn_router_w1", (FEAT, RH), F32), ("L0_ffn_router_b1", (RH,), F32),
        ("L0_ffn_router_w2", (RH, EXPERTS), F32), ("L0_ffn_router_b2", (EXPERTS,), F32)]
_INS += [(f"L0_ffn_expert_w{i}", (EXPERTS, FEAT, FEAT), F32) for i in (1, 2, 3)]
_INS += [(f"L0_ffn_expert_b{i}", (EXPERTS, FEAT), F32) for i in (1, 2, 3)]


def kernel(**inputs):
    import concourse.bacc as bacc
    from concourse.bass_utils import run_bass_kernel_spmd as run

    nc = bacc.Bacc("TRN2", target_bir_lowering=False, num_devices=1)
    arrays, args = {}, {}
    for name, shape, dt in _INS:
        v = np.asarray(inputs["adj"]).T if name == "adjT" else inputs[name]
        arrays[name] = np.ascontiguousarray(v).reshape(shape)
        args[name] = nc.dram_tensor(name, shape, dt, kind="ExternalInput").ap()
    out = nc.dram_tensor("out", (OUT_ROWS, FEAT), F32, kind="ExternalOutput").ap()
    tokens = "(n u p) f -> n p u f"
    A = {
        "x": args["x"].rearrange(tokens, u=GT, p=P),
        "adjT": args["adjT"].rearrange("(k p) i -> k p i", p=P),
        "W": args["L0_gnn_W"], "a": args["L0_gnn_a"], "out": out,
        "x1": out[0:TOKENS, :].rearrange(tokens, u=GT, p=P),
        "out_pad": out[TOKENS:TOKENS+GW, :].rearrange("(u p) f -> p u f", u=GT),
        "out_pad2": out[TOKENS+GW:TOKENS+2*GW, :].rearrange("(u p) f -> p u f", u=GT),
        "out_pad3": out[TOKENS+2*GW:TOKENS+3*GW, :].rearrange("(u p) f -> p u f", u=GT),
        "out_pad4": out[TOKENS+3*GW:TOKENS+4*GW, :].rearrange("(u p) f -> p u f", u=GT),
        "router_w1": args["L0_ffn_router_w1"], "router_b1": args["L0_ffn_router_b1"],
        "router_w2": args["L0_ffn_router_w2"], "router_b2": args["L0_ffn_router_b2"],
        "w": [args[f"L0_ffn_expert_w{i}"] for i in (1, 2, 3)], "b1": args["L0_ffn_expert_b1"],
        "b2": args["L0_ffn_expert_b2"], "b3": args["L0_ffn_expert_b3"],
        "lists": nc.dram_tensor("lists", (LIST_ROWS, ROW), F32, kind="Internal").ap(),
        "h": nc.dram_tensor("h", (GROUPS, P, GT, FEAT), F32, kind="Internal").ap(),
    }
    s1 = nc.dram_tensor("s1_rows", (TOKENS,), F32, kind="Internal").ap()
    A["s1_save"] = s1.rearrange("(t p) -> t p", p=P)
    A["s1_rows"] = s1.rearrange("(n one i) -> n one i", one=1, i=GW)
    A["hmean_rows"] = nc.dram_tensor("hmean_rows", (BATCH, 1, FEAT), F32, kind="Internal").ap()
    build(nc, A)
    r = run(nc, [arrays], core_ids=[0])
    return r.results[0]["out"][:TOKENS].reshape(BATCH, NODES, FEAT)
```

```python
from contextlib import ExitStack

import numpy as np

import concourse.bass as bass
from concourse import mybir

ALU = mybir.AluOpType
ACT = mybir.ActivationFunctionType
AX = mybir.AxisListType
RMAX = bass.bass_isa.ReduceOp.max
F32 = mybir.dt.float32
F32R = mybir.dt.float32r
BF16 = mybir.dt.bfloat16
U8 = mybir.dt.uint8
I32 = mybir.dt.int32
U32 = mybir.dt.uint32

P = 128
BATCH, NODES, FEAT = 8, 2048, 256
TOKENS = BATCH * NODES
KF = FEAT // P
TILES = TOKENS // P
BT = NODES // P
GT = 2
GROUPS = TILES // GT
BG = BT // GT
GW = GT * P
EXPERTS, LAYERS, RH = 6, 3, 128
TOPK = 2
ROW = FEAT + 4
C_W2, C_DW, C_TOKEN, C_FIRST = range(FEAT, ROW)
CHUNK = 512
CU = CHUNK // P
PAIR = 2
TURNS = -(-(TOPK * TOKENS // CHUNK + EXPERTS - 1) // PAIR)
CHUNKS = TURNS * PAIR
STRIDE = TOKENS + CHUNK
IDLE = EXPERTS * STRIDE
LIST_ROWS = IDLE + CHUNK
OUT_ROWS = TOKENS + CHUNK
CH = 4
NC = BT // CH
XG = 2
XB = BG // XG
SLOTS = 2 * BT - CH
AHEAD = BG - 1
CENTER = 60.0
SLOPE = 0.2
EPS = 1e-5
SW = 2 * FEAT + 2


def at_least(eng, sem, value):
    if not (isinstance(value, int) and value <= 0):
        eng.wait_ge(sem, value)


def waits_apart(eng, passed, *waits):
    for sem, v in waits:
        at_least(eng, sem, v)
    eng.sem_inc(passed, 1)


def project_stage(nc, t, A):
    with ExitStack() as ctx:
        def sb(name, shape, dt):
            return ctx.enter_context(nc.sbuf_tensor(name, shape, dt))

        def sem(name):
            return ctx.enter_context(nc.semaphore(name))

        xin = sb("xin", [P, XB, XG * GT, FEAT], F32)
        stats = sb("stats1", [P, 2, GT, 6], F32)
        meanvar = sb("meanvar1", [P, 2, GT, 2], F32)
        std = sb("std1", [P, 2, GT], F32)
        rstd = sb("rstd1", [P, 2, GT], F32)
        eps = sb("eps1", [P, 1], F32)
        xn = sb("xn1", [P, 2, GT, FEAT], F32)
        xT_hi = sb("xT_hi", [P, 2, KF, GW], F32R)
        xT_lo = sb("xT_lo", [P, 2, KF, GW], F32R)
        w = sb("w_f32", [P, KF, FEAT + 2], F32)
        w_hi = sb("w_hi", [P, KF, FEAT + 2], F32R)
        w_lo = sb("w_lo", [P, KF, FEAT + 2], F32R)
        arow = sb("arow", [P, 2, FEAT], F32)
        junk = sb("junk", [P, 2, KF, FEAT], F32)
        hsb = sb("hsb", [P, 2, GT, FEAT], F32)
        score = sb("score", [P, TILES, 2], F32)
        xsum = sb("xsum", [P, GROUPS, KF], F32)
        bsum = sb("bsum", [P, KF, BATCH], F32)
        hmean = sb("hmean", [BATCH, FEAT], F32)
        raw = sb("adj_raw", [P, 2, NODES], I32)
        adj_bf = sb("adj_bf", [P, 2, NODES], BF16)
        ones = sb("ones_bf", [P, 2], BF16)
        mx = sb("mx", [P, BATCH], F32)
        mb = sb("mb", [P, BATCH], F32)
        s1 = sb("s1", [P, TILES], F32)
        s1T = sb("s1T", [P, TILES], F32)
        rel = sb("rel", [P, TILES], F32)
        relc = sb("relc", [P, TILES], F32)
        q = sb("q", [P, TILES], F32)
        qs = sb("qs", [P, TILES], F32)
        qc = sb("qc", [P, TILES], F32)
        top = sb("top", [P, TILES], F32)

        ps_T = ctx.enter_context(nc.psum_tensor("ps_T", [P, 2, KF, GW], F32))
        ps_h = ctx.enter_context(nc.psum_tensor("ps_h", [P, 2, GT, 512], F32))
        ps_deg = ctx.enter_context(nc.psum_tensor("ps_deg", [P, BT, 2], F32))
        ps_misc = ctx.enter_context(nc.psum_tensor("ps_misc", [P, 512], F32))

        weights_in = sem("weights_in")
        x_in = [sem(f"x_in{i}") for i in range(XB)]
        adj_in = [sem(f"adj_in{i}") for i in range(2)]
        consts = sem("consts")
        ident_zero = sem("ident_zero")
        ident_ready = sem("ident_ready")
        wa_ready = sem("wa_ready")
        whi_ready = sem("whi_ready")
        wlo_ready = sem("wlo_ready")
        stats_ready = sem("stats_ready")
        meanvar_ready = sem("meanvar_ready")
        stats_passed = sem("stats_passed")
        adj_passed = sem("adj_passed")
        std_ready = sem("std_ready")
        rstd_ready = sem("rstd_ready")
        xn_ready = sem("xn_ready")
        transposed = sem("transposed")
        xhi_ready = sem("xhi_ready")
        xlo_ready = sem("xlo_ready")
        h_ready = sem("h_ready")
        h_copied = sem("h_copied")
        h_saved = [sem(f"h_saved{i}") for i in range(2)]
        scores_copied = sem("scores_copied")
        adj_bytes = sem("adj_bytes")
        adj_float = sem("adj_float")
        deg_counted = sem("deg_counted")
        bsum_ready = sem("bsum_ready")
        hsum_ready = sem("hsum_ready")
        hmean_ready = sem("hmean_ready")
        rows_saved = sem("rows_saved")
        max_part = sem("max_part")
        max_ready = sem("max_ready")
        tail = sem("tail")
        exps_ready = sem("exps_ready")
        exp_in = sem("exp_in")
        s1_ready = sem("s1_ready")
        s1T_ready = sem("s1T_ready")
        s1T_copied = sem("s1T_copied")

        block = ctx.enter_context(nc.Block())

        def batches(eng, body):
            body(0)
            with eng.Fori(1, BATCH) as b:
                body(b)

        @block.sync
        def _(sp):
            sp.dma_start(w[:, :, 0:FEAT], A["W"].rearrange("(k p) f -> p k f", p=P)).then_inc(weights_in, 16)
            sp.dma_start(arow[:, :, :], A["a"].rearrange("(s f) one -> one s f", s=2).to_broadcast([P, 2, FEAT])
                         ).then_inc(weights_in, 16)

            def store(n, s):
                sp.wait_ge(h_copied, n + 1)
                sp.dma_start(A["h"][n], hsb[:, s, :, :]).then_inc(h_saved[s], 16)

            def load_x(b, j):
                at_least(sp, xn_ready, ((b - 1) * XB + j + 1) * XG * GT)
                sp.dma_start(xin[:, j, :, :], A["x_blocks"][b * XB + j]).then_inc(x_in[j], 16)

            def load_adj(b, j):
                at_least(sp, adj_float, (b - 1) * 2 + j + 1)
                sp.dma_start(raw[:, j, :], A["adjT"][b * 2 + j]).then_inc(adj_in[j], 16)

            def batch(b, more=True):
                for u in range(BG):
                    n = b * BG + u
                    if u > 2 or not isinstance(b, int) or b:
                        store(n - 3, (u + 1) % 2)
                    if u == 1 and not (isinstance(b, int) and b == 0):
                        load_x(b, XB - 1)
                    if u % 2 and u > 1 and more:
                        load_x(b + 1, (u - 3) // 2)
                    if u % 4 == 3 and more:
                        load_adj(b + 1, u // 4)
            for j in range(XB):
                load_x(0, j)
                if j % 2 == 0:
                    load_adj(0, j // 2)
            batch(0)
            with sp.Fori(1, BATCH - 1) as b:
                batch(b)
            batch(BATCH - 1, more=False)
            for n in range(GROUPS - 3, GROUPS):
                store(n, n % 2)
            sp.wait_ge(s1T_copied, 1)
            sp.dma_start(A["s1_save"], s1T[:, :]).then_inc(rows_saved, 16)
            sp.wait_ge(hmean_ready, 1)
            sp.dma_start(A["hmean_rows"][:, 0, :], hmean[:, :]).then_inc(rows_saved, 16)
            sp.wait_ge(rows_saved, 32)
            for s in range(2):
                sp.wait_ge(h_saved[s], GROUPS // 2 * 16)

        @block.gpsimd
        def _(pool):
            pool.memset(t.ident[:, :], 0.0).then_inc(ident_zero, 1)
            pool.memset(ones[:, :], 1.0).then_inc(consts, 1)
            pool.memset(eps[:, :], EPS).then_inc(consts, 1)
            pool.wait_ge(ident_zero, 1)
            pool.affine_select(out=t.ident[:, :], in_=t.ident[:, :], compare_op=ALU.not_equal, fill=1.0,
                               base=0, pattern=[[-1, P]], channel_multiplier=1).then_inc(ident_ready, 1)

            def batch(b):
                for s in range(2):
                    k = b * 2 + s
                    waits_apart(pool, adj_passed, (adj_in[s], (b + 1) * 16), (deg_counted, k - 1), (adj_bytes, k - 1))
                    pool.tensor_scalar(adj_bf[:, s, :], raw[:, s, :], 0.0, None, ALU.is_gt).then_inc(adj_float, 1)
            batches(pool, batch)
            pool.wait_ge(max_part, 1)
            pool.partition_all_reduce(mb[:, :], mx[:, :], P, RMAX).then_inc(max_ready, 1)

        @block.tensor
        def _(pe):
            def transposes(n, s):
                at_least(pe, xlo_ready, n - 1)
                pe.wait_ge(xn_ready, (n + 1) * GT)
                for k in range(KF):
                    for u in range(GT):
                        last = pe.transpose(ps_T[:, s, k, u * P:(u + 1) * P], xn[:, s, u, k * P:(k + 1) * P],
                                            t.ident[:, :])
                last.then_inc(transposed, 1)

            def project(n, s):
                at_least(pe, scores_copied, n - 1)
                pe.wait_ge(xlo_ready, n + 1)
                for u in range(GT):
                    for i, (l, r) in enumerate([(xT_hi, w_hi), (xT_hi, w_lo), (xT_lo, w_hi)]):
                        for k in range(KF):
                            last = pe.matmul(ps_h[:, s, u, 0:FEAT + 2], l[:, s, k, u * P:(u + 1) * P], r[:, k, :],
                                             start=(i == 0 and k == 0), stop=(i == 2 and k == KF - 1))
                last.then_inc(h_ready, 1)

            def count(b, s):
                k = b * 2 + s
                pe.wait_ge(adj_float, k + 1)
                for i in range(BT):
                    last = pe.matmul(ps_deg[:, i, :], adj_bf[:, s, i * P:(i + 1) * P], ones[:, :],
                                     start=(isinstance(b, int) and s == 0 and i == 0), stop=True,
                                     skip_group_check=True)
                last.then_inc(deg_counted, 1)

            def batch(b):
                for u in range(BG):
                    n = b * BG + u
                    transposes(n, u % 2)
                    if u or not isinstance(b, int):
                        project(n - 1, (u + 1) % 2)
                    if u % 4 == 3:
                        count(b, u // 4)
            pe.wait_ge(ident_ready, 1)
            pe.wait_ge(consts, 2)
            pe.wait_ge(wlo_ready, 1)
            batches(pe, batch)
            project(GROUPS - 1, 1)
            pe.wait_ge(bsum_ready, 1)
            for k in range(KF):
                last = pe.matmul(ps_misc[0:BATCH, 0:FEAT], bsum[:, k, :], w[:, k, 0:FEAT],
                                 start=(k == 0), stop=(k == KF - 1))
            last.then_inc(hsum_ready, 1)
            pe.wait_ge(s1_ready, 1)
            pe.wait_ge(hmean_ready, 1)
            pe.transpose(ps_misc[:, 0:TILES], s1[:, :], t.ident[:, :]).then_inc(s1T_ready, 1)

        @block.scalar
        def _(act):
            act.wait_ge(consts, 2)

            def rows(n, s):
                act.wait_ge(meanvar_ready, (n + 1) * GT)
                act.activation(std[:, s, :], meanvar[:, s, :, 1], ACT.Sqrt, bias=eps[:, 0:1]).then_inc(std_ready, 1)

            def split(n, s):
                act.wait_ge(transposed, n + 1)
                at_least(act, h_ready, n - 1)
                for k in range(KF):
                    last = act.activation(xT_hi[:, s, k, :], ps_T[:, s, k, :], ACT.Copy,
                                          accum_out=xsum[:, n, k:k + 1])
                last.then_inc(xhi_ready, 1)

            def save(n, s, n2):
                act.wait_ge(h_ready, n + 1)
                at_least(act, h_saved[s], n2 * 16)
                act.activation(hsb[:, s, :, :], ps_h[:, s, :, 0:FEAT], ACT.Copy).then_inc(h_copied, 1)
                act.activation(score[:, bass.ds(n * GT, GT), :], ps_h[:, s, :, FEAT:FEAT + 2], ACT.Copy
                               ).then_inc(scores_copied, 1)

            def batch(b):
                for u in range(BG):
                    n = b * BG + u
                    rows(n, u % 2)
                    if u or not isinstance(b, int):
                        split(n - 1, (u + 1) % 2)
                    if u > 2 or not isinstance(b, int):
                        save(n - 3, (u + 1) % 2, b * (BG // 2) + (u - 3) // 2)
                    if u % 4 == 3:
                        k = b * 2 + u // 4
                        act.wait_ge(adj_float, k + 1)
                        act.activation(t.adj[:, k, :], adj_bf[:, u // 4, :], ACT.Copy).then_inc(adj_bytes, 1)
            batches(act, batch)
            split(GROUPS - 1, 1)
            save(GROUPS - 3, 1, GROUPS // 2 - 2)
            save(GROUPS - 2, 0, GROUPS // 2 - 1)
            save(GROUPS - 1, 1, GROUPS // 2 - 1)
            act.wait_ge(exp_in, 1)
            act.activation(t.col_neg[:, :], rel[:, :], ACT.Exp, scale=SLOPE).then_inc(exps_ready, 1)
            act.activation(t.col_pos[:, :], relc[:, :], ACT.Exp).then_inc(exps_ready, 1)
            act.wait_ge(exp_in, 2)
            act.activation(t.row_pos[:, :], qc[:, :], ACT.Exp).then_inc(exps_ready, 1)
            act.activation(t.row_neg[:, :], qs[:, :], ACT.Exp).then_inc(exps_ready, 1)
        @block.vector
        def _(dve):
            dve.wait_ge(weights_in, 32)
            for s in range(2):
                for k in range(KF):
                    last = dve.tensor_tensor_reduce(junk[:, s, k, :], w[:, k, 0:FEAT], arow[:, s, :], 1.0, 0.0, ALU.mult,
                                                    ALU.add, w[:, k, FEAT + s:FEAT + s + 1])
                    last.then_inc(wa_ready, 1)
            dve.wait_ge(wa_ready, 4)
            dve.tensor_copy(w_hi[:, :, :], w[:, :, :]).then_inc(whi_ready, 1)
            dve.wait_ge(whi_ready, 1)
            dve.tensor_tensor(w_lo[:, :, :], w[:, :, :], w_hi[:, :, :].bitcast(F32), ALU.subtract).then_inc(wlo_ready, 1)

            def x_tile(j, u):
                return xin[:, j // XG, j % XG * GT + u, :]

            def moments_and_rows(n, j, b):
                s, o, before = j % 2, 1 - j % 2, j > 0 or not isinstance(b, int)
                if j % XG == 0:
                    dve.wait_ge(x_in[j // XG], (b + 1) * 16)
                for u in range(GT):
                    dve.bn_stats(stats[:, s, u, :], x_tile(j, u)).then_inc(stats_ready, 1)
                if before:
                    reciprocal(n - 1, o)
                waits_apart(dve, stats_passed, (stats_ready, (n + 1) * GT))
                for u in range(GT):
                    dve.bn_aggr(meanvar[:, s, u, :], stats[:, s, u, :]).then_inc(meanvar_ready, 1)
                if before:
                    normalise(n - 1, o, (j - 1) % BG)

            def reciprocal(n, s):
                dve.wait_ge(std_ready, n + 1)
                dve.reciprocal(rstd[:, s, :], std[:, s, :]).then_inc(rstd_ready, 1)

            def normalise(n, s, j):
                dve.wait_ge(rstd_ready, n + 1)
                at_least(dve, transposed, n - 1)
                for u in range(GT):
                    dve.tensor_scalar(xn[:, s, u, :], x_tile(j, u), meanvar[:, s, u, 0:1], rstd[:, s, u:u + 1],
                                      ALU.subtract, ALU.mult).then_inc(xn_ready, 1)

            def split(n, s):
                dve.wait_ge(xhi_ready, n + 1)
                at_least(dve, h_ready, n - 1)
                dve.tensor_tensor(xT_lo[:, s, :, :], ps_T[:, s, :, :], xT_hi[:, s, :, :].bitcast(F32), ALU.subtract
                                  ).then_inc(xlo_ready, 1)

            def batch(b):
                for u in range(BG):
                    n = b * BG + u
                    moments_and_rows(n, u, b)
                    if u > 1 or not isinstance(b, int):
                        split(n - 2, u % 2)
            batches(dve, batch)
            reciprocal(GROUPS - 1, 1)
            normalise(GROUPS - 1, 1, BG - 1)
            split(GROUPS - 2, 0)
            split(GROUPS - 1, 1)
            dve.wait_ge(xhi_ready, GROUPS)
            dve.tensor_reduce(bsum[:, :, :], xsum[:, :, :].rearrange("p (b g) k -> p k b g", b=BATCH), AX.X, ALU.add
                              ).then_inc(bsum_ready, 1)
            dve.wait_ge(scores_copied, GROUPS)
            s2 = score[:, :, 1]
            dve.tensor_reduce(mx[:, :], s2.rearrange("p (b t) -> p b t", b=BATCH), AX.X, ALU.max).then_inc(max_part, 1)
            dve.tensor_copy(s1[:, :], score[:, :, 0]).then_inc(s1_ready, 1)
            dve.tensor_scalar(t.neg_s2[:, :], s2, -1.0, None, ALU.mult).then_inc(tail, 1)
            dve.wait_ge(deg_counted, BT)
            dve.tensor_scalar(t.alone[:, :], ps_deg[:, :, 0], 0.0, None, ALU.is_equal).then_inc(tail, 1)
            dve.wait_ge(hsum_ready, 1)
            dve.tensor_scalar(hmean[:, :], ps_misc[0:BATCH, 0:FEAT], 1.0 / NODES, None, ALU.mult).then_inc(hmean_ready, 1)
            dve.wait_ge(s1T_ready, 1)
            dve.tensor_copy(s1T[:, :], ps_misc[:, 0:TILES]).then_inc(s1T_copied, 1)

            def of_batch(tile):
                return tile[:, :].rearrange("p (b t) -> p b t", b=BATCH)
            peak = mb[:, :].unsqueeze(2).to_broadcast([P, BATCH, BT])
            dve.wait_ge(max_ready, 1)
            dve.tensor_tensor(of_batch(rel), s2.rearrange("p (b t) -> p b t", b=BATCH), peak, ALU.subtract).then_inc(tail, 1)
            dve.tensor_tensor(of_batch(q), score[:, :, 0].rearrange("p (b t) -> p b t", b=BATCH), peak, ALU.add).then_inc(tail, 1)
            dve.wait_ge(tail, 4)
            dve.tensor_scalar(relc[:, :], rel[:, :], CENTER, None, ALU.add).then_inc(exp_in, 1)
            dve.tensor_scalar(qs[:, :], q[:, :], SLOPE, None, ALU.mult).then_inc(tail, 1)
            dve.tensor_scalar(qc[:, :], q[:, :], -CENTER, None, ALU.add).then_inc(tail, 1)
            dve.wait_ge(tail, 6)
            dve.tensor_tensor(top[:, :], qs[:, :], qc[:, :], ALU.max).then_inc(tail, 1)
            dve.wait_ge(tail, 7)
            dve.tensor_tensor(qs[:, :], qs[:, :], top[:, :], ALU.subtract).then_inc(tail, 1)
            dve.wait_ge(tail, 8)
            dve.tensor_tensor(qc[:, :], qc[:, :], top[:, :], ALU.subtract).then_inc(exp_in, 1)
            dve.wait_ge(exps_ready, 2)
            for i, col in enumerate((t.col_pos, t.col_neg)):
                dve.tensor_copy(t.col_parts[:, :, i, 0], col[:, :]).then_inc(tail, 1)
            dve.wait_ge(tail, 10)
            for i, col in enumerate((t.col_pos, t.col_neg)):
                dve.tensor_tensor(t.col_parts[:, :, i, 1], col[:, :], t.col_parts[:, :, i, 0].bitcast(F32),
                                  ALU.subtract).then_inc(tail, 1)


def attend_stage(nc, t, A):
    with ExitStack() as ctx:
        def sb(name, shape, dt):
            return ctx.enter_context(nc.sbuf_tensor(name, shape, dt))

        def sem(name):
            return ctx.enter_context(nc.semaphore(name))

        def psum(name, shape):
            return ctx.enter_context(nc.psum_tensor(name, shape, F32))

        scaled = sb("scaled", [P, SLOTS, 2, SW], F32R)
        mask_pos = sb("mask_pos", [P, BT, GW], F32R)
        mask_neg = sb("mask_neg", [P, BT, GW], F32R)
        s1row = sb("s1row", [P, 2, GW], F32)
        hmean = sb("hmean_all", [P, 2, FEAT], F32)
        hin = sb("hin", [P, GT, FEAT], F32)
        xres = sb("xres", [P, 2, GT, FEAT], F32)
        att = sb("att", [P, GT, FEAT + 2], F32)
        expo = sb("expo", [P, GT, FEAT], F32)
        xrow = sb("xrow", [P, 2, GT, ROW], F32)
        xT = sb("xT_router", [P, KF, GW], F32)
        rh = sb("rh", [P, GW], F32)
        wr1 = sb("wr1", [P, KF, RH], F32)
        wr2 = sb("wr2", [P, EXPERTS], F32)
        br1 = sb("br1", [P, 1], F32)
        br2 = sb("br2", [P, EXPERTS], F32)
        eps = sb("eps2", [P, 1], F32)
        tri = sb("tri", [P, P], BF16)
        ones = sb("ones2", [P, P], BF16)
        iota_e = sb("iota_e", [P, EXPERTS], F32)
        den = sb("den", [P, GT], F32)
        den1 = sb("den1", [P, GT], F32)
        rden = sb("rden", [P, GT], F32)
        stats = sb("stats2", [P, GT, 6], F32)
        meanvar = sb("meanvar2", [P, GT, 2], F32)
        std = sb("std2", [P, GT], F32)
        rstd = sb("rstd2", [P, GT], F32)
        logits = sb("logits", [P, GT, 8], F32)
        best = sb("best", [P, GT, 8], F32)
        bidx = sb("bidx", [P, GT, 8], U32)
        exin = sb("exin", [P, GT, EXPERTS + 1], F32)
        exout = sb("exout", [P, GT, EXPERTS + 1], F32)
        idxf = sb("idxf", [P, GT, TOPK], F32)
        chosen = sb("chosen", [P, GT, TOPK, EXPERTS], F32)
        sel = sb("sel", [P, GT, EXPERTS], BF16)
        prob = sb("prob", [P, 4, GT], F32)
        edif = sb("edif", [P, GT], F32)
        rank = sb("rank", [P, 2, GT, 2, EXPERTS], F32)
        place = sb("place", [P, GT, TOPK, EXPERTS], F32)
        posf = sb("posf", [P, GT, TOPK], F32)
        pos = sb("pos", [P, 2, GT, TOPK], I32)

        u_pos = [psum(f"u_pos{i}", [P, 512]) for i in range(GT)]
        u_neg = [psum(f"u_neg{i}", [P, 512]) for i in range(GT)]
        ps_xT = psum("ps_xT", [P, KF, GW])
        ps_rh = psum("ps_rh", [P, 512])
        ps_lg = psum("ps_lg", [P, 512])
        ps_rk = psum("ps_rk", [P, 512])
        lg = ps_lg[:, 0:GT * 8].rearrange("p (u e) -> p u e", u=GT)
        rk = ps_rk[:, 0:2 * GT * EXPERTS].rearrange("p (s u e) -> p s u e", s=2, u=GT)

        small_in = sem("small_in")
        const_zero = sem("const_zero")
        const_ready = sem("const_ready")
        s1_in = [sem(f"s1_in{i}") for i in range(2)]
        hm_in = [sem(f"hm_in{i}") for i in range(2)]
        xr_in = [sem(f"xr_in{i}") for i in range(2)]
        first_h_in = sem("first_h_in")
        h_in = sem("h_in")
        hi_ready = sem("hi_ready")
        parts_ready = sem("parts_ready")
        lo_ready = sem("lo_ready")
        mp_ready = sem("mp_ready")
        pos_passed = sem("pos_passed")
        adj_ready = sem("adj_ready")
        mm_ready = sem("mm_ready")
        masks_used = sem("masks_used")
        u_ready = sem("u_ready")
        v_ready = sem("v_ready")
        att_ready = sem("att_ready")
        den_ready = sem("den_ready")
        den1_ready = sem("den1_ready")
        rden_ready = sem("rden_ready")
        mean_added = sem("mean_added")
        expo_ready = sem("expo_ready")
        elu_pos = sem("elu_pos")
        elu_ready = sem("elu_ready")
        x1_ready = sem("x1_ready")
        x1_saved = [sem(f"x1_saved{i}") for i in range(2)]
        stats_ready = sem("stats2_ready")
        stats_passed = sem("stats2_passed")
        meanvar_ready = sem("meanvar2_ready")
        std_ready = sem("std2_ready")
        rstd_ready = sem("rstd2_ready")
        xn_ready = sem("xn2_ready")
        xT_ready = sem("xT_ready")
        xT_copied = sem("xT_copied")
        rh_ready = sem("rh_ready")
        rh_copied = sem("rh_copied")
        logits_ready = sem("logits_ready")
        route = sem("route")
        route_passed = sem("route_passed")
        exin_ready = sem("exin_ready")
        exout_ready = sem("exout_ready")
        edif_in = sem("edif_in")
        edif_ready = sem("edif_ready")
        sel_ready = sem("sel_ready")
        rank_ready = sem("rank_ready")
        pos_ready = sem("pos_ready")
        scattered = [sem(f"scattered{i}") for i in range(2)]
        counts_ready = sem("counts_ready")
        zero_ready = sem("zero_ready")
        zero_saved = sem("zero_saved")

        (R_LOGITS, R_BEST0, R_BEST1, R_IDX0, R_IDX1, R_DIF, R_IDXF, R_CHOSEN, R_SUM, R_RSUM, R_ONE, R_W1, R_W2,
         R_RANK0, R_DW, R_RANK1, R_TOK, R_FIRST, R_PLACE, R_POSF) = range(1, 21)
        STEPS = 20

        block = ctx.enter_context(nc.Block())

        def first_h(m):
            return lambda u: mask_pos[:, m * GT + u, :].bitcast(F32)

        def later_h(u):
            return hin[:, u, :]

        def pipeline(eng, body):
            for n in range(4):
                body(n, n % 2, True)
            with eng.Fori(2, (GROUPS - BG) // 2) as i:
                for s in range(2):
                    body(i * 2 + s, s, True)
            body(GROUPS - BG, 0, True)
            body(GROUPS - BG + 1, 1, False)
            with eng.Fori((GROUPS - BG) // 2 + 1, GROUPS // 2) as i:
                for s in range(2):
                    body(i * 2 + s, s, False)
            for n in range(GROUPS, GROUPS + 3):
                body(n, n % 2, False)

        def runs(n, lag=0):
            return not isinstance(n, int) or lag <= n < GROUPS + lag

        def half(n, s):
            return (n - s) // 2 if isinstance(n, int) else (n - s) // 2

        @block.sync
        def _(sp):
            sp.dma_start(wr1[:, :, :], A["router_w1"].rearrange("(k p) f -> p k f", p=P)).then_inc(small_in, 16)
            sp.dma_start(wr2[:, :], A["router_w2"]).then_inc(small_in, 16)
            sp.dma_start(br1[:, :], A["router_b1"].rearrange("(p one) -> p one", one=1)).then_inc(small_in, 16)
            sp.dma_start(br2[:, :], A["router_b2"].rearrange("(one e) -> one e", one=1).to_broadcast([P, EXPERTS])
                         ).then_inc(small_in, 16)

            def load_h(m):
                at_least(sp, lo_ready, m * 2 * GT)
                sp.dma_start(hin[:, :, :], A["h"][m]).then_inc(h_in, 16)
            sp.dma_start(mask_pos[:, 0:AHEAD * GT, :].rearrange("p (g u) f -> p g u f", u=GT).bitcast(F32),
                         A["h"][0:AHEAD].rearrange("g p u f -> p g u f")).then_inc(first_h_in, 16)

            def body(n, s, ahead):
                if runs(n):
                    at_least(sp, mp_ready, (n - 1) * BT)
                    sp.dma_start(s1row[:, s, :], A["s1_rows"][n].to_broadcast([P, GW])).then_inc(s1_in[s], 16)
                    if not isinstance(n, int) or n >= 2:
                        sp.wait_ge(mean_added, (n - 1) * GT)
                    sp.dma_start(hmean[:, s, :], A["hmean_rows"][n // BG].to_broadcast([P, FEAT])).then_inc(hm_in[s], 16)
                    if ahead:
                        load_h(n + AHEAD)
                if runs(n, 2):
                    m = n - 2
                    sp.wait_ge(x1_ready, m + 1)
                    sp.dma_start(A["x1"][m], xres[:, s, :, :]).then_inc(x1_saved[s], 16)
                if runs(n):
                    if not isinstance(n, int) or n >= 2:
                        sp.wait_ge(x1_saved[s], half(n, s) * 16)
                        sp.wait_ge(xn_ready, (n - 1) * GT)
                    sp.dma_start(xres[:, s, :, :], A["x"][n]).then_inc(xr_in[s], 16)
            pipeline(sp, body)
            for s in range(2):
                sp.wait_ge(x1_saved[s], GROUPS // 2 * 16)
            sp.wait_ge(zero_ready, 1)
            sp.dma_start(A["out_pad"], hin[:, :, :]).then_inc(zero_saved, 16)
            sp.dma_start(A["out_pad2"], hin[:, :, :]).then_inc(zero_saved, 16)
            sp.wait_ge(zero_saved, 32)

        @block.gpsimd
        def _(pool):
            pool.memset(eps[:, :], EPS).then_inc(const_zero, 1)
            pool.memset(ones[:, :], 1.0).then_inc(const_zero, 1)
            pool.memset(logits[:, :, :], -3.0e38).then_inc(const_zero, 1)
            pool.iota(iota_e[:, :], [[1, EXPERTS]], base=0, channel_multiplier=0,
                      allow_small_or_imprecise_dtypes=True).then_inc(const_zero, 1)
            pool.iota(rank[:, 1, 1, 1, :], [[STRIDE, EXPERTS]], base=0, channel_multiplier=0,
                      allow_small_or_imprecise_dtypes=True).then_inc(const_zero, 1)
            pool.iota(xrow[:, 1, :, C_TOKEN], [[P, GT]], base=-GW, channel_multiplier=1,
                      allow_small_or_imprecise_dtypes=True).then_inc(const_zero, 1)
            pool.wait_ge(const_zero, 6)
            pool.affine_select(out=tri[:, :], in_=ones[:, :], compare_op=ALU.is_gt, fill=0.0, base=0,
                               pattern=[[1, P]], channel_multiplier=-1).then_inc(const_ready, 1)

            def body(n, s, ahead):
                if runs(n):
                    for c in range(NC):
                        r = slice(c * CH, (c + 1) * CH)
                        pool.wait_ge(adj_ready, n * NC + c + 1)
                        pool.wait_ge(mp_ready, n * BT + (c + 1) * CH)
                        pool.tensor_tensor(mask_neg[:, r, :], mask_neg[:, r, :].bitcast(F32),
                                           mask_pos[:, r, :].bitcast(F32), ALU.subtract).then_inc(mm_ready, 1)
                if runs(n, 3):
                    m = n - 3
                    o = 1 - s
                    waits_apart(pool, pos_passed, (pos_ready, m + 1))
                    for u in range(GT):
                        for k in range(TOPK):
                            pool.indirect_dma_start(
                                A["lists"], bass.IndirectOffsetOnAxis(ap=pos[:, o, u, k:k + 1].bitcast(U32), axis=0),
                                xrow[:, o, u, :], None, bounds_check=LIST_ROWS - 1).then_inc(scattered[o], 16)
            pipeline(pool, body)
            for s in range(2):
                pool.wait_ge(scattered[s], GROUPS // 2 * 16 * GT * TOPK)

        @block.tensor
        def _(pe):
            def attend(n, c):
                pe.wait_ge(mm_ready, n * NC + c + 1)
                if c == 0:
                    pe.wait_ge(parts_ready, n // BG * BG + AHEAD)
                    pe.wait_ge(lo_ready, (n // BG * BG + AHEAD) * 2 * GT)
                if c == NC - 1:
                    pe.wait_ge(parts_ready, (n // BG + 1) * BG)
                    pe.wait_ge(lo_ready, (n // BG + 1) * BG * 2 * GT)
                for u in range(GT):
                    if c == 0:
                        at_least(pe, att_ready, (n - 1) * GT + u + 1)
                    for j in range(c * CH, (c + 1) * CH):
                        slot = (n // BG * BT + c * CH) % SLOTS + j % CH
                        for i, (mask, acc) in enumerate(((mask_pos, u_pos[u]), (mask_neg, u_neg[u]))):
                            st = mask[:, j, u * P:(u + 1) * P]
                            pe.matmul(acc[:, 0:FEAT + 2], st, scaled[:, slot, i, 0:FEAT + 2], start=(j == 0), stop=False,
                                      skip_group_check=True)
                            last = pe.matmul(acc[:, 0:FEAT], st, scaled[:, slot, i, FEAT + 2:SW], start=False,
                                             stop=(j == BT - 1), skip_group_check=True)
                    if u == 1:
                        last.then_inc(masks_used, 1)
                    if u == 0 and c == NC - 1:
                        last.then_inc(u_ready, 1)

            def turn_rows(m, s):
                pe.wait_ge(xn_ready, (m + 1) * GT)
                at_least(pe, xT_copied, m)
                for k in range(KF):
                    for u in range(GT):
                        last = pe.transpose(ps_xT[:, k, u * P:(u + 1) * P], xrow[:, s, u, k * P:(k + 1) * P],
                                            t.ident[:, :])
                last.then_inc(xT_ready, 1)

            def router_hidden(m):
                pe.wait_ge(xT_copied, m + 1)
                at_least(pe, rh_copied, m)
                for k in range(KF):
                    last = pe.matmul(ps_rh[:, 0:GW], wr1[:, k, :], xT[:, k, :], start=(k == 0), stop=(k == KF - 1))
                last.then_inc(rh_ready, 1)

            def router_logits(m):
                pe.wait_ge(rh_copied, m + 1)
                at_least(pe, route, (m - 1) * STEPS + R_LOGITS)
                for u in range(GT):
                    last = pe.matmul(lg[:, u, 0:EXPERTS], rh[:, u * P:(u + 1) * P], wr2[:, :], start=(u == 0),
                                     stop=True, skip_group_check=True)
                last.then_inc(logits_ready, 1)

            def count_ranks(m):
                pe.wait_ge(sel_ready, m + 1)
                for i, w in enumerate((tri, ones)):
                    last = pe.matmul(ps_rk[:, i * GT * EXPERTS:(i + 1) * GT * EXPERTS], w[:, :],
                                     sel[:, :, :], start=(i == 0), stop=True, skip_group_check=True)
                last.then_inc(rank_ready, 1)

            def body(n, s, ahead):
                if runs(n, 2):
                    turn_rows(n - 2, s)
                if runs(n, 3):
                    count_ranks(n - 3)
                if runs(n):
                    attend(n, 0)
                if runs(n, 2):
                    router_hidden(n - 2)
                if runs(n):
                    attend(n, 1)
                if runs(n, 2):
                    router_logits(n - 2)
                if runs(n):
                    attend(n, 2)
                    attend(n, 3)
            pe.wait_ge(small_in, 64)
            pe.wait_ge(const_ready, 1)
            pipeline(pe, body)

        @block.scalar
        def _(act):
            act.wait_ge(const_zero, 6)
            act.wait_ge(small_in, 64)

            def scale(m, h_tile):
                for u in range(GT):
                    slot = (m * GT + u) % SLOTS
                    for i, col in enumerate((t.col_pos, t.col_neg)):
                        act.activation(scaled[:, slot, i, 0:FEAT], h_tile(u), ACT.Copy,
                                       scale=col[:, bass.ds(m * GT + u, 1)]).then_inc(hi_ready, 1)
                act.activation(scaled[:, bass.ds(m * GT % SLOTS, GT), :, FEAT:FEAT + 2],
                               t.col_parts[:, bass.ds(m * GT, GT), :, :].bitcast(F32), ACT.Copy).then_inc(parts_ready, 1)

            act.wait_ge(first_h_in, 16)
            for m in range(AHEAD):
                scale(m, first_h(m))

            def spread(n, c):
                at_least(act, masks_used, (n - 1) * NC + c + 1)
                act.activation(mask_neg[:, c * CH:(c + 1) * CH, :],
                               t.adj[:, c * CH:(c + 1) * CH, bass.ds((n % BG) * GW, GW)], ACT.Copy
                               ).then_inc(adj_ready, 1)

            def body(n, s, ahead):
                if runs(n):
                    spread(n, 0)
                    spread(n, 1)
                if runs(n, 3):
                    act.wait_ge(exin_ready, n - 3 + 1)
                    act.activation(exout[:, :, :], exin[:, :, :], ACT.Exp).then_inc(exout_ready, 1)
                if runs(n, 1):
                    m = n - 1
                    for u in range(GT):
                        if u == 0:
                            act.wait_ge(u_ready, m + 1)
                            at_least(act, elu_ready, m)
                        else:
                            act.wait_ge(masks_used, (m + 1) * NC)
                        act.activation(att[:, u, :], u_pos[u][:, 0:FEAT + 2], ACT.Copy,
                                       scale=t.row_pos[:, bass.ds(m * GT + u, 1)]).then_inc(v_ready, 1)
                if runs(n, 3):
                    act.wait_ge(edif_in, n - 3 + 1)
                    act.activation(edif[:, :], prob[:, 2, :], ACT.Exp).then_inc(edif_ready, 1)
                if runs(n, 2):
                    act.wait_ge(xT_ready, n - 2 + 1)
                    act.activation(xT[:, :, :], ps_xT[:, :, :], ACT.Copy).then_inc(xT_copied, 1)
                if runs(n):
                    spread(n, 2)
                    spread(n, 3)
                if runs(n, 1):
                    act.wait_ge(rden_ready, m + 1)
                    act.wait_ge(mean_added, (m + 1) * GT)
                    for u in range(GT):
                        act.activation(expo[:, u, :], att[:, u, 0:FEAT], ACT.Exp, scale=rden[:, u:u + 1]
                                       ).then_inc(expo_ready, 1)
                    act.wait_ge(expo_ready, (m + 1) * GT)
                    for u in range(GT):
                        act.activation(att[:, u, 0:FEAT], att[:, u, 0:FEAT], ACT.Relu, scale=rden[:, u:u + 1]
                                       ).then_inc(elu_pos, 1)
                if runs(n, 2):
                    act.wait_ge(rh_ready, n - 2 + 1)
                    act.activation(rh[:, :], ps_rh[:, 0:GW], ACT.Relu, bias=br1[:, 0:1]).then_inc(rh_copied, 1)
                if runs(n) and ahead:
                    act.wait_ge(masks_used, n * NC + 1)
                    act.wait_ge(h_in, (n + 1) * 16)
                    scale(n + AHEAD, later_h)
                if runs(n, 1):
                    act.wait_ge(meanvar_ready, (m + 1) * GT)
                    act.activation(std[:, :], meanvar[:, :, 1], ACT.Sqrt, bias=eps[:, 0:1]).then_inc(std_ready, 1)
            pipeline(act, body)

        @block.vector
        def _(dve):
            def scale(m, h_tile):
                dve.wait_ge(hi_ready, (m + 1) * 2 * GT)
                for u in range(GT):
                    slot = (m * GT + u) % SLOTS
                    for i, col in enumerate((t.col_pos, t.col_neg)):
                        dve.scalar_tensor_tensor(scaled[:, slot, i, FEAT + 2:SW], h_tile(u),
                                                 col[:, bass.ds(m * GT + u, 1)],
                                                 scaled[:, slot, i, 0:FEAT].bitcast(F32), ALU.mult, ALU.subtract
                                                 ).then_inc(lo_ready, 1)
            for m in range(AHEAD):
                scale(m, first_h(m))
            dve.wait_ge(lo_ready, AHEAD * 2 * GT)

            def masks_of(n, s):
                def mask(j):
                    if not runs(n):
                        return
                    if j == 0:
                        dve.wait_ge(s1_in[s], (half(n, s) + 1) * 16)
                    if j % CH == 0:
                        at_least(dve, masks_used, (n - 1) * NC + j // CH + 1)
                    dve.scalar_tensor_tensor(mask_pos[:, j, :], s1row[:, s, :],
                                             t.neg_s2[:, bass.ds(n // BG * BT + j, 1)],
                                             t.adj[:, j, bass.ds((n % BG) * GW, GW)], ALU.is_gt, ALU.mult
                                             ).then_inc(mp_ready, 1)
                return mask

            def take_out(m, s, u):
                dve.wait_ge(v_ready, m * GT + u + 1)
                dve.scalar_tensor_tensor(att[:, u, :], u_neg[u][:, 0:FEAT + 2], t.row_neg[:, bass.ds(m * GT + u, 1)],
                                         att[:, u, :], ALU.mult, ALU.add).then_inc(att_ready, 1)

            def finish_a(m, s, mask):
                tile = (m % BG) * GT
                dve.wait_ge(att_ready, (m + 1) * GT)
                dve.tensor_tensor(den[:, :], att[:, :, FEAT], att[:, :, FEAT + 1], ALU.add).then_inc(den_ready, 1)
                dve.wait_ge(hm_in[s], (half(m, s) + 1) * 16)
                for u in range(GT):
                    dve.scalar_tensor_tensor(att[:, u, 0:FEAT], hmean[:, s, :], t.alone[:, bass.ds(tile + u, 1)],
                                             att[:, u, 0:FEAT], ALU.mult, ALU.add).then_inc(mean_added, 1)
                dve.wait_ge(den_ready, m + 1)
                dve.tensor_tensor(den1[:, :], den[:, :], t.alone[:, bass.ds(tile, GT)], ALU.add).then_inc(den1_ready, 1)
                mask(9)
                dve.wait_ge(den1_ready, m + 1)
                dve.reciprocal(rden[:, :], den1[:, :]).then_inc(rden_ready, 1)

            def elu(m):
                dve.wait_ge(expo_ready, (m + 1) * GT)
                dve.wait_ge(elu_pos, (m + 1) * GT)
                dve.scalar_tensor_tensor(expo[:, :, :], expo[:, :, :], 1.0, att[:, :, 0:FEAT], ALU.min, ALU.add
                                         ).then_inc(elu_ready, 1)

            def residual(m, s):
                dve.wait_ge(elu_ready, m + 1)
                dve.wait_ge(xr_in[s], (half(m, s) + 1) * 16)
                dve.scalar_tensor_tensor(xres[:, s, :, :], expo[:, :, :], -1.0, xres[:, s, :, :], ALU.add, ALU.add
                                         ).then_inc(x1_ready, 1)

            def moments(m, s):
                dve.wait_ge(x1_ready, m + 1)
                for u in range(GT):
                    dve.bn_stats(stats[:, u, :], xres[:, s, u, :]).then_inc(stats_ready, 1)
                waits_apart(dve, stats_passed, (stats_ready, (m + 1) * GT))
                for u in range(GT):
                    dve.bn_aggr(meanvar[:, u, :], stats[:, u, :]).then_inc(meanvar_ready, 1)

            def normalise(m, s, mask):
                dve.wait_ge(std_ready, m + 1)
                dve.reciprocal(rstd[:, :], std[:, :]).then_inc(rstd_ready, 1)
                mask(7)
                dve.wait_ge(rstd_ready, m + 1)
                at_least(dve, scattered[s], half(m, s) * 16 * GT * TOPK)
                for u in range(GT):
                    dve.tensor_scalar(xrow[:, s, u, 0:FEAT], xres[:, s, u, :], meanvar[:, u, 0:1], rstd[:, u:u + 1],
                                      ALU.subtract, ALU.mult).then_inc(xn_ready, 1)

            def step(m, k, ins):
                ins.then_inc(route, 1)

            def need(m, k):
                dve.wait_ge(route, m * STEPS + k)

            def choose(m, s, mask):
                mask(0)
                dve.wait_ge(logits_ready, m + 1)
                step(m, R_LOGITS, dve.tensor_tensor(
                    logits[:, :, 0:EXPERTS], lg[:, :, 0:EXPERTS],
                    br2[:, :].unsqueeze(1).to_broadcast([P, GT, EXPERTS]), ALU.add))
                mask(1)
                waits_apart(dve, route_passed, (route, m * STEPS + R_LOGITS))
                for u in range(GT):
                    step(m, R_BEST0 + u, dve.max(best[:, u, :], logits[:, u, :]))
                mask(2)
                waits_apart(dve, route_passed, (route, m * STEPS + R_BEST1))
                for u in range(GT):
                    step(m, R_IDX0 + u, dve.max_index(bidx[:, u, :], best[:, u, :], logits[:, u, :]))
                step(m, R_DIF, dve.tensor_tensor(exin[:, :, 0:EXPERTS], logits[:, :, 0:EXPERTS],
                                                 best[:, :, 0:1].to_broadcast([P, GT, EXPERTS]), ALU.subtract))
                mask(3)
                dve.wait_ge(route, m * STEPS + R_DIF)
                dve.tensor_tensor(exin[:, :, EXPERTS], best[:, :, 1], best[:, :, 0], ALU.subtract
                                  ).then_inc(exin_ready, 1)
                step(m, R_IDXF, dve.tensor_copy(idxf[:, :, :], bidx[:, :, 0:TOPK]))
                mask(4)
                need(m, R_IDXF)
                step(m, R_CHOSEN, dve.tensor_tensor(
                    chosen[:, :, :, :], idxf[:, :, :].unsqueeze(3).to_broadcast([P, GT, TOPK, EXPERTS]),
                    iota_e[:, :].unsqueeze(1).unsqueeze(1).to_broadcast([P, GT, TOPK, EXPERTS]), ALU.is_equal))
                mask(5)
                need(m, R_CHOSEN)
                dve.tensor_tensor(sel[:, :, :], chosen[:, :, 0, :], chosen[:, :, 1, :], ALU.add).then_inc(sel_ready, 1)
                mask(6)

            def weigh(m, s, mask):
                dve.wait_ge(exout_ready, m + 1)
                step(m, R_SUM, dve.tensor_reduce(prob[:, 0, :], exout[:, :, 0:EXPERTS], AX.X, ALU.add))
                mask(8)
                need(m, R_SUM)
                step(m, R_RSUM, dve.reciprocal(prob[:, 1, :], prob[:, 0, :]))
                need(m, R_RSUM)
                dve.scalar_tensor_tensor(prob[:, 2, :], exout[:, :, EXPERTS], -1.0, prob[:, 1, :], ALU.add, ALU.mult
                                         ).then_inc(edif_in, 1)

            def pair_weights(m, s, mask):
                dve.wait_ge(edif_ready, m + 1)
                step(m, R_ONE, dve.tensor_scalar(prob[:, 0, :], edif[:, :], 1.0, None, ALU.add))
                mask(10)
                need(m, R_ONE)
                step(m, R_W1, dve.reciprocal(prob[:, 3, :], prob[:, 0, :]))
                mask(11)
                need(m, R_W1)
                step(m, R_W2, dve.tensor_tensor(xrow[:, s, :, C_W2], edif[:, :], prob[:, 3, :], ALU.mult))
                dve.wait_ge(rank_ready, m + 1)
                step(m, R_RANK0, dve.tensor_tensor(
                    rank[:, s, 0, :, :], rk[:, :, 0, :],
                    rank[:, 1 - s, 1, 1, :].unsqueeze(1).to_broadcast([P, 2, EXPERTS]), ALU.add))
                mask(12)
                need(m, R_RANK0)
                step(m, R_DW, dve.tensor_tensor(xrow[:, s, :, C_DW], prob[:, 3, :], xrow[:, s, :, C_W2], ALU.subtract))
                step(m, R_RANK1, dve.tensor_tensor(
                    rank[:, s, 1, :, :], rk[:, :, 1, :],
                    rank[:, s, 0, 1, :].unsqueeze(1).to_broadcast([P, 2, EXPERTS]), ALU.add))
                step(m, R_TOK, dve.tensor_scalar(xrow[:, s, :, C_TOKEN], xrow[:, 1 - s, :, C_TOKEN], float(GW), None,
                                                 ALU.add))
                step(m, R_FIRST, dve.tensor_copy(xrow[:, s, :, C_FIRST], idxf[:, :, 0]))
                mask(13)
                mask(14)
                need(m, R_RANK1)
                step(m, R_PLACE, dve.tensor_tensor(
                    place[:, :, :, :], chosen[:, :, :, :],
                    rank[:, s, :, 0, :].unsqueeze(2).to_broadcast([P, GT, TOPK, EXPERTS]), ALU.mult))

            def position(m, s):
                need(m, R_PLACE)
                step(m, R_POSF, dve.tensor_reduce(posf[:, :, :], place[:, :, :, :], AX.X, ALU.add))

            def place_rows(m, s):
                need(m, R_POSF)
                dve.tensor_copy(pos[:, s, :, :], posf[:, :, :]).then_inc(pos_ready, 1)

            def body(n, s, ahead):
                o = 1 - s
                mask = masks_of(n, s)
                if runs(n, 3):
                    choose(n - 3, o, mask)
                else:
                    for j in range(0, 7):
                        mask(j)
                if runs(n, 2):
                    normalise(n - 2, s, mask)
                else:
                    mask(7)
                if runs(n, 3):
                    weigh(n - 3, o, mask)
                else:
                    mask(8)
                if runs(n, 1):
                    for u in range(GT):
                        take_out(n - 1, o, u)
                    finish_a(n - 1, o, mask)
                else:
                    mask(9)
                if runs(n, 3):
                    pair_weights(n - 3, o, mask)
                else:
                    for j in range(10, 15):
                        mask(j)
                mask(15)
                if runs(n, 1):
                    elu(n - 1)
                if runs(n, 3):
                    position(n - 3, o)
                if runs(n, 1):
                    residual(n - 1, o)
                if runs(n, 3):
                    place_rows(n - 3, o)
                if runs(n, 1):
                    moments(n - 1, o)
                if runs(n) and ahead:
                    scale(n + AHEAD, later_h)
            dve.wait_ge(small_in, 64)
            dve.wait_ge(const_ready, 1)
            pipeline(dve, body)
            dve.memset(hin[:, :, :], 0.0).then_inc(zero_ready, 1)
            dve.wait_ge(route, GROUPS * STEPS)
            dve.tensor_copy(t.ends[:, :], rank[:, 1, 1, 1, :]).then_inc(counts_ready, 1)


def expert_stage(nc, t, A):
    with ExitStack() as ctx:
        def sb(name, shape, dt):
            return ctx.enter_context(nc.sbuf_tensor(name, shape, dt))

        def sem(name):
            return ctx.enter_context(nc.semaphore(name))

        def psum(name, shape):
            return ctx.enter_context(nc.psum_tensor(name, shape, F32))

        M = FEAT // P
        all_hi = sb("all_hi", [P, EXPERTS, LAYERS, KF, FEAT], F32R)
        all_lo = sb("all_lo", [P, EXPERTS, LAYERS, KF, FEAT], F32R)
        cur_hi = sb("cur_hi", [P, 2, PAIR, 2, KF, FEAT], F32R)
        cur_lo = sb("cur_lo", [P, 2, PAIR, 2, KF, FEAT], F32R)
        bias_all = sb("bias_all", [P, 2, EXPERTS, M], F32)
        bias = sb("bias", [P, 2, PAIR, 2, M], F32)
        b3 = sb("b3", [P, EXPERTS, FEAT], F32)
        b3_cur = sb("b3_cur", [P, 2, PAIR, FEAT], F32)
        rows = sb("rows", [P, 2, PAIR, CU, ROW], F32)
        x_hi, a1_hi, a2_hi = ([sb(f"{n}_hi{h}", [P, KF, CHUNK], F32R) for h in range(PAIR)] for n in ("x", "a1", "a2"))
        x_lo, a1_lo, a2_lo = ([sb(f"{n}_lo{h}", [P, KF, CHUNK], F32R) for h in range(PAIR)] for n in ("x", "a1", "a2"))
        relu = sb("relu", [P, 2, CHUNK], F32)
        y = sb("y", [P, 2, PAIR, CU, FEAT], F32)
        RAWS = 2 * PAIR * CU // KF
        pad = rows[:, 0, 0, :, :]
        first = sb("first", [P, 2, PAIR, CU], F32)
        weight = sb("weight", [P, 2, PAIR, CU], F32)
        token = sb("token", [P, 2, PAIR, CU], I32)
        iota_m = sb("iota_m", [P, TOKENS // CHUNK], F32)
        iota_c = sb("iota_c", [P, CHUNKS], F32)
        starts = sb("starts", [P, EXPERTS], F32)
        counts = sb("counts", [P, EXPERTS], F32)
        more = sb("more", [P, EXPERTS, TOKENS // CHUNK], F32)
        chunks = sb("chunks", [P, EXPERTS], F32)
        upto = sb("upto", [P, EXPERTS], F32)
        passed = sb("passed", [P, CHUNKS, EXPERTS], F32)
        owner = sb("owner", [P, CHUNKS], F32)
        before = sb("before", [P, CHUNKS], F32)
        offset = sb("offset", [P, CHUNKS], F32)
        base = sb("base", [P, CHUNKS], F32)
        owner5 = sb("owner5", [P, CHUNKS], F32)
        base_i = sb("base_i", [P, CHUNKS], I32)
        owner_i = sb("owner_i", [P, CHUNKS], I32)
        ends_i = sb("ends_i", [P, EXPERTS], I32)

        ps_x = [psum(f"ps_x{k}", [P, CHUNK]) for k in range(KF)]
        ps_a = [[psum(f"ps_a{h}{m}", [P, CHUNK]) for m in range(M)] for h in range(PAIR)]
        ps_y = [psum(f"ps_y{i}", [P, 2, FEAT]) for i in range(CU // 2)]

        consts = sem("consts3")
        biases_in = sem("biases_in")
        raw_in = [sem(f"raw_in{i}") for i in range(RAWS)]
        whi_ready = sem("whi3_ready")
        wlo_ready = sem("wlo3_ready")
        plan = sem("plan")
        plan_ready = sem("plan_ready")
        pad_zero = sem("pad_zero")
        pad_ready = sem("pad_ready")
        pads_saved = sem("pads_saved")
        rows_in = [sem(f"rows_in{i}") for i in range(2)]
        cur_ready = sem("cur_ready")
        bias_ready = sem("bias_ready")
        b3_ready = sem("b3_ready")
        x_turned = sem("x_turned")
        xhi_ready = sem("xhi3_ready")
        xlo_ready = sem("xlo3_ready")
        z_ready = sem("z_ready")
        relu_ready = sem("relu_ready")
        ahi_ready = sem("ahi_ready")
        alo_ready = sem("alo_ready")
        first_ready = sem("first_ready")
        weight_ready = sem("weight_ready")
        token_ready = sem("token_ready")
        out_ready = sem("out_ready")
        y_scaled = sem("y_scaled")
        y_ready = sem("y_ready")
        added = sem("added")
        add_passed = sem("add_passed")
        load_passed = sem("load_passed")

        ZC = 2 * PAIR * M
        TU = PAIR * CU

        block = ctx.enter_context(nc.Block())

        def turns(eng, body):
            body(0, 0)
            body(1, 1)
            with eng.Fori(1, (TURNS - 1) // 2) as i:
                body(i * 2, 0)
                body(i * 2 + 1, 1)
            for c in range((TURNS - 1) // 2 * 2, TURNS):
                body(c, c % 2)

        def follows(c):
            return not isinstance(c, int) or c + 1 < TURNS

        def half(c, s):
            return (c - s) // 2

        def raw(n):
            r = n % RAWS
            per = CU // KF
            return y[:, r // (PAIR * per), r // per % PAIR, r % per * KF:(r % per + 1) * KF, :]

        @block.sync
        def _(sp):
            def load_weights(n):
                e, l = n // LAYERS, n % LAYERS
                at_least(sp, wlo_ready, n - RAWS + 1)
                sp.dma_start(raw(n), A["w"][l][e].rearrange("(k p) f -> p k f", p=P)).then_inc(raw_in[n % RAWS], 16)
            for n in range(RAWS):
                load_weights(n)
            with nc.allow_non_contiguous_dma(reason="biases, one number for each partition"):
                sp.dma_start(bias_all[:, 0, :, :], A["b1"].rearrange("e (m p) -> p e m", p=P)).then_inc(biases_in, 16)
                sp.dma_start(bias_all[:, 1, :, :], A["b2"].rearrange("e (m p) -> p e m", p=P)).then_inc(biases_in, 16)
            sp.dma_start(b3[:, :, :], A["b3"].rearrange("(one e) f -> one e f", one=1).to_broadcast([P, EXPERTS, FEAT])
                         ).then_inc(biases_in, 16)
            for n in range(RAWS, EXPERTS * LAYERS):
                load_weights(n)
            sp.wait_ge(plan_ready, 1)
            sp.wait_ge(pad_ready, 1)
            for e in range(EXPERTS):
                end = sp.value_load(ends_i[0:1, e:e + 1], min_val=e * STRIDE, max_val=e * STRIDE + TOKENS)
                sp.dma_start(A["lists"][bass.ds(end, CHUNK), :].rearrange("(p u) f -> p u f", p=P), pad
                             ).then_inc(pads_saved, 16)
            sp.dma_start(A["lists"][IDLE:LIST_ROWS, :].rearrange("(p u) f -> p u f", p=P), pad
                         ).then_inc(pads_saved, 16)
            sp.wait_ge(pads_saved, 16 * (EXPERTS + 1))

            def turn(c, s):
                starts_at = [sp.value_load(base_i[0:1, bass.ds(c * PAIR + h, 1)], min_val=0, max_val=IDLE)
                             for h in range(PAIR)]
                waits_apart(sp, load_passed, (token_ready, (c - 1) * PAIR))
                waits_apart(sp, load_passed, (x_turned, (c - 1) * PAIR))
                for h in range(PAIR):
                    sp.dma_start(rows[:, s, h, :, :],
                                 A["lists"][bass.ds(starts_at[h], CHUNK), :].rearrange("(p u) f -> p u f", p=P)
                                 ).then_inc(rows_in[s], 16)
            turns(sp, turn)

        @block.gpsimd
        def _(pool):
            pool.memset(pad, 0.0).then_inc(pad_zero, 1)
            pool.iota(iota_m[:, :], [[CHUNK, TOKENS // CHUNK]], base=0, channel_multiplier=0,
                      allow_small_or_imprecise_dtypes=True).then_inc(consts, 1)
            pool.iota(iota_c[:, :], [[1, CHUNKS]], base=0, channel_multiplier=0,
                      allow_small_or_imprecise_dtypes=True).then_inc(consts, 1)
            pool.iota(starts[:, :], [[STRIDE, EXPERTS]], base=0, channel_multiplier=0,
                      allow_small_or_imprecise_dtypes=True).then_inc(consts, 1)
            pool.wait_ge(pad_zero, 1)
            pool.iota(rows[:, 0, 0, :, C_TOKEN], [[1, CU]], base=TOKENS, channel_multiplier=CU,
                      allow_small_or_imprecise_dtypes=True).then_inc(pad_ready, 1)

            def turn(c, s):
                for h in range(PAIR):
                    waits_apart(pool, add_passed, (token_ready, c * PAIR + h + 1))
                    for u in range(CU):
                        waits_apart(pool, add_passed, (y_ready, c * TU + h * CU + u + 1),
                                    (added, (c * PAIR + h) * CU * 16))
                        pool.indirect_dma_start(
                            A["out"], bass.IndirectOffsetOnAxis(ap=token[:, s, h, u:u + 1].bitcast(U32), axis=0),
                            y[:, s, h, u, :], None, bounds_check=OUT_ROWS - 1, compute_op=ALU.add).then_inc(added, 16)
            turns(pool, turn)
            pool.wait_ge(added, CHUNKS * CU * 16)

        @block.tensor
        def _(pe):
            def turn_rows(c, s, h):
                at_least(pe, xlo_ready, c * PAIR + h)
                if h == 0:
                    pe.wait_ge(rows_in[s], (half(c, s) + 1) * 16 * PAIR)
                for k in range(KF):
                    for u in range(CU):
                        last = pe.transpose(ps_x[k][:, u * P:(u + 1) * P], rows[:, s, h, u, k * P:(k + 1) * P],
                                            t.ident[:, :])
                last.then_inc(x_turned, 1)

            def layer(c, s, l, h):
                if l == 0:
                    a_hi, a_lo = x_hi[h], x_lo[h]
                    pe.wait_ge(xlo_ready, c * PAIR + h + 1)
                    pe.wait_ge(cur_ready, (c * PAIR + h + 1) * 2)
                else:
                    a_hi, a_lo = a1_hi[h], a1_lo[h]
                    pe.wait_ge(alo_ready, c * ZC + (h + 1) * M)
                for m in range(M):
                    at_least(pe, ahi_ready, c * ZC + (l - 1) * PAIR * M + h * M + m + 1)
                    products = [(w[:, s, h, l, k, m * P:(m + 1) * P], a[:, k, :]) for w, a in
                                ((cur_hi, a_hi), (cur_lo, a_hi), (cur_hi, a_lo)) for k in range(KF)]
                    for i, (w, a) in enumerate(products):
                        last = pe.matmul(ps_a[h][m][:, :], w, a, start=(i == 0), stop=(i == len(products) - 1))
                    last.then_inc(z_ready, 1)

            def last_layer(c, s, h, e):
                pe.wait_ge(alo_ready, c * ZC + (PAIR + h + 1) * M)
                for u in range(CU):
                    n = c * TU + h * CU + u
                    if u % 2 == 0:
                        at_least(pe, y_scaled, n - CU + 2)
                    tok = slice(u * P, (u + 1) * P)
                    products = [(a[h][:, k, tok], w[:, bass.ds(e, 1), 2, k, :].squeeze(1)) for a, w in
                                ((a2_hi, all_hi), (a2_hi, all_lo), (a2_lo, all_hi)) for k in range(KF)]
                    for i, (a, w) in enumerate(products):
                        last = pe.matmul(ps_y[u // 2][:, u % 2, :], a, w, start=(i == 0 and u % 2 == 0),
                                         stop=(i == len(products) - 1), skip_group_check=True)
                    last.then_inc(out_ready, 1)

            def turn(c, s):
                experts = [pe.value_load(owner_i[0:1, bass.ds(c * PAIR + h, 1)], min_val=0, max_val=EXPERTS - 1)
                           for h in range(PAIR)]
                for l in range(2):
                    for h in range(PAIR):
                        layer(c, s, l, h)
                for h in range(PAIR):
                    if follows(c):
                        turn_rows(c + 1, 1 - s, h)
                    last_layer(c, s, h, experts[h])

            pe.wait_ge(plan_ready, 1)
            for h in range(PAIR):
                turn_rows(0, 0, h)
            turns(pe, turn)

        @block.scalar
        def _(act):
            for n in range(EXPERTS * LAYERS):
                e, l = n // LAYERS, n % LAYERS
                act.wait_ge(raw_in[n % RAWS], (n // RAWS + 1) * 16)
                act.activation(all_hi[:, e, l, :, :], raw(n), ACT.Copy).then_inc(whi_ready, 1)

            def split_rows(c, h):
                act.wait_ge(x_turned, c * PAIR + h + 1)
                for k in range(KF):
                    last = act.activation(x_hi[h][:, k, :], ps_x[k][:, :], ACT.Copy)
                last.then_inc(xhi_ready, 1)

            def turn(c, s):
                act.wait_ge(bias_ready, (c + 1) * PAIR)
                for l, a_hi in enumerate((a1_hi, a2_hi)):
                    for h in range(PAIR):
                        for m in range(M):
                            i = (l * PAIR + h) * M + m
                            act.wait_ge(z_ready, c * ZC + i + 1)
                            at_least(act, alo_ready, c * ZC + i - 1)
                            act.activation(relu[:, i % 2, :], ps_a[h][m][:, :], ACT.Relu,
                                           bias=bias[:, s, h, l, m:m + 1]).then_inc(relu_ready, 1)
                            act.activation(a_hi[h][:, m, :], ps_a[h][m][:, :], ACT.Relu,
                                           bias=bias[:, s, h, l, m:m + 1]).then_inc(ahi_ready, 1)
                for h in range(PAIR):
                    if follows(c):
                        split_rows(c + 1, h)
                    act.wait_ge(weight_ready, c * PAIR + h + 1)
                    for u in range(CU):
                        n = c * TU + h * CU + u
                        if u % 2 == 0:
                            act.wait_ge(out_ready, n + 2)
                        if h == 0 and u == 0:
                            at_least(act, added, (c - 1) * TU * 16)
                        act.activation(y[:, s, h, u, :], ps_y[u // 2][:, u % 2, :], ACT.Copy,
                                       scale=weight[:, s, h, u:u + 1]).then_inc(y_scaled, 1)
            for h in range(PAIR):
                split_rows(0, h)
            act.wait_ge(wlo_ready, EXPERTS * LAYERS)
            turns(act, turn)

        @block.vector
        def _(dve):
            def next_step(v, ins):
                ins.then_inc(plan, 1)
                dve.wait_ge(plan, v)
            dve.wait_ge(consts, 3)
            next_step(1, dve.tensor_tensor(counts[:, :], t.ends[:, :], starts[:, :], ALU.subtract))
            next_step(2, dve.tensor_tensor(
                more[:, :, :], counts[:, :].unsqueeze(2).to_broadcast([P, EXPERTS, TOKENS // CHUNK]),
                iota_m[:, :].unsqueeze(1).to_broadcast([P, EXPERTS, TOKENS // CHUNK]), ALU.is_gt))
            next_step(3, dve.tensor_reduce(chunks[:, :], more[:, :, :], AX.X, ALU.add))
            next_step(4, dve.tensor_copy(upto[:, 0:1], chunks[:, 0:1]))
            for e in range(1, EXPERTS):
                next_step(4 + e, dve.tensor_tensor(upto[:, e:e + 1], upto[:, e - 1:e], chunks[:, e:e + 1], ALU.add))
            wide = [P, CHUNKS, EXPERTS]
            next_step(10, dve.tensor_tensor(passed[:, :, :], iota_c[:, :].unsqueeze(2).to_broadcast(wide),
                                            upto[:, :].unsqueeze(1).to_broadcast(wide), ALU.is_ge))
            next_step(11, dve.tensor_reduce(owner[:, :], passed[:, :, :], AX.X, ALU.add))
            next_step(12, dve.tensor_tensor(passed[:, :, :], passed[:, :, :],
                                            chunks[:, :].unsqueeze(1).to_broadcast(wide), ALU.mult))
            next_step(13, dve.tensor_reduce(before[:, :], passed[:, :, :], AX.X, ALU.add))
            next_step(14, dve.tensor_tensor(offset[:, :], iota_c[:, :], before[:, :], ALU.subtract))
            next_step(15, dve.tensor_scalar(offset[:, :], offset[:, :], float(CHUNK), None, ALU.mult))
            next_step(16, dve.scalar_tensor_tensor(base[:, :], owner[:, :], float(STRIDE), offset[:, :], ALU.mult, ALU.add))
            next_step(17, dve.tensor_scalar(base[:, :], base[:, :], float(IDLE), None, ALU.min))
            next_step(18, dve.tensor_scalar(owner5[:, :], owner[:, :], float(EXPERTS - 1), None, ALU.min))
            next_step(19, dve.tensor_copy(base_i[:, :], base[:, :]))
            next_step(20, dve.tensor_copy(ends_i[:, :], t.ends[:, :]))
            dve.tensor_copy(owner_i[:, :], owner5[:, :]).then_inc(plan_ready, 1)

            for n in range(EXPERTS * LAYERS):
                e, l = n // LAYERS, n % LAYERS
                dve.wait_ge(whi_ready, n + 1)
                dve.tensor_tensor(all_lo[:, e, l, :, :], raw(n), all_hi[:, e, l, :, :].bitcast(F32), ALU.subtract
                                  ).then_inc(wlo_ready, 1)
            dve.wait_ge(wlo_ready, EXPERTS * LAYERS)
            dve.wait_ge(biases_in, 48)
            dve.wait_ge(plan_ready, 1)

            def expert_of(c, h):
                return dve.value_load(owner_i[0:1, bass.ds(c * PAIR + h, 1)], min_val=0, max_val=EXPERTS - 1)

            def take_matrices(c, s, h, e, part):
                cur, whole = ((cur_hi, all_hi), (cur_lo, all_lo))[part]
                if h == 0 and part == 0:
                    at_least(dve, z_ready, (c - 1) * ZC)
                dve.tensor_copy(cur[:, s, h, :, :, :], whole[:, bass.ds(e, 1), 0:2, :, :].squeeze(1).bitcast(F32)
                                ).then_inc(cur_ready, 1)

            def take_biases(c, s, experts):
                at_least(dve, ahi_ready, (c - 1) * ZC)
                for h, e in enumerate(experts):
                    dve.tensor_copy(bias[:, s, h, :, :], bias_all[:, :, bass.ds(e, 1), :].squeeze(2)).then_inc(bias_ready, 1)
                    dve.tensor_copy(b3_cur[:, s, h, :], b3[:, bass.ds(e, 1), :].squeeze(1)).then_inc(b3_ready, 1)

            def take_weights(c, s):
                dve.wait_ge(rows_in[s], (half(c, s) + 1) * 16 * PAIR)
                for h in range(PAIR):
                    q = c * PAIR + h
                    dve.tensor_scalar(first[:, s, h, :], rows[:, s, h, :, C_FIRST], owner5[:, bass.ds(q, 1)], None,
                                      ALU.is_equal).then_inc(first_ready, 1)
                dve.wait_ge(first_ready, (2 * c + 1) * PAIR)
                dve.tensor_tensor(first[:, s, :, :], first[:, s, :, :], rows[:, s, :, :, C_DW], ALU.mult
                                  ).then_inc(first_ready, PAIR)
                dve.wait_ge(first_ready, (2 * c + 2) * PAIR)
                at_least(dve, y_scaled, (c - 1) * TU)
                dve.tensor_tensor(weight[:, s, :, :], first[:, s, :, :], rows[:, s, :, :, C_W2], ALU.add
                                  ).then_inc(weight_ready, PAIR)
                at_least(dve, added, (c - 1) * TU * 16)
                dve.tensor_copy(token[:, s, :, :], rows[:, s, :, :, C_TOKEN]).then_inc(token_ready, PAIR)

            def split_rows(c, h):
                dve.wait_ge(xhi_ready, c * PAIR + h + 1)
                for k in range(KF):
                    last = dve.tensor_tensor(x_lo[h][:, k, :], ps_x[k][:, :], x_hi[h][:, k, :].bitcast(F32), ALU.subtract)
                last.then_inc(xlo_ready, 1)

            def turn(c, s):
                experts = []
                for l, (a_hi, a_lo) in enumerate(((a1_hi, a1_lo), (a2_hi, a2_lo))):
                    for h in range(PAIR):
                        for m in range(M):
                            i = (l * PAIR + h) * M + m
                            dve.wait_ge(ahi_ready, c * ZC + i + 1)
                            dve.tensor_tensor(a_lo[h][:, m, :], relu[:, i % 2, :], a_hi[h][:, m, :].bitcast(F32),
                                              ALU.subtract).then_inc(alo_ready, 1)
                            if follows(c) and l == 0 and m == 1:
                                experts.append(expert_of(c + 1, h))
                            if follows(c) and l == 1:
                                take_matrices(c + 1, 1 - s, h, experts[h], m)
                for h in range(PAIR):
                    if follows(c):
                        split_rows(c + 1, h)
                    if h == 0:
                        dve.wait_ge(b3_ready, (c + 1) * PAIR)
                    for u in range(CU):
                        dve.wait_ge(y_scaled, c * TU + h * CU + u + 1)
                        dve.scalar_tensor_tensor(y[:, s, h, u, :], b3_cur[:, s, h, :], weight[:, s, h, u:u + 1],
                                                 y[:, s, h, u, :], ALU.mult, ALU.add).then_inc(y_ready, 1)
                if follows(c):
                    take_biases(c + 1, 1 - s, experts)
                    take_weights(c + 1, 1 - s)
            experts = [expert_of(0, h) for h in range(PAIR)]
            for h in range(PAIR):
                for part in range(2):
                    take_matrices(0, 0, h, experts[h], part)
            take_biases(0, 0, experts)
            for h in range(PAIR):
                split_rows(0, h)
            take_weights(0, 0)
            turns(dve, turn)


class Kept:
    pass


def build(nc, A):
    with ExitStack() as ctx:
        def sb(name, shape, dt):
            return ctx.enter_context(nc.sbuf_tensor(name, shape, dt))
        k = Kept()
        k.ident = sb("ident", [P, P], F32)
        k.ends = sb("ends", [P, EXPERTS], F32)
        with ExitStack() as attention:
            def sa(name, shape, dt):
                return attention.enter_context(nc.sbuf_tensor(name, shape, dt))
            k.adj = sa("adj01", [P, BT, NODES], U8)
            k.col_pos = sa("col_pos", [P, TILES], F32)
            k.col_neg = sa("col_neg", [P, TILES], F32)
            k.row_pos = sa("row_pos", [P, TILES], F32)
            k.row_neg = sa("row_neg", [P, TILES], F32)
            k.neg_s2 = sa("neg_s2", [P, TILES], F32)
            k.alone = sa("alone", [P, BT], F32)
            k.col_parts = sa("col_parts", [P, TILES, 2, 2], F32R)
            project_stage(nc, k, A)
            attend_stage(nc, k, A)
        expert_stage(nc, k, A)


_INS = [("x", (TOKENS, FEAT), F32), ("adjT", (NODES, NODES), I32), ("L0_gnn_W", (FEAT, FEAT), F32),
        ("L0_gnn_a", (2 * FEAT, 1), F32), ("L0_ffn_router_w1", (FEAT, RH), F32), ("L0_ffn_router_b1", (RH,), F32),
        ("L0_ffn_router_w2", (RH, EXPERTS), F32), ("L0_ffn_router_b2", (EXPERTS,), F32)]
_INS += [(f"L0_ffn_expert_w{i}", (EXPERTS, FEAT, FEAT), F32) for i in (1, 2, 3)]
_INS += [(f"L0_ffn_expert_b{i}", (EXPERTS, FEAT), F32) for i in (1, 2, 3)]


def kernel(**inputs):
    import concourse.bacc as bacc
    from concourse.bass_utils import run_bass_kernel_spmd as run

    nc = bacc.Bacc("TRN2", target_bir_lowering=False, num_devices=1)
    arrays, args = {}, {}
    for name, shape, dt in _INS:
        v = np.asarray(inputs["adj"]).T if name == "adjT" else inputs[name]
        arrays[name] = np.ascontiguousarray(v).reshape(shape)
        args[name] = nc.dram_tensor(name, shape, dt, kind="ExternalInput").ap()
    out = nc.dram_tensor("out", (OUT_ROWS, FEAT), F32, kind="ExternalOutput").ap()
    tokens = "(n u p) f -> n p u f"
    A = {
        "x": args["x"].rearrange(tokens, u=GT, p=P),
        "x_blocks": args["x"].rearrange("(k g p) f -> k p g f", g=XG * GT, p=P),
        "adjT": args["adjT"].rearrange("(k p) i -> k p i", p=P),
        "W": args["L0_gnn_W"], "a": args["L0_gnn_a"], "out": out,
        "x1": out[0:TOKENS, :].rearrange(tokens, u=GT, p=P),
        "out_pad": out[TOKENS:TOKENS+GW, :].rearrange("(u p) f -> p u f", u=GT),
        "out_pad2": out[TOKENS+GW:TOKENS+2*GW, :].rearrange("(u p) f -> p u f", u=GT),
        "router_w1": args["L0_ffn_router_w1"], "router_b1": args["L0_ffn_router_b1"],
        "router_w2": args["L0_ffn_router_w2"], "router_b2": args["L0_ffn_router_b2"],
        "w": [args[f"L0_ffn_expert_w{i}"] for i in (1, 2, 3)], "b1": args["L0_ffn_expert_b1"],
        "b2": args["L0_ffn_expert_b2"], "b3": args["L0_ffn_expert_b3"],
        "lists": nc.dram_tensor("lists", (LIST_ROWS, ROW), F32, kind="Internal").ap(),
        "h": nc.dram_tensor("h", (GROUPS, P, GT, FEAT), F32, kind="Internal").ap(),
    }
    s1 = nc.dram_tensor("s1_rows", (TOKENS,), F32, kind="Internal").ap()
    A["s1_save"] = s1.rearrange("(t p) -> t p", p=P)
    A["s1_rows"] = s1.rearrange("(n one i) -> n one i", one=1, i=GW)
    A["hmean_rows"] = nc.dram_tensor("hmean_rows", (BATCH, 1, FEAT), F32, kind="Internal").ap()
    build(nc, A)
    r = run(nc, [arrays], core_ids=[0])
    return r.results[0]["out"][:TOKENS].reshape(BATCH, NODES, FEAT)
```

```python
from contextlib import ExitStack

import numpy as np

import concourse.bass as bass
from concourse import mybir

ALU = mybir.AluOpType
ACT = mybir.ActivationFunctionType
AX = mybir.AxisListType
RMAX = bass.bass_isa.ReduceOp.max
F32 = mybir.dt.float32
F32R = mybir.dt.float32r
BF16 = mybir.dt.bfloat16
U8 = mybir.dt.uint8
I32 = mybir.dt.int32
U32 = mybir.dt.uint32

P = 128
BATCH, NODES, FEAT = 8, 2048, 256
TOKENS = BATCH * NODES
KF = FEAT // P
TILES = TOKENS // P
BT = NODES // P
GT = 2
GROUPS = TILES // GT
BG = BT // GT
GW = GT * P
EXPERTS, LAYERS, RH = 6, 3, 128
TOPK = 2
ROW = FEAT + 4
C_W2, C_DW, C_TOKEN, C_FIRST = range(FEAT, ROW)
CHUNK = 512
CU = CHUNK // P
PAIR = 2
TURNS = -(-(TOPK * TOKENS // CHUNK + EXPERTS - 1) // PAIR)
CHUNKS = TURNS * PAIR
STRIDE = TOKENS + CHUNK
IDLE = EXPERTS * STRIDE
LIST_ROWS = IDLE + CHUNK
OUT_ROWS = TOKENS + CHUNK
CH = 4
NC = BT // CH
XG = 2
XB = BG // XG
SLOTS = 2 * BT - CH
AHEAD = BG - 1
CENTER = 60.0
SLOPE = 0.2
EPS = 1e-5
SW = 2 * FEAT + 2
WEIGHTS = EXPERTS * LAYERS * KF * FEAT
ARENA = SLOTS * 2 * SW
ROWS_SIZE = 2 * PAIR * CU * ROW
Y_SIZE = 2 * PAIR * CU * FEAT


def at_least(eng, sem, value):
    if not (isinstance(value, int) and value <= 0):
        eng.wait_ge(sem, value)


def waits_apart(eng, passed, *waits):
    for sem, v in waits:
        at_least(eng, sem, v)
    eng.sem_inc(passed, 1)


def part(arena, start, pattern, **sizes):
    size = 1
    for v in sizes.values():
        size *= v
    return arena[:, start:start + size].rearrange(f"p ({pattern}) -> p {pattern}", **sizes)


def expert_weights(arena):
    sizes = dict(e=EXPERTS, l=LAYERS, k=KF, f=FEAT)
    return part(arena, 0, "e l k f", **sizes), part(arena, WEIGHTS, "e l k f", **sizes)


def project_stage(nc, t, A):
    with ExitStack() as ctx:
        def sb(name, shape, dt):
            return ctx.enter_context(nc.sbuf_tensor(name, shape, dt))

        def sem(name):
            return ctx.enter_context(nc.semaphore(name))

        xin = sb("xin", [P, XB, XG * GT, FEAT], F32)
        stats = sb("stats1", [P, 2, GT, 6], F32)
        meanvar = sb("meanvar1", [P, 2, GT, 2], F32)
        std = sb("std1", [P, 2, GT], F32)
        rstd = sb("rstd1", [P, 2, GT], F32)
        eps = sb("eps1", [P, 1], F32)
        xn = sb("xn1", [P, 2, GT, FEAT], F32)
        xT_hi = sb("xT_hi", [P, 2, KF, GW], F32R)
        xT_lo = sb("xT_lo", [P, 2, KF, GW], F32R)
        w = sb("w_f32", [P, KF, FEAT + 2], F32)
        w_hi = sb("w_hi", [P, KF, FEAT + 2], F32R)
        w_lo = sb("w_lo", [P, KF, FEAT + 2], F32R)
        arow = sb("arow", [P, 2, FEAT], F32)
        junk = sb("junk", [P, 2, KF, FEAT], F32)
        hsb = sb("hsb", [P, 2, GT, FEAT], F32)
        score = sb("score", [P, TILES, 2], F32)
        xsum = sb("xsum", [P, GROUPS, KF], F32)
        bsum = sb("bsum", [P, KF, BATCH], F32)
        hmean = sb("hmean", [BATCH, FEAT], F32)
        raw = sb("adj_raw", [P, 2, NODES], I32)
        adj_bf = sb("adj_bf", [P, 2, NODES], BF16)
        ones = sb("ones_bf", [P, 2], BF16)
        mx = sb("mx", [P, BATCH], F32)
        mb = sb("mb", [P, BATCH], F32)
        s1 = sb("s1", [P, TILES], F32)
        s1T = sb("s1T", [P, TILES], F32)
        rel = sb("rel", [P, TILES], F32)
        relc = sb("relc", [P, TILES], F32)
        q = sb("q", [P, TILES], F32)
        qs = sb("qs", [P, TILES], F32)
        qc = sb("qc", [P, TILES], F32)
        top = sb("top", [P, TILES], F32)

        ps_T = ctx.enter_context(nc.psum_tensor("ps_T", [P, 2, KF, GW], F32))
        ps_h = ctx.enter_context(nc.psum_tensor("ps_h", [P, 2, GT, 512], F32))
        ps_deg = ctx.enter_context(nc.psum_tensor("ps_deg", [P, BT, 2], F32))
        ps_misc = ctx.enter_context(nc.psum_tensor("ps_misc", [P, 512], F32))

        weights_in = sem("weights_in")
        x_in = [sem(f"x_in{i}") for i in range(XB)]
        adj_in = [sem(f"adj_in{i}") for i in range(2)]
        consts = sem("consts")
        ident_zero = sem("ident_zero")
        ident_ready = sem("ident_ready")
        wa_ready = sem("wa_ready")
        whi_ready = sem("whi_ready")
        wlo_ready = sem("wlo_ready")
        stats_ready = sem("stats_ready")
        meanvar_ready = sem("meanvar_ready")
        stats_passed = sem("stats_passed")
        adj_passed = sem("adj_passed")
        std_ready = sem("std_ready")
        rstd_ready = sem("rstd_ready")
        xn_ready = sem("xn_ready")
        transposed = sem("transposed")
        xhi_ready = sem("xhi_ready")
        xlo_ready = sem("xlo_ready")
        h_ready = sem("h_ready")
        h_copied = sem("h_copied")
        h_saved = [sem(f"h_saved{i}") for i in range(2)]
        scores_copied = sem("scores_copied")
        adj_bytes = sem("adj_bytes")
        adj_float = sem("adj_float")
        deg_counted = sem("deg_counted")
        bsum_ready = sem("bsum_ready")
        hsum_ready = sem("hsum_ready")
        hmean_ready = sem("hmean_ready")
        rows_saved = sem("rows_saved")
        max_part = sem("max_part")
        max_ready = sem("max_ready")
        tail = sem("tail")
        exps_ready = sem("exps_ready")
        exp_in = sem("exp_in")
        s1_ready = sem("s1_ready")
        s1T_ready = sem("s1T_ready")
        s1T_copied = sem("s1T_copied")

        block = ctx.enter_context(nc.Block())

        def batches(eng, body):
            body(0)
            with eng.Fori(1, BATCH) as b:
                body(b)

        @block.sync
        def _(sp):
            sp.dma_start(w[:, :, 0:FEAT], A["W"].rearrange("(k p) f -> p k f", p=P)).then_inc(weights_in, 16)
            sp.dma_start(arow[:, :, :], A["a"].rearrange("(s f) one -> one s f", s=2).to_broadcast([P, 2, FEAT])
                         ).then_inc(weights_in, 16)

            def store(n, s):
                sp.wait_ge(h_copied, n + 1)
                sp.dma_start(A["h"][n], hsb[:, s, :, :]).then_inc(h_saved[s], 16)

            def load_x(b, j):
                at_least(sp, xn_ready, ((b - 1) * XB + j + 1) * XG * GT)
                sp.dma_start(xin[:, j, :, :], A["x_blocks"][b * XB + j]).then_inc(x_in[j], 16)

            def load_adj(b, j):
                at_least(sp, adj_float, (b - 1) * 2 + j + 1)
                sp.dma_start(raw[:, j, :], A["adjT"][b * 2 + j]).then_inc(adj_in[j], 16)

            def batch(b, more=True):
                for u in range(BG):
                    n = b * BG + u
                    if u > 2 or not isinstance(b, int) or b:
                        store(n - 3, (u + 1) % 2)
                    if u == 1 and not (isinstance(b, int) and b == 0):
                        load_x(b, XB - 1)
                    if u % 2 and u > 1 and more:
                        load_x(b + 1, (u - 3) // 2)
                    if u % 4 == 3 and more:
                        load_adj(b + 1, u // 4)
            for j in range(XB):
                load_x(0, j)
                if j % 2 == 0:
                    load_adj(0, j // 2)
            batch(0)
            with sp.Fori(1, BATCH - 1) as b:
                batch(b)
            batch(BATCH - 1, more=False)
            for n in range(GROUPS - 3, GROUPS):
                store(n, n % 2)
            sp.wait_ge(s1T_copied, 1)
            sp.dma_start(A["s1_save"], s1T[:, :]).then_inc(rows_saved, 16)
            sp.wait_ge(hmean_ready, 1)
            sp.dma_start(A["hmean_rows"][:, 0, :], hmean[:, :]).then_inc(rows_saved, 16)
            sp.wait_ge(rows_saved, 32)
            for s in range(2):
                sp.wait_ge(h_saved[s], GROUPS // 2 * 16)

        @block.gpsimd
        def _(pool):
            pool.memset(t.ident[:, :], 0.0).then_inc(ident_zero, 1)
            pool.memset(ones[:, :], 1.0).then_inc(consts, 1)
            pool.memset(eps[:, :], EPS).then_inc(consts, 1)
            pool.wait_ge(ident_zero, 1)
            pool.affine_select(out=t.ident[:, :], in_=t.ident[:, :], compare_op=ALU.not_equal, fill=1.0,
                               base=0, pattern=[[-1, P]], channel_multiplier=1).then_inc(ident_ready, 1)

            def batch(b):
                for s in range(2):
                    k = b * 2 + s
                    waits_apart(pool, adj_passed, (adj_in[s], (b + 1) * 16), (deg_counted, k - 1), (adj_bytes, k - 1))
                    pool.tensor_scalar(adj_bf[:, s, :], raw[:, s, :], 0.0, None, ALU.is_gt).then_inc(adj_float, 1)
            batches(pool, batch)
            pool.wait_ge(max_part, 1)
            pool.partition_all_reduce(mb[:, :], mx[:, :], P, RMAX).then_inc(max_ready, 1)

        @block.tensor
        def _(pe):
            def transposes(n, s):
                at_least(pe, xlo_ready, n - 1)
                pe.wait_ge(xn_ready, (n + 1) * GT)
                for k in range(KF):
                    for u in range(GT):
                        last = pe.transpose(ps_T[:, s, k, u * P:(u + 1) * P], xn[:, s, u, k * P:(k + 1) * P],
                                            t.ident[:, :])
                last.then_inc(transposed, 1)

            def project(n, s):
                at_least(pe, scores_copied, n - 1)
                pe.wait_ge(xlo_ready, n + 1)
                for u in range(GT):
                    for i, (l, r) in enumerate([(xT_hi, w_hi), (xT_hi, w_lo), (xT_lo, w_hi)]):
                        for k in range(KF):
                            last = pe.matmul(ps_h[:, s, u, 0:FEAT + 2], l[:, s, k, u * P:(u + 1) * P], r[:, k, :],
                                             start=(i == 0 and k == 0), stop=(i == 2 and k == KF - 1))
                last.then_inc(h_ready, 1)

            def count(b, s):
                k = b * 2 + s
                pe.wait_ge(adj_float, k + 1)
                for i in range(BT):
                    last = pe.matmul(ps_deg[:, i, :], adj_bf[:, s, i * P:(i + 1) * P], ones[:, :],
                                     start=(isinstance(b, int) and s == 0 and i == 0), stop=True,
                                     skip_group_check=True)
                last.then_inc(deg_counted, 1)

            def batch(b):
                for u in range(BG):
                    n = b * BG + u
                    transposes(n, u % 2)
                    if u or not isinstance(b, int):
                        project(n - 1, (u + 1) % 2)
                    if u % 4 == 3:
                        count(b, u // 4)
            pe.wait_ge(ident_ready, 1)
            pe.wait_ge(consts, 2)
            pe.wait_ge(wlo_ready, 1)
            batches(pe, batch)
            project(GROUPS - 1, 1)
            pe.wait_ge(bsum_ready, 1)
            for k in range(KF):
                last = pe.matmul(ps_misc[0:BATCH, 0:FEAT], bsum[:, k, :], w[:, k, 0:FEAT],
                                 start=(k == 0), stop=(k == KF - 1))
            last.then_inc(hsum_ready, 1)
            pe.wait_ge(s1_ready, 1)
            pe.wait_ge(hmean_ready, 1)
            pe.transpose(ps_misc[:, 0:TILES], s1[:, :], t.ident[:, :]).then_inc(s1T_ready, 1)

        @block.scalar
        def _(act):
            act.wait_ge(consts, 2)

            def rows(n, s):
                act.wait_ge(meanvar_ready, (n + 1) * GT)
                act.activation(std[:, s, :], meanvar[:, s, :, 1], ACT.Sqrt, bias=eps[:, 0:1]).then_inc(std_ready, 1)

            def split(n, s):
                act.wait_ge(transposed, n + 1)
                at_least(act, h_ready, n - 1)
                for k in range(KF):
                    last = act.activation(xT_hi[:, s, k, :], ps_T[:, s, k, :], ACT.Copy,
                                          accum_out=xsum[:, n, k:k + 1])
                last.then_inc(xhi_ready, 1)

            def save(n, s, n2):
                act.wait_ge(h_ready, n + 1)
                at_least(act, h_saved[s], n2 * 16)
                act.activation(hsb[:, s, :, :], ps_h[:, s, :, 0:FEAT], ACT.Copy).then_inc(h_copied, 1)
                act.activation(score[:, bass.ds(n * GT, GT), :], ps_h[:, s, :, FEAT:FEAT + 2], ACT.Copy
                               ).then_inc(scores_copied, 1)

            def batch(b):
                for u in range(BG):
                    n = b * BG + u
                    rows(n, u % 2)
                    if u or not isinstance(b, int):
                        split(n - 1, (u + 1) % 2)
                    if u > 2 or not isinstance(b, int):
                        save(n - 3, (u + 1) % 2, b * (BG // 2) + (u - 3) // 2)
                    if u % 4 == 3:
                        k = b * 2 + u // 4
                        act.wait_ge(adj_float, k + 1)
                        act.activation(t.adj[:, k, :], adj_bf[:, u // 4, :], ACT.Copy).then_inc(adj_bytes, 1)
            batches(act, batch)
            split(GROUPS - 1, 1)
            save(GROUPS - 3, 1, GROUPS // 2 - 2)
            save(GROUPS - 2, 0, GROUPS // 2 - 1)
            save(GROUPS - 1, 1, GROUPS // 2 - 1)
            act.wait_ge(exp_in, 1)
            act.activation(t.col_neg[:, :], rel[:, :], ACT.Exp, scale=SLOPE).then_inc(exps_ready, 1)
            act.activation(t.col_pos[:, :], relc[:, :], ACT.Exp).then_inc(exps_ready, 1)
            act.wait_ge(exp_in, 2)
            act.activation(t.row_pos[:, :], qc[:, :], ACT.Exp).then_inc(exps_ready, 1)
            act.activation(t.row_neg[:, :], qs[:, :], ACT.Exp).then_inc(exps_ready, 1)
        @block.vector
        def _(dve):
            dve.wait_ge(weights_in, 32)
            for s in range(2):
                for k in range(KF):
                    last = dve.tensor_tensor_reduce(junk[:, s, k, :], w[:, k, 0:FEAT], arow[:, s, :], 1.0, 0.0, ALU.mult,
                                                    ALU.add, w[:, k, FEAT + s:FEAT + s + 1])
                    last.then_inc(wa_ready, 1)
            dve.wait_ge(wa_ready, 4)
            dve.tensor_copy(w_hi[:, :, :], w[:, :, :]).then_inc(whi_ready, 1)
            dve.wait_ge(whi_ready, 1)
            dve.tensor_tensor(w_lo[:, :, :], w[:, :, :], w_hi[:, :, :].bitcast(F32), ALU.subtract).then_inc(wlo_ready, 1)

            def x_tile(j, u):
                return xin[:, j // XG, j % XG * GT + u, :]

            def moments_and_rows(n, j, b):
                s, o, before = j % 2, 1 - j % 2, j > 0 or not isinstance(b, int)
                if j % XG == 0:
                    dve.wait_ge(x_in[j // XG], (b + 1) * 16)
                for u in range(GT):
                    dve.bn_stats(stats[:, s, u, :], x_tile(j, u)).then_inc(stats_ready, 1)
                if before:
                    reciprocal(n - 1, o)
                waits_apart(dve, stats_passed, (stats_ready, (n + 1) * GT))
                for u in range(GT):
                    dve.bn_aggr(meanvar[:, s, u, :], stats[:, s, u, :]).then_inc(meanvar_ready, 1)
                if before:
                    normalise(n - 1, o, (j - 1) % BG)

            def reciprocal(n, s):
                dve.wait_ge(std_ready, n + 1)
                dve.reciprocal(rstd[:, s, :], std[:, s, :]).then_inc(rstd_ready, 1)

            def normalise(n, s, j):
                dve.wait_ge(rstd_ready, n + 1)
                at_least(dve, transposed, n - 1)
                for u in range(GT):
                    dve.tensor_scalar(xn[:, s, u, :], x_tile(j, u), meanvar[:, s, u, 0:1], rstd[:, s, u:u + 1],
                                      ALU.subtract, ALU.mult).then_inc(xn_ready, 1)

            def split(n, s):
                dve.wait_ge(xhi_ready, n + 1)
                at_least(dve, h_ready, n - 1)
                dve.tensor_tensor(xT_lo[:, s, :, :], ps_T[:, s, :, :], xT_hi[:, s, :, :].bitcast(F32), ALU.subtract
                                  ).then_inc(xlo_ready, 1)

            def batch(b):
                for u in range(BG):
                    n = b * BG + u
                    moments_and_rows(n, u, b)
                    if u > 1 or not isinstance(b, int):
                        split(n - 2, u % 2)
            batches(dve, batch)
            reciprocal(GROUPS - 1, 1)
            normalise(GROUPS - 1, 1, BG - 1)
            split(GROUPS - 2, 0)
            split(GROUPS - 1, 1)
            dve.wait_ge(xhi_ready, GROUPS)
            dve.tensor_reduce(bsum[:, :, :], xsum[:, :, :].rearrange("p (b g) k -> p k b g", b=BATCH), AX.X, ALU.add
                              ).then_inc(bsum_ready, 1)
            dve.wait_ge(scores_copied, GROUPS)
            s2 = score[:, :, 1]
            dve.tensor_reduce(mx[:, :], s2.rearrange("p (b t) -> p b t", b=BATCH), AX.X, ALU.max).then_inc(max_part, 1)
            dve.tensor_copy(s1[:, :], score[:, :, 0]).then_inc(s1_ready, 1)
            dve.tensor_scalar(t.neg_s2[:, :], s2, -1.0, None, ALU.mult).then_inc(tail, 1)
            dve.wait_ge(deg_counted, BT)
            dve.tensor_scalar(t.alone[:, :], ps_deg[:, :, 0], 0.0, None, ALU.is_equal).then_inc(tail, 1)
            dve.wait_ge(hsum_ready, 1)
            dve.tensor_scalar(hmean[:, :], ps_misc[0:BATCH, 0:FEAT], 1.0 / NODES, None, ALU.mult).then_inc(hmean_ready, 1)
            dve.wait_ge(s1T_ready, 1)
            dve.tensor_copy(s1T[:, :], ps_misc[:, 0:TILES]).then_inc(s1T_copied, 1)

            def of_batch(tile):
                return tile[:, :].rearrange("p (b t) -> p b t", b=BATCH)
            peak = mb[:, :].unsqueeze(2).to_broadcast([P, BATCH, BT])
            dve.wait_ge(max_ready, 1)
            dve.tensor_tensor(of_batch(rel), s2.rearrange("p (b t) -> p b t", b=BATCH), peak, ALU.subtract).then_inc(tail, 1)
            dve.tensor_tensor(of_batch(q), score[:, :, 0].rearrange("p (b t) -> p b t", b=BATCH), peak, ALU.add).then_inc(tail, 1)
            dve.wait_ge(tail, 4)
            dve.tensor_scalar(relc[:, :], rel[:, :], CENTER, None, ALU.add).then_inc(exp_in, 1)
            dve.tensor_scalar(qs[:, :], q[:, :], SLOPE, None, ALU.mult).then_inc(tail, 1)
            dve.tensor_scalar(qc[:, :], q[:, :], -CENTER, None, ALU.add).then_inc(tail, 1)
            dve.wait_ge(tail, 6)
            dve.tensor_tensor(top[:, :], qs[:, :], qc[:, :], ALU.max).then_inc(tail, 1)
            dve.wait_ge(tail, 7)
            dve.tensor_tensor(qs[:, :], qs[:, :], top[:, :], ALU.subtract).then_inc(tail, 1)
            dve.wait_ge(tail, 8)
            dve.tensor_tensor(qc[:, :], qc[:, :], top[:, :], ALU.subtract).then_inc(exp_in, 1)
            dve.wait_ge(exps_ready, 2)
            for i, col in enumerate((t.col_pos, t.col_neg)):
                dve.tensor_copy(t.col_parts[:, :, i, 0], col[:, :]).then_inc(tail, 1)
            dve.wait_ge(tail, 10)
            for i, col in enumerate((t.col_pos, t.col_neg)):
                dve.tensor_tensor(t.col_parts[:, :, i, 1], col[:, :], t.col_parts[:, :, i, 0].bitcast(F32),
                                  ALU.subtract).then_inc(tail, 1)


def attend_stage(nc, t, A):
    with ExitStack() as ctx:
        def sb(name, shape, dt):
            return ctx.enter_context(nc.sbuf_tensor(name, shape, dt))

        def sem(name):
            return ctx.enter_context(nc.semaphore(name))

        def psum(name, shape):
            return ctx.enter_context(nc.psum_tensor(name, shape, F32))

        scaled = part(t.arena, 0, "s i w", s=SLOTS, i=2, w=SW)
        mask_pos = sb("mask_pos", [P, BT, GW], F32R)
        mask_neg = sb("mask_neg", [P, BT, GW], F32R)
        s1row = sb("s1row", [P, 2, GW], F32)
        hmean = sb("hmean_all", [P, 2, FEAT], F32)
        hin = sb("hin", [P, GT, FEAT], F32)
        xres = sb("xres", [P, 2, GT, FEAT], F32)
        att = sb("att", [P, GT, FEAT + 2], F32)
        expo = sb("expo", [P, GT, FEAT], F32)
        xrow = sb("xrow", [P, 2, GT, ROW], F32)
        xT = sb("xT_router", [P, KF, GW], F32)
        rh = sb("rh", [P, GW], F32)
        wr1 = sb("wr1", [P, KF, RH], F32)
        wr2 = sb("wr2", [P, EXPERTS], F32)
        br1 = sb("br1", [P, 1], F32)
        br2 = sb("br2", [P, EXPERTS], F32)
        eps = sb("eps2", [P, 1], F32)
        tri = sb("tri", [P, P], BF16)
        ones = sb("ones2", [P, P], BF16)
        iota_e = sb("iota_e", [P, EXPERTS], F32)
        den = sb("den", [P, GT], F32)
        den1 = sb("den1", [P, GT], F32)
        rden = sb("rden", [P, GT], F32)
        stats = sb("stats2", [P, GT, 6], F32)
        meanvar = sb("meanvar2", [P, GT, 2], F32)
        std = sb("std2", [P, GT], F32)
        rstd = sb("rstd2", [P, GT], F32)
        logits = sb("logits", [P, GT, 8], F32)
        best = sb("best", [P, GT, 8], F32)
        bidx = sb("bidx", [P, GT, 8], U32)
        exin = sb("exin", [P, GT, EXPERTS + 1], F32)
        exout = sb("exout", [P, GT, EXPERTS + 1], F32)
        idxf = sb("idxf", [P, GT, TOPK], F32)
        chosen = sb("chosen", [P, GT, TOPK, EXPERTS], F32)
        sel = sb("sel", [P, GT, EXPERTS], BF16)
        prob = sb("prob", [P, 4, GT], F32)
        edif = sb("edif", [P, GT], F32)
        rank = sb("rank", [P, 2, GT, 2, EXPERTS], F32)
        place = sb("place", [P, GT, TOPK, EXPERTS], F32)
        posf = sb("posf", [P, GT, TOPK], F32)
        pos = sb("pos", [P, 2, GT, TOPK], I32)

        u_pos = [psum(f"u_pos{i}", [P, 512]) for i in range(GT)]
        u_neg = [psum(f"u_neg{i}", [P, 512]) for i in range(GT)]
        ps_xT = psum("ps_xT", [P, KF, GW])
        ps_rh = psum("ps_rh", [P, 512])
        ps_lg = psum("ps_lg", [P, 512])
        ps_rk = psum("ps_rk", [P, 512])
        lg = ps_lg[:, 0:GT * 8].rearrange("p (u e) -> p u e", u=GT)
        rk = ps_rk[:, 0:2 * GT * EXPERTS].rearrange("p (s u e) -> p s u e", s=2, u=GT)

        RAWS = 10
        all_hi, all_lo = expert_weights(t.arena)

        def raw(n):
            return part(spare, n % RAWS * KF * FEAT, "k f", k=KF, f=FEAT)

        spare = t.bytes[:, :].bitcast(F32)
        LISTS = TOKENS // CHUNK
        taken = [RAWS * KF * FEAT]

        def piece(pattern, **sizes):
            start = taken[0]
            view = part(spare, start, pattern, **sizes)
            size = 1
            for v in sizes.values():
                size *= v
            taken[0] += size
            return view
        pad = piece("u f", u=CU, f=ROW)
        more = piece("e m", e=EXPERTS, m=LISTS)
        passed = piece("c e", c=CHUNKS, e=EXPERTS)
        ends, starts, counts, chunks, upto, ends_f = (piece("e", e=EXPERTS) for _ in range(6))
        owners, before, offset, base, iota_c = (piece("c", c=CHUNKS) for _ in range(5))
        iota_m = piece("m", m=LISTS)
        ends_i = ends_f.bitcast(I32)

        small_in = sem("small_in")
        const_zero = sem("const_zero")
        const_ready = sem("const_ready")
        s1_in = [sem(f"s1_in{i}") for i in range(2)]
        hm_in = [sem(f"hm_in{i}") for i in range(2)]
        xr_in = [sem(f"xr_in{i}") for i in range(2)]
        first_h_in = sem("first_h_in")
        h_in = sem("h_in")
        hi_ready = sem("hi_ready")
        parts_ready = sem("parts_ready")
        lo_ready = sem("lo_ready")
        pos_masks_ready = sem("pos_masks_ready")
        pos_passed = sem("pos_passed")
        adj_ready = sem("adj_ready")
        neg_masks_ready = sem("neg_masks_ready")
        masks_used = sem("masks_used")
        u_ready = sem("u_ready")
        v_ready = sem("v_ready")
        att_ready = sem("att_ready")
        den_ready = sem("den_ready")
        den1_ready = sem("den1_ready")
        rden_ready = sem("rden_ready")
        mean_added = sem("mean_added")
        expo_ready = sem("expo_ready")
        elu_pos = sem("elu_pos")
        elu_ready = sem("elu_ready")
        x1_ready = sem("x1_ready")
        x1_saved = [sem(f"x1_saved{i}") for i in range(2)]
        stats_ready = sem("stats2_ready")
        stats_passed = sem("stats2_passed")
        meanvar_ready = sem("meanvar2_ready")
        std_ready = sem("std2_ready")
        rstd_ready = sem("rstd2_ready")
        xn_ready = sem("xn2_ready")
        xT_ready = sem("xT_ready")
        xT_copied = sem("xT_copied")
        rh_ready = sem("rh_ready")
        rh_copied = sem("rh_copied")
        logits_ready = sem("logits_ready")
        route = sem("route")
        route_passed = sem("route_passed")
        exin_ready = sem("exin_ready")
        exout_ready = sem("exout_ready")
        edif_in = sem("edif_in")
        edif_ready = sem("edif_ready")
        sel_ready = sem("sel_ready")
        rank_ready = sem("rank_ready")
        pos_ready = sem("pos_ready")
        scattered = [sem(f"scattered{i}") for i in range(2)]
        zero_ready = sem("zero_ready")
        zero_saved = sem("zero_saved")
        raw_in = [sem(f"raw_in{i}") for i in range(RAWS)]
        whi_ready = sem("whi3_ready")
        wlo_ready = sem("wlo3_ready")
        plan_consts = sem("plan_consts")
        plan = sem("plan")
        plan_ready = sem("plan_ready")
        pad_zero = sem("pad_zero")
        pad_ready = sem("pad_ready")
        pads_saved = sem("pads_saved")

        (R_LOGITS, R_BEST0, R_BEST1, R_IDX0, R_IDX1, R_DIF, R_IDXF, R_CHOSEN, R_SUM, R_RSUM, R_ONE, R_W1, R_W2,
         R_RANK0, R_DW, R_RANK1, R_TOK, R_FIRST, R_PLACE, R_POSF) = range(1, 21)
        STEPS = 20
        FILL = (0, 6, 6, 6, EXPERTS * LAYERS)

        block = ctx.enter_context(nc.Block())

        def first_h(m):
            if m == AHEAD - 1:
                return later_h
            return lambda u: mask_pos[:, CH + m * GT + u, :].bitcast(F32)

        def later_h(u):
            return hin[:, u, :]

        def pipeline(eng, body, fill=None):
            for n in range(4):
                body(n, n % 2, True)
            with eng.Fori(2, (GROUPS - BG) // 2) as i:
                for s in range(2):
                    body(i * 2 + s, s, True)
            body(GROUPS - BG, 0, True)
            body(GROUPS - BG + 1, 1, False)
            with eng.Fori((GROUPS - BG) // 2 + 1, GROUPS // 2) as i:
                for s in range(2):
                    body(i * 2 + s, s, False)
            for n in range(GROUPS, GROUPS + 3):
                body(n, n % 2, False)
                if fill:
                    fill(n - GROUPS)

        def runs(n, lag=0):
            return not isinstance(n, int) or lag <= n < GROUPS + lag

        def first(n):
            return isinstance(n, int) and n == 0

        def last(n):
            return isinstance(n, int) and n >= GROUPS

        def half(n, s):
            return (n - s) // 2

        @block.sync
        def _(sp):
            sp.dma_start(s1row[:, 0, :], A["s1_rows"][0].to_broadcast([P, GW])).then_inc(s1_in[0], 16)
            sp.dma_start(wr1[:, :, :], A["router_w1"].rearrange("(k p) f -> p k f", p=P)).then_inc(small_in, 16)
            sp.dma_start(wr2[:, :], A["router_w2"]).then_inc(small_in, 16)
            sp.dma_start(br1[:, :], A["router_b1"].rearrange("(p one) -> p one", one=1)).then_inc(small_in, 16)
            sp.dma_start(br2[:, :], A["router_b2"].rearrange("(one e) -> one e", one=1).to_broadcast([P, EXPERTS])
                         ).then_inc(small_in, 16)

            def load_h(m):
                at_least(sp, lo_ready, m * 2 * GT)
                sp.dma_start(hin[:, :, :], A["h"][m]).then_inc(h_in, 16)
            sp.wait_ge(zero_ready, 1)
            for i in range(CHUNK // GW):
                sp.dma_start(A["out_pad"][i], hin[:, :, :]).then_inc(zero_saved, 16)
            before = AHEAD - 1
            sp.dma_start(mask_pos[:, CH:CH + before * GT, :].rearrange("p (g u) f -> p g u f", u=GT).bitcast(F32),
                         A["h"][0:before].rearrange("g p u f -> p g u f")).then_inc(first_h_in, 16)
            sp.wait_ge(zero_saved, CHUNK // GW * 16)
            sp.dma_start(hin[:, :, :], A["h"][before]).then_inc(first_h_in, 16)

            def body(n, s, ahead):
                if runs(n):
                    if not first(n):
                        at_least(sp, pos_masks_ready, (n - 1) * BT)
                        sp.dma_start(s1row[:, s, :], A["s1_rows"][n].to_broadcast([P, GW])).then_inc(s1_in[s], 16)
                    if not isinstance(n, int) or n >= 2:
                        sp.wait_ge(mean_added, (n - 1) * GT)
                    sp.dma_start(hmean[:, s, :], A["hmean_rows"][n // BG].to_broadcast([P, FEAT])).then_inc(hm_in[s], 16)
                    if ahead:
                        load_h(n + AHEAD)
                if runs(n, 2):
                    m = n - 2
                    sp.wait_ge(x1_ready, m + 1)
                    sp.dma_start(A["x1"][m], xres[:, s, :, :]).then_inc(x1_saved[s], 16)
                if runs(n):
                    if not isinstance(n, int) or n >= 2:
                        sp.wait_ge(x1_saved[s], half(n, s) * 16)
                        sp.wait_ge(xn_ready, (n - 1) * GT)
                    sp.dma_start(xres[:, s, :, :], A["x"][n]).then_inc(xr_in[s], 16)

            def load_weights(i):
                if i == 0:
                    sp.wait_ge(pos_masks_ready, GROUPS * BT)
                    sp.wait_ge(adj_ready, GROUPS * NC)
                for n in {0: range(RAWS), 3: range(RAWS, EXPERTS * LAYERS)}.get(i, ()):
                    e, l = n // LAYERS, n % LAYERS
                    at_least(sp, wlo_ready, n - RAWS + 1)
                    sp.dma_start(raw(n), A["w"][l][e].rearrange("(k p) f -> p k f", p=P)).then_inc(raw_in[n % RAWS], 16)

            pipeline(sp, body, load_weights)
            load_weights(3)
            for s in range(2):
                sp.wait_ge(x1_saved[s], GROUPS // 2 * 16)
            sp.wait_ge(pad_ready, 1)
            sp.dma_start(A["lists"][IDLE:LIST_ROWS, :].rearrange("(p u) f -> p u f", p=P), pad).then_inc(pads_saved, 16)
            sp.wait_ge(plan_ready, 1)
            for e in range(EXPERTS):
                end = sp.value_load(ends_i[0:1, e:e + 1], min_val=e * STRIDE, max_val=e * STRIDE + TOKENS)
                sp.dma_start(A["lists"][bass.ds(end, CHUNK), :].rearrange("(p u) f -> p u f", p=P), pad
                             ).then_inc(pads_saved, 16)
            sp.wait_ge(pads_saved, 16 * (EXPERTS + 1))

        @block.gpsimd
        def _(pool):
            pool.memset(hin[:, :, :], 0.0).then_inc(zero_ready, 1)
            pool.memset(eps[:, :], EPS).then_inc(const_zero, 1)
            pool.memset(ones[:, :], 1.0).then_inc(const_zero, 1)
            pool.memset(logits[:, :, :], -3.0e38).then_inc(const_zero, 1)
            pool.iota(iota_e[:, :], [[1, EXPERTS]], base=0, channel_multiplier=0,
                      allow_small_or_imprecise_dtypes=True).then_inc(const_zero, 1)
            pool.iota(rank[:, 1, 1, 1, :], [[STRIDE, EXPERTS]], base=0, channel_multiplier=0,
                      allow_small_or_imprecise_dtypes=True).then_inc(const_zero, 1)
            pool.iota(xrow[:, 1, :, C_TOKEN], [[P, GT]], base=-GW, channel_multiplier=1,
                      allow_small_or_imprecise_dtypes=True).then_inc(const_zero, 1)
            pool.wait_ge(const_zero, 6)
            pool.affine_select(out=tri[:, :], in_=ones[:, :], compare_op=ALU.is_gt, fill=0.0, base=0,
                               pattern=[[1, P]], channel_multiplier=-1).then_inc(const_ready, 1)

            def body(n, s, ahead):
                if runs(n):
                    for c in range(NC):
                        r = slice(c * CH, (c + 1) * CH)
                        pool.wait_ge(adj_ready, n * NC + c + 1)
                        pool.wait_ge(pos_masks_ready, n * BT + (c + 1) * CH)
                        pool.tensor_tensor(mask_neg[:, r, :], mask_neg[:, r, :].bitcast(F32),
                                           mask_pos[:, r, :].bitcast(F32), ALU.subtract).then_inc(neg_masks_ready, 1)
                if runs(n, 3):
                    m = n - 3
                    o = 1 - s
                    waits_apart(pool, pos_passed, (pos_ready, m + 1))
                    for u in range(GT):
                        for k in range(TOPK):
                            pool.indirect_dma_start(
                                A["lists"], bass.IndirectOffsetOnAxis(ap=pos[:, o, u, k:k + 1].bitcast(U32), axis=0),
                                xrow[:, o, u, :], None, bounds_check=LIST_ROWS - 1).then_inc(scattered[o], 16)
            def plan_constants(i):
                if i:
                    return
                pool.wait_ge(pos_masks_ready, GROUPS * BT)
                pool.wait_ge(adj_ready, GROUPS * NC)
                pool.memset(pad, 0.0).then_inc(pad_zero, 1)
                pool.iota(iota_m, [[CHUNK, LISTS]], base=0, channel_multiplier=0,
                          allow_small_or_imprecise_dtypes=True).then_inc(plan_consts, 1)
                pool.iota(iota_c, [[1, CHUNKS]], base=0, channel_multiplier=0,
                          allow_small_or_imprecise_dtypes=True).then_inc(plan_consts, 1)
                pool.iota(starts, [[STRIDE, EXPERTS]], base=0, channel_multiplier=0,
                          allow_small_or_imprecise_dtypes=True).then_inc(plan_consts, 1)
                pool.wait_ge(pad_zero, 1)
                pool.iota(pad[:, :, C_TOKEN], [[1, CU]], base=TOKENS, channel_multiplier=CU,
                          allow_small_or_imprecise_dtypes=True).then_inc(pad_ready, 1)
            pipeline(pool, body, plan_constants)
            for s in range(2):
                pool.wait_ge(scattered[s], GROUPS // 2 * 16 * GT * TOPK)

        @block.tensor
        def _(pe):
            def attend(n, c):
                pe.wait_ge(neg_masks_ready, n * NC + c + 1)
                if c == 0:
                    pe.wait_ge(parts_ready, n // BG * BG + AHEAD)
                    pe.wait_ge(lo_ready, (n // BG * BG + AHEAD) * 2 * GT)
                if c == NC - 1:
                    pe.wait_ge(parts_ready, (n // BG + 1) * BG)
                    pe.wait_ge(lo_ready, (n // BG + 1) * BG * 2 * GT)
                for u in range(GT):
                    if c == 0:
                        at_least(pe, att_ready, (n - 1) * GT + u + 1)
                    for j in range(c * CH, (c + 1) * CH):
                        slot = (n // BG * BT + c * CH) % SLOTS + j % CH
                        for i, (mask, acc) in enumerate(((mask_pos, u_pos[u]), (mask_neg, u_neg[u]))):
                            st = mask[:, j, u * P:(u + 1) * P]
                            pe.matmul(acc[:, 0:FEAT + 2], st, scaled[:, slot, i, 0:FEAT + 2], start=(j == 0), stop=False,
                                      skip_group_check=True)
                            last = pe.matmul(acc[:, 0:FEAT], st, scaled[:, slot, i, FEAT + 2:SW], start=False,
                                             stop=(j == BT - 1), skip_group_check=True)
                    if u == 1:
                        last.then_inc(masks_used, 1)
                    if u == 0 and c == NC - 1:
                        last.then_inc(u_ready, 1)

            def turn_rows(m, s):
                pe.wait_ge(xn_ready, (m + 1) * GT)
                at_least(pe, xT_copied, m)
                for k in range(KF):
                    for u in range(GT):
                        last = pe.transpose(ps_xT[:, k, u * P:(u + 1) * P], xrow[:, s, u, k * P:(k + 1) * P],
                                            t.ident[:, :])
                last.then_inc(xT_ready, 1)

            def router_hidden(m):
                pe.wait_ge(xT_copied, m + 1)
                at_least(pe, rh_copied, m)
                for k in range(KF):
                    last = pe.matmul(ps_rh[:, 0:GW], wr1[:, k, :], xT[:, k, :], start=(k == 0), stop=(k == KF - 1))
                last.then_inc(rh_ready, 1)

            def router_logits(m):
                pe.wait_ge(rh_copied, m + 1)
                at_least(pe, route, (m - 1) * STEPS + R_LOGITS)
                for u in range(GT):
                    last = pe.matmul(lg[:, u, 0:EXPERTS], rh[:, u * P:(u + 1) * P], wr2[:, :], start=(u == 0),
                                     stop=True, skip_group_check=True)
                last.then_inc(logits_ready, 1)

            def count_ranks(m):
                pe.wait_ge(sel_ready, m + 1)
                for i, w in enumerate((tri, ones)):
                    last = pe.matmul(ps_rk[:, i * GT * EXPERTS:(i + 1) * GT * EXPERTS], w[:, :],
                                     sel[:, :, :], start=(i == 0), stop=True, skip_group_check=True)
                last.then_inc(rank_ready, 1)

            def body(n, s, ahead):
                if runs(n, 2):
                    turn_rows(n - 2, s)
                if runs(n, 3):
                    count_ranks(n - 3)
                if runs(n):
                    attend(n, 0)
                if runs(n, 2):
                    router_hidden(n - 2)
                if runs(n):
                    attend(n, 1)
                if runs(n, 2):
                    router_logits(n - 2)
                if runs(n):
                    attend(n, 2)
                    attend(n, 3)
            pe.wait_ge(small_in, 64)
            pe.wait_ge(const_ready, 1)
            pipeline(pe, body)

        @block.scalar
        def _(act):
            act.wait_ge(const_zero, 6)
            act.wait_ge(small_in, 64)

            def scale(m, h_tile):
                for u in range(GT):
                    slot = (m * GT + u) % SLOTS
                    for i, col in enumerate((t.col_pos, t.col_neg)):
                        act.activation(scaled[:, slot, i, 0:FEAT], h_tile(u), ACT.Copy,
                                       scale=col[:, bass.ds(m * GT + u, 1)]).then_inc(hi_ready, 1)
                act.activation(scaled[:, bass.ds(m * GT % SLOTS, GT), :, FEAT:FEAT + 2],
                               t.col_parts[:, bass.ds(m * GT, GT), :, :].bitcast(F32), ACT.Copy).then_inc(parts_ready, 1)

            def spread(n, c):
                at_least(act, masks_used, (n - 1) * NC + c + 1)
                act.activation(mask_neg[:, c * CH:(c + 1) * CH, :],
                               t.adj[:, c * CH:(c + 1) * CH, bass.ds((n % BG) * GW, GW)], ACT.Copy
                               ).then_inc(adj_ready, 1)

            spread(0, 0)
            act.wait_ge(first_h_in, 32)
            for m in range(AHEAD):
                scale(m, first_h(m))

            def copy_turned(m):
                act.wait_ge(xT_ready, m + 1)
                act.activation(xT[:, :, :], ps_xT[:, :, :], ACT.Copy).then_inc(xT_copied, 1)

            def body(n, s, ahead):
                if runs(n):
                    if not first(n):
                        spread(n, 0)
                    spread(n, 1)
                if last(n) and runs(n, 2):
                    copy_turned(n - 2)
                if runs(n, 3):
                    act.wait_ge(exin_ready, n - 3 + 1)
                    act.activation(exout[:, :, :], exin[:, :, :], ACT.Exp).then_inc(exout_ready, 1)
                if runs(n, 1):
                    m = n - 1
                    for u in range(GT):
                        if u == 0:
                            act.wait_ge(u_ready, m + 1)
                            at_least(act, elu_ready, m)
                        else:
                            act.wait_ge(masks_used, (m + 1) * NC)
                        act.activation(att[:, u, :], u_pos[u][:, 0:FEAT + 2], ACT.Copy,
                                       scale=t.row_pos[:, bass.ds(m * GT + u, 1)]).then_inc(v_ready, 1)
                if runs(n, 3):
                    act.wait_ge(edif_in, n - 3 + 1)
                    act.activation(edif[:, :], prob[:, 2, :], ACT.Exp).then_inc(edif_ready, 1)
                if runs(n, 2) and not last(n):
                    copy_turned(n - 2)
                if runs(n):
                    spread(n, 2)
                    spread(n, 3)
                if runs(n, 1):
                    act.wait_ge(rden_ready, m + 1)
                    act.wait_ge(mean_added, (m + 1) * GT)
                    for u in range(GT):
                        act.activation(expo[:, u, :], att[:, u, 0:FEAT], ACT.Exp, scale=rden[:, u:u + 1]
                                       ).then_inc(expo_ready, 1)
                    act.wait_ge(expo_ready, (m + 1) * GT)
                    for u in range(GT):
                        act.activation(att[:, u, 0:FEAT], att[:, u, 0:FEAT], ACT.Relu, scale=rden[:, u:u + 1]
                                       ).then_inc(elu_pos, 1)
                if runs(n, 2):
                    act.wait_ge(rh_ready, n - 2 + 1)
                    act.activation(rh[:, :], ps_rh[:, 0:GW], ACT.Relu, bias=br1[:, 0:1]).then_inc(rh_copied, 1)
                if runs(n) and ahead:
                    act.wait_ge(masks_used, n * NC + 1)
                    act.wait_ge(h_in, (n + 1) * 16)
                    scale(n + AHEAD, later_h)
                if runs(n, 1):
                    act.wait_ge(meanvar_ready, (m + 1) * GT)
                    act.activation(std[:, :], meanvar[:, :, 1], ACT.Sqrt, bias=eps[:, 0:1]).then_inc(std_ready, 1)
            def split_hi(i):
                if i == 0:
                    act.wait_ge(masks_used, GROUPS * NC)
                for n in range(FILL[i], FILL[i + 1]):
                    act.wait_ge(raw_in[n % RAWS], (n // RAWS + 1) * 16)
                    act.activation(all_hi[:, n // LAYERS, n % LAYERS, :, :], raw(n), ACT.Copy).then_inc(whi_ready, 1)
            pipeline(act, body, split_hi)
            split_hi(3)

        @block.vector
        def _(dve):
            def scale(m, h_tile):
                dve.wait_ge(hi_ready, (m + 1) * 2 * GT)
                for u in range(GT):
                    slot = (m * GT + u) % SLOTS
                    for i, col in enumerate((t.col_pos, t.col_neg)):
                        dve.scalar_tensor_tensor(scaled[:, slot, i, FEAT + 2:SW], h_tile(u),
                                                 col[:, bass.ds(m * GT + u, 1)],
                                                 scaled[:, slot, i, 0:FEAT].bitcast(F32), ALU.mult, ALU.subtract
                                                 ).then_inc(lo_ready, 1)

            def masks_of(n, s):
                def mask(j):
                    if not runs(n):
                        return
                    if j == 0:
                        dve.wait_ge(s1_in[s], (half(n, s) + 1) * 16)
                    if j % CH == 0:
                        at_least(dve, masks_used, (n - 1) * NC + j // CH + 1)
                    dve.scalar_tensor_tensor(mask_pos[:, j, :], s1row[:, s, :],
                                             t.neg_s2[:, bass.ds(n // BG * BT + j, 1)],
                                             t.adj[:, j, bass.ds((n % BG) * GW, GW)], ALU.is_gt, ALU.mult
                                             ).then_inc(pos_masks_ready, 1)
                return mask

            for j in range(CH):
                masks_of(0, 0)(j)
            for m in range(AHEAD):
                scale(m, first_h(m))
            dve.wait_ge(lo_ready, AHEAD * 2 * GT)

            def take_out(m, s, u):
                dve.wait_ge(v_ready, m * GT + u + 1)
                dve.scalar_tensor_tensor(att[:, u, :], u_neg[u][:, 0:FEAT + 2], t.row_neg[:, bass.ds(m * GT + u, 1)],
                                         att[:, u, :], ALU.mult, ALU.add).then_inc(att_ready, 1)

            def sum_and_mean(m, s, mask):
                tile = (m % BG) * GT
                dve.wait_ge(att_ready, (m + 1) * GT)
                dve.tensor_tensor(den[:, :], att[:, :, FEAT], att[:, :, FEAT + 1], ALU.add).then_inc(den_ready, 1)
                dve.wait_ge(hm_in[s], (half(m, s) + 1) * 16)
                for u in range(GT):
                    dve.scalar_tensor_tensor(att[:, u, 0:FEAT], hmean[:, s, :], t.alone[:, bass.ds(tile + u, 1)],
                                             att[:, u, 0:FEAT], ALU.mult, ALU.add).then_inc(mean_added, 1)
                dve.wait_ge(den_ready, m + 1)
                dve.tensor_tensor(den1[:, :], den[:, :], t.alone[:, bass.ds(tile, GT)], ALU.add).then_inc(den1_ready, 1)
                mask(9)
                dve.wait_ge(den1_ready, m + 1)
                dve.reciprocal(rden[:, :], den1[:, :]).then_inc(rden_ready, 1)

            def elu(m):
                dve.wait_ge(expo_ready, (m + 1) * GT)
                dve.wait_ge(elu_pos, (m + 1) * GT)
                dve.scalar_tensor_tensor(expo[:, :, :], expo[:, :, :], 1.0, att[:, :, 0:FEAT], ALU.min, ALU.add
                                         ).then_inc(elu_ready, 1)

            def residual(m, s):
                dve.wait_ge(elu_ready, m + 1)
                dve.wait_ge(xr_in[s], (half(m, s) + 1) * 16)
                dve.scalar_tensor_tensor(xres[:, s, :, :], expo[:, :, :], -1.0, xres[:, s, :, :], ALU.add, ALU.add
                                         ).then_inc(x1_ready, 1)

            def moments(m, s):
                dve.wait_ge(x1_ready, m + 1)
                for u in range(GT):
                    dve.bn_stats(stats[:, u, :], xres[:, s, u, :]).then_inc(stats_ready, 1)
                waits_apart(dve, stats_passed, (stats_ready, (m + 1) * GT))
                for u in range(GT):
                    dve.bn_aggr(meanvar[:, u, :], stats[:, u, :]).then_inc(meanvar_ready, 1)

            def normalise(m, s, mask):
                dve.wait_ge(std_ready, m + 1)
                dve.reciprocal(rstd[:, :], std[:, :]).then_inc(rstd_ready, 1)
                mask(7)
                dve.wait_ge(rstd_ready, m + 1)
                at_least(dve, scattered[s], half(m, s) * 16 * GT * TOPK)
                for u in range(GT):
                    dve.tensor_scalar(xrow[:, s, u, 0:FEAT], xres[:, s, u, :], meanvar[:, u, 0:1], rstd[:, u:u + 1],
                                      ALU.subtract, ALU.mult).then_inc(xn_ready, 1)

            def step(m, k, ins):
                ins.then_inc(route, 1)

            def need(m, k):
                dve.wait_ge(route, m * STEPS + k)

            def choose(m, s, mask):
                mask(0)
                dve.wait_ge(logits_ready, m + 1)
                step(m, R_LOGITS, dve.tensor_tensor(
                    logits[:, :, 0:EXPERTS], lg[:, :, 0:EXPERTS],
                    br2[:, :].unsqueeze(1).to_broadcast([P, GT, EXPERTS]), ALU.add))
                mask(1)
                waits_apart(dve, route_passed, (route, m * STEPS + R_LOGITS))
                for u in range(GT):
                    step(m, R_BEST0 + u, dve.max(best[:, u, :], logits[:, u, :]))
                mask(2)
                waits_apart(dve, route_passed, (route, m * STEPS + R_BEST1))
                for u in range(GT):
                    step(m, R_IDX0 + u, dve.max_index(bidx[:, u, :], best[:, u, :], logits[:, u, :]))
                step(m, R_DIF, dve.tensor_tensor(exin[:, :, 0:EXPERTS], logits[:, :, 0:EXPERTS],
                                                 best[:, :, 0:1].to_broadcast([P, GT, EXPERTS]), ALU.subtract))
                mask(3)
                dve.wait_ge(route, m * STEPS + R_DIF)
                dve.tensor_tensor(exin[:, :, EXPERTS], best[:, :, 1], best[:, :, 0], ALU.subtract
                                  ).then_inc(exin_ready, 1)
                step(m, R_IDXF, dve.tensor_copy(idxf[:, :, :], bidx[:, :, 0:TOPK]))
                mask(4)
                need(m, R_IDXF)
                step(m, R_CHOSEN, dve.tensor_tensor(
                    chosen[:, :, :, :], idxf[:, :, :].unsqueeze(3).to_broadcast([P, GT, TOPK, EXPERTS]),
                    iota_e[:, :].unsqueeze(1).unsqueeze(1).to_broadcast([P, GT, TOPK, EXPERTS]), ALU.is_equal))
                mask(5)
                need(m, R_CHOSEN)
                dve.tensor_tensor(sel[:, :, :], chosen[:, :, 0, :], chosen[:, :, 1, :], ALU.add).then_inc(sel_ready, 1)
                mask(6)

            def weigh(m, s, mask):
                dve.wait_ge(exout_ready, m + 1)
                step(m, R_SUM, dve.tensor_reduce(prob[:, 0, :], exout[:, :, 0:EXPERTS], AX.X, ALU.add))
                mask(8)
                need(m, R_SUM)
                step(m, R_RSUM, dve.reciprocal(prob[:, 1, :], prob[:, 0, :]))
                need(m, R_RSUM)
                dve.scalar_tensor_tensor(prob[:, 2, :], exout[:, :, EXPERTS], -1.0, prob[:, 1, :], ALU.add, ALU.mult
                                         ).then_inc(edif_in, 1)

            def pair_weights(m, s, mask):
                dve.wait_ge(edif_ready, m + 1)
                step(m, R_ONE, dve.tensor_scalar(prob[:, 0, :], edif[:, :], 1.0, None, ALU.add))
                mask(10)
                need(m, R_ONE)
                step(m, R_W1, dve.reciprocal(prob[:, 3, :], prob[:, 0, :]))
                mask(11)
                need(m, R_W1)
                step(m, R_W2, dve.tensor_tensor(xrow[:, s, :, C_W2], edif[:, :], prob[:, 3, :], ALU.mult))
                dve.wait_ge(rank_ready, m + 1)
                step(m, R_RANK0, dve.tensor_tensor(
                    rank[:, s, 0, :, :], rk[:, :, 0, :],
                    rank[:, 1 - s, 1, 1, :].unsqueeze(1).to_broadcast([P, 2, EXPERTS]), ALU.add))
                mask(12)
                need(m, R_RANK0)
                step(m, R_DW, dve.tensor_tensor(xrow[:, s, :, C_DW], prob[:, 3, :], xrow[:, s, :, C_W2], ALU.subtract))
                step(m, R_RANK1, dve.tensor_tensor(
                    rank[:, s, 1, :, :], rk[:, :, 1, :],
                    rank[:, s, 0, 1, :].unsqueeze(1).to_broadcast([P, 2, EXPERTS]), ALU.add))
                step(m, R_TOK, dve.tensor_scalar(xrow[:, s, :, C_TOKEN], xrow[:, 1 - s, :, C_TOKEN], float(GW), None,
                                                 ALU.add))
                step(m, R_FIRST, dve.tensor_copy(xrow[:, s, :, C_FIRST], idxf[:, :, 0]))
                mask(13)
                mask(14)
                need(m, R_RANK1)
                step(m, R_PLACE, dve.tensor_tensor(
                    place[:, :, :, :], chosen[:, :, :, :],
                    rank[:, s, :, 0, :].unsqueeze(2).to_broadcast([P, GT, TOPK, EXPERTS]), ALU.mult))

            def position(m, s):
                need(m, R_PLACE)
                step(m, R_POSF, dve.tensor_reduce(posf[:, :, :], place[:, :, :, :], AX.X, ALU.add))

            def place_rows(m, s):
                need(m, R_POSF)
                dve.tensor_copy(pos[:, s, :, :], posf[:, :, :]).then_inc(pos_ready, 1)

            def body(n, s, ahead):
                o = 1 - s
                mask = masks_of(n, s)
                if runs(n, 3):
                    choose(n - 3, o, mask)
                else:
                    for j in range(CH if first(n) else 0, 7):
                        mask(j)
                if runs(n, 2):
                    normalise(n - 2, s, mask)
                else:
                    mask(7)
                if runs(n, 3):
                    weigh(n - 3, o, mask)
                else:
                    mask(8)
                if runs(n, 1):
                    for u in range(GT):
                        take_out(n - 1, o, u)
                    sum_and_mean(n - 1, o, mask)
                else:
                    mask(9)
                if runs(n, 3):
                    pair_weights(n - 3, o, mask)
                else:
                    for j in range(10, 15):
                        mask(j)
                mask(15)
                if runs(n, 1):
                    elu(n - 1)
                if runs(n, 3):
                    position(n - 3, o)
                if runs(n, 1):
                    residual(n - 1, o)
                if runs(n, 3):
                    place_rows(n - 3, o)
                if runs(n, 1):
                    moments(n - 1, o)
                if runs(n) and ahead:
                    scale(n + AHEAD, later_h)
            dve.wait_ge(small_in, 64)
            dve.wait_ge(const_ready, 1)
            def split_lo(i):
                for n in range(FILL[i], FILL[i + 1]):
                    w = (slice(None), n // LAYERS, n % LAYERS, slice(None), slice(None))
                    dve.wait_ge(whi_ready, n + 1)
                    dve.tensor_tensor(all_lo[w], raw(n), all_hi[w].bitcast(F32), ALU.subtract).then_inc(wlo_ready, 1)
            pipeline(dve, body, split_lo)

            def next_step(v, ins):
                ins.then_inc(plan, 1)
                dve.wait_ge(plan, v)
            dve.wait_ge(route, GROUPS * STEPS)
            dve.wait_ge(plan_consts, 3)
            next_step(1, dve.tensor_copy(ends, rank[:, 1, 1, 1, :]))
            next_step(2, dve.tensor_tensor(counts, ends, starts, ALU.subtract))
            next_step(3, dve.tensor_copy(ends_i, ends))
            wide_m = [P, EXPERTS, LISTS]
            next_step(4, dve.tensor_tensor(more, counts.unsqueeze(2).to_broadcast(wide_m),
                                           iota_m.unsqueeze(1).to_broadcast(wide_m), ALU.is_gt))
            next_step(5, dve.tensor_reduce(chunks, more, AX.X, ALU.add))
            next_step(6, dve.tensor_copy(upto[:, 0:1], chunks[:, 0:1]))
            for e in range(1, EXPERTS):
                next_step(6 + e, dve.tensor_tensor(upto[:, e:e + 1], upto[:, e - 1:e], chunks[:, e:e + 1], ALU.add))
            wide = [P, CHUNKS, EXPERTS]
            next_step(12, dve.tensor_tensor(passed, iota_c.unsqueeze(2).to_broadcast(wide),
                                            upto.unsqueeze(1).to_broadcast(wide), ALU.is_ge))
            next_step(13, dve.tensor_reduce(owners, passed, AX.X, ALU.add))
            next_step(14, dve.tensor_tensor(passed, passed, chunks.unsqueeze(1).to_broadcast(wide), ALU.mult))
            next_step(15, dve.tensor_reduce(before, passed, AX.X, ALU.add))
            next_step(16, dve.tensor_tensor(offset, iota_c, before, ALU.subtract))
            next_step(17, dve.tensor_scalar(offset, offset, float(CHUNK), None, ALU.mult))
            next_step(18, dve.scalar_tensor_tensor(base, owners, float(STRIDE), offset, ALU.mult, ALU.add))
            next_step(19, dve.tensor_scalar(base, base, float(IDLE), None, ALU.min))
            next_step(20, dve.tensor_scalar(t.owner[:, :], owners, float(EXPERTS - 1), None, ALU.min))
            next_step(21, dve.tensor_copy(t.base_i[:, :], base))
            dve.tensor_copy(t.owner_i[:, :], t.owner[:, :]).then_inc(plan_ready, 1)
            split_lo(3)


def expert_stage(nc, t, A):
    with ExitStack() as ctx:
        def sb(name, shape, dt):
            return ctx.enter_context(nc.sbuf_tensor(name, shape, dt))

        def sem(name):
            return ctx.enter_context(nc.semaphore(name))

        def psum(name, shape):
            return ctx.enter_context(nc.psum_tensor(name, shape, F32))

        M = FEAT // P
        all_hi, all_lo = expert_weights(t.arena)
        sizes = dict(s=2, h=PAIR, l=2, k=KF, f=FEAT)
        CUR = 2 * PAIR * 2 * KF * FEAT
        cur_hi = part(t.arena, 2 * WEIGHTS, "s h l k f", **sizes)
        cur_lo = part(t.arena, 2 * WEIGHTS + CUR, "s h l k f", **sizes)
        relu = sb("relu", [P, 2, CHUNK], F32)
        b3_cur = sb("b3_cur", [P, 2, PAIR, FEAT], F32)
        bias_all = sb("bias_all", [P, 2, EXPERTS, M], F32)
        bias = sb("bias", [P, 2, PAIR, 2, M], F32)
        b3 = sb("b3", [P, EXPERTS, FEAT], F32)
        kept = t.bytes[:, :].bitcast(F32)
        rows = part(kept, 0, "s h u f", s=2, h=PAIR, u=CU, f=ROW)
        def blocks(name):
            return [sb(f"{name}{h}", [P, KF, CHUNK], F32R) for h in range(PAIR)]
        x_hi = [part(t.arena, 2 * (WEIGHTS + CUR), "k r", k=KF, r=CHUNK), sb("x_hi1", [P, KF, CHUNK], F32R)]
        x_lo = [part(t.arena, 2 * (WEIGHTS + CUR) + KF * CHUNK, "k r", k=KF, r=CHUNK), sb("x_lo1", [P, KF, CHUNK], F32R)]
        a1_hi, a1_lo, a2_hi, a2_lo = (blocks(name) for name in ("a1_hi", "a1_lo", "a2_hi", "a2_lo"))
        y = part(kept, ROWS_SIZE, "s h u f", s=2, h=PAIR, u=CU, f=FEAT)
        first = sb("first", [P, 2, PAIR, CU], F32)
        weight = sb("weight", [P, 2, PAIR, CU], F32)
        token = sb("token", [P, 2, PAIR, CU], I32)
        ps_x = [psum(f"ps_x{k}", [P, CHUNK]) for k in range(KF)]
        ps_a = [[psum(f"ps_a{h}{m}", [P, CHUNK]) for m in range(M)] for h in range(PAIR)]
        ps_y = [psum(f"ps_y{i}", [P, 2, FEAT]) for i in range(CU // 2)]

        biases_in = sem("biases_in")
        rows_in = [sem(f"rows_in{i}") for i in range(2)]
        cur_ready = sem("cur_ready")
        bias_ready = sem("bias_ready")
        b3_ready = sem("b3_ready")
        x_turned = sem("x_turned")
        xhi_ready = sem("xhi3_ready")
        xlo_ready = sem("xlo3_ready")
        z_ready = sem("z_ready")
        relu_ready = sem("relu_ready")
        ahi_ready = sem("ahi_ready")
        alo_ready = sem("alo_ready")
        first_ready = sem("first_ready")
        weight_ready = sem("weight_ready")
        token_ready = sem("token_ready")
        out_ready = sem("out_ready")
        y_scaled = sem("y_scaled")
        y_ready = sem("y_ready")
        added = sem("added")
        add_passed = sem("add_passed")
        load_passed = sem("load_passed")

        ZC = 2 * PAIR * M
        TU = PAIR * CU

        block = ctx.enter_context(nc.Block())

        def turns(eng, body):
            body(0, 0)
            body(1, 1)
            with eng.Fori(1, (TURNS - 1) // 2) as i:
                body(i * 2, 0)
                body(i * 2 + 1, 1)
            for c in range((TURNS - 1) // 2 * 2, TURNS):
                body(c, c % 2)

        def follows(c):
            return not isinstance(c, int) or c + 1 < TURNS

        def half(c, s):
            return (c - s) // 2

        @block.sync
        def _(sp):
            def turn(c, s):
                starts_at = [sp.value_load(t.base_i[0:1, bass.ds(c * PAIR + h, 1)], min_val=0, max_val=IDLE)
                             for h in range(PAIR)]
                waits_apart(sp, load_passed, (token_ready, (c - 1) * PAIR))
                waits_apart(sp, load_passed, (x_turned, (c - 1) * PAIR))
                for h in range(PAIR):
                    sp.dma_start(rows[:, s, h, :, :],
                                 A["lists"][bass.ds(starts_at[h], CHUNK), :].rearrange("(p u) f -> p u f", p=P)
                                 ).then_inc(rows_in[s], 16)
            turns(sp, turn)

        @block.gpsimd
        def _(pool):
            pool.wait_ge(rows_in[0], 16 * PAIR)
            with nc.allow_non_contiguous_dma(reason="biases, one number for each partition"):
                pool.dma_start(bias_all[:, 0, :, :], A["b1"].rearrange("e (m p) -> p e m", p=P)).then_inc(biases_in, 16)
                pool.dma_start(bias_all[:, 1, :, :], A["b2"].rearrange("e (m p) -> p e m", p=P)).then_inc(biases_in, 16)
            pool.dma_start(b3[:, :, :], A["b3"].rearrange("(one e) f -> one e f", one=1).to_broadcast([P, EXPERTS, FEAT])
                         ).then_inc(biases_in, 16)
            def turn(c, s):
                for h in range(PAIR):
                    waits_apart(pool, add_passed, (token_ready, c * PAIR + h + 1))
                    for u in range(CU):
                        waits_apart(pool, add_passed, (y_ready, c * TU + h * CU + u + 1),
                                    (added, (c * PAIR + h) * CU * 16))
                        pool.indirect_dma_start(
                            A["out"], bass.IndirectOffsetOnAxis(ap=token[:, s, h, u:u + 1].bitcast(U32), axis=0),
                            y[:, s, h, u, :], None, bounds_check=OUT_ROWS - 1, compute_op=ALU.add).then_inc(added, 16)
            turns(pool, turn)
            pool.wait_ge(added, CHUNKS * CU * 16)

        @block.tensor
        def _(pe):
            def turn_rows(c, s, h):
                at_least(pe, xlo_ready, c * PAIR + h)
                if h == 0:
                    pe.wait_ge(rows_in[s], (half(c, s) + 1) * 16 * PAIR)
                for k in range(KF):
                    for u in range(CU):
                        last = pe.transpose(ps_x[k][:, u * P:(u + 1) * P], rows[:, s, h, u, k * P:(k + 1) * P],
                                            t.ident[:, :])
                last.then_inc(x_turned, 1)

            def layer(c, s, l, h):
                if l == 0:
                    a_hi, a_lo = x_hi[h], x_lo[h]
                    pe.wait_ge(xlo_ready, c * PAIR + h + 1)
                    pe.wait_ge(cur_ready, (c * PAIR + h + 1) * 2)
                else:
                    a_hi, a_lo = a1_hi[h], a1_lo[h]
                    pe.wait_ge(alo_ready, c * ZC + (h + 1) * M)
                for m in range(M):
                    at_least(pe, ahi_ready, c * ZC + (l - 1) * PAIR * M + h * M + m + 1)
                    products = [(w[:, s, h, l, k, m * P:(m + 1) * P], a[:, k, :]) for w, a in
                                ((cur_hi, a_hi), (cur_lo, a_hi), (cur_hi, a_lo)) for k in range(KF)]
                    for i, (w, a) in enumerate(products):
                        last = pe.matmul(ps_a[h][m][:, :], w, a, start=(i == 0), stop=(i == len(products) - 1))
                    last.then_inc(z_ready, 1)

            def last_layer(c, s, h, e):
                pe.wait_ge(alo_ready, c * ZC + (PAIR + h + 1) * M)
                for u in range(CU):
                    n = c * TU + h * CU + u
                    if u % 2 == 0:
                        at_least(pe, y_scaled, n - CU + 2)
                    tok = slice(u * P, (u + 1) * P)
                    products = [(a[h][:, k, tok], w[:, bass.ds(e, 1), 2, k, :].squeeze(1)) for a, w in
                                ((a2_hi, all_hi), (a2_hi, all_lo), (a2_lo, all_hi)) for k in range(KF)]
                    for i, (a, w) in enumerate(products):
                        last = pe.matmul(ps_y[u // 2][:, u % 2, :], a, w, start=(i == 0 and u % 2 == 0),
                                         stop=(i == len(products) - 1), skip_group_check=True)
                    last.then_inc(out_ready, 1)

            def turn(c, s):
                experts = [pe.value_load(t.owner_i[0:1, bass.ds(c * PAIR + h, 1)], min_val=0, max_val=EXPERTS - 1)
                           for h in range(PAIR)]
                for l in range(2):
                    for h in range(PAIR):
                        layer(c, s, l, h)
                for h in range(PAIR):
                    if follows(c):
                        turn_rows(c + 1, 1 - s, h)
                    last_layer(c, s, h, experts[h])

            for h in range(PAIR):
                turn_rows(0, 0, h)
            turns(pe, turn)

        @block.scalar
        def _(act):
            def split_rows(c, h):
                act.wait_ge(x_turned, c * PAIR + h + 1)
                for k in range(KF):
                    last = act.activation(x_hi[h][:, k, :], ps_x[k][:, :], ACT.Copy)
                last.then_inc(xhi_ready, 1)

            def turn(c, s):
                act.wait_ge(bias_ready, (c + 1) * PAIR)
                for l, a_hi in enumerate((a1_hi, a2_hi)):
                    for h in range(PAIR):
                        for m in range(M):
                            i = (l * PAIR + h) * M + m
                            act.wait_ge(z_ready, c * ZC + i + 1)
                            at_least(act, alo_ready, c * ZC + i - 1)
                            act.activation(relu[:, i % 2, :], ps_a[h][m][:, :], ACT.Relu,
                                           bias=bias[:, s, h, l, m:m + 1]).then_inc(relu_ready, 1)
                            act.activation(a_hi[h][:, m, :], ps_a[h][m][:, :], ACT.Relu,
                                           bias=bias[:, s, h, l, m:m + 1]).then_inc(ahi_ready, 1)
                for h in range(PAIR):
                    if follows(c):
                        split_rows(c + 1, h)
                    act.wait_ge(weight_ready, c * PAIR + h + 1)
                    for u in range(CU):
                        n = c * TU + h * CU + u
                        if u % 2 == 0:
                            act.wait_ge(out_ready, n + 2)
                        if h == 0 and u == 0:
                            at_least(act, added, (c - 1) * TU * 16)
                        act.activation(y[:, s, h, u, :], ps_y[u // 2][:, u % 2, :], ACT.Copy,
                                       scale=weight[:, s, h, u:u + 1]).then_inc(y_scaled, 1)
            for h in range(PAIR):
                split_rows(0, h)
            turns(act, turn)

        @block.vector
        def _(dve):

            def expert_of(c, h):
                return dve.value_load(t.owner_i[0:1, bass.ds(c * PAIR + h, 1)], min_val=0, max_val=EXPERTS - 1)

            def take_matrices(c, s, h, e, part):
                cur, whole = ((cur_hi, all_hi), (cur_lo, all_lo))[part]
                if h == 0 and part == 0:
                    at_least(dve, z_ready, (c - 1) * ZC)
                dve.tensor_copy(cur[:, s, h, :, :, :], whole[:, bass.ds(e, 1), 0:2, :, :].squeeze(1).bitcast(F32)
                                ).then_inc(cur_ready, 1)

            def take_biases(c, s, experts):
                at_least(dve, ahi_ready, (c - 1) * ZC)
                for h, e in enumerate(experts):
                    dve.tensor_copy(bias[:, s, h, :, :], bias_all[:, :, bass.ds(e, 1), :].squeeze(2)).then_inc(bias_ready, 1)
                    dve.tensor_copy(b3_cur[:, s, h, :], b3[:, bass.ds(e, 1), :].squeeze(1)).then_inc(b3_ready, 1)

            def take_weights(c, s):
                dve.wait_ge(rows_in[s], (half(c, s) + 1) * 16 * PAIR)
                for h in range(PAIR):
                    q = c * PAIR + h
                    dve.tensor_scalar(first[:, s, h, :], rows[:, s, h, :, C_FIRST], t.owner[:, bass.ds(q, 1)], None,
                                      ALU.is_equal).then_inc(first_ready, 1)
                dve.wait_ge(first_ready, (2 * c + 1) * PAIR)
                dve.tensor_tensor(first[:, s, :, :], first[:, s, :, :], rows[:, s, :, :, C_DW], ALU.mult
                                  ).then_inc(first_ready, PAIR)
                dve.wait_ge(first_ready, (2 * c + 2) * PAIR)
                at_least(dve, y_scaled, (c - 1) * TU)
                dve.tensor_tensor(weight[:, s, :, :], first[:, s, :, :], rows[:, s, :, :, C_W2], ALU.add
                                  ).then_inc(weight_ready, PAIR)
                at_least(dve, added, (c - 1) * TU * 16)
                dve.tensor_copy(token[:, s, :, :], rows[:, s, :, :, C_TOKEN]).then_inc(token_ready, PAIR)

            def split_rows(c, h):
                dve.wait_ge(xhi_ready, c * PAIR + h + 1)
                for k in range(KF):
                    last = dve.tensor_tensor(x_lo[h][:, k, :], ps_x[k][:, :], x_hi[h][:, k, :].bitcast(F32), ALU.subtract)
                last.then_inc(xlo_ready, 1)

            def turn(c, s):
                experts = []
                for l, (a_hi, a_lo) in enumerate(((a1_hi, a1_lo), (a2_hi, a2_lo))):
                    for h in range(PAIR):
                        for m in range(M):
                            i = (l * PAIR + h) * M + m
                            dve.wait_ge(ahi_ready, c * ZC + i + 1)
                            dve.tensor_tensor(a_lo[h][:, m, :], relu[:, i % 2, :], a_hi[h][:, m, :].bitcast(F32),
                                              ALU.subtract).then_inc(alo_ready, 1)
                            if follows(c) and l == 0 and m == 1:
                                experts.append(expert_of(c + 1, h))
                            if follows(c) and l == 1:
                                take_matrices(c + 1, 1 - s, h, experts[h], m)
                for h in range(PAIR):
                    if follows(c):
                        split_rows(c + 1, h)
                    if h == 0:
                        dve.wait_ge(b3_ready, (c + 1) * PAIR)
                    for u in range(CU):
                        dve.wait_ge(y_scaled, c * TU + h * CU + u + 1)
                        dve.scalar_tensor_tensor(y[:, s, h, u, :], b3_cur[:, s, h, :], weight[:, s, h, u:u + 1],
                                                 y[:, s, h, u, :], ALU.mult, ALU.add).then_inc(y_ready, 1)
                if follows(c):
                    take_biases(c + 1, 1 - s, experts)
                    take_weights(c + 1, 1 - s)
            experts = [expert_of(0, h) for h in range(PAIR)]
            for h in range(PAIR):
                for part in range(2):
                    take_matrices(0, 0, h, experts[h], part)
            for h in range(PAIR):
                split_rows(0, h)
            dve.wait_ge(biases_in, 48)
            take_biases(0, 0, experts)
            take_weights(0, 0)
            turns(dve, turn)


class Kept:
    pass


def build(nc, A):
    with ExitStack() as ctx:
        def sb(name, shape, dt):
            return ctx.enter_context(nc.sbuf_tensor(name, shape, dt))
        k = Kept()
        k.ident = sb("ident", [P, P], F32)
        k.owner = sb("owner", [P, CHUNKS], F32)
        k.owner_i = sb("owner_i", [P, CHUNKS], I32)
        k.base_i = sb("base_i", [P, CHUNKS], I32)
        k.bytes = sb("bytes", [P, 4 * (ROWS_SIZE + Y_SIZE)], U8)
        k.adj = k.bytes[:, 0:BT * NODES].rearrange("p (k i) -> p k i", k=BT)
        k.col_pos = sb("col_pos", [P, TILES], F32)
        k.col_neg = sb("col_neg", [P, TILES], F32)
        k.row_pos = sb("row_pos", [P, TILES], F32)
        k.row_neg = sb("row_neg", [P, TILES], F32)
        k.neg_s2 = sb("neg_s2", [P, TILES], F32)
        k.alone = sb("alone", [P, BT], F32)
        k.col_parts = sb("col_parts", [P, TILES, 2, 2], F32R)
        project_stage(nc, k, A)
        k.arena = sb("arena", [P, ARENA], F32R)
        attend_stage(nc, k, A)
        expert_stage(nc, k, A)


_INS = [("x", (TOKENS, FEAT), F32), ("adjT", (NODES, NODES), I32), ("L0_gnn_W", (FEAT, FEAT), F32),
        ("L0_gnn_a", (2 * FEAT, 1), F32), ("L0_ffn_router_w1", (FEAT, RH), F32), ("L0_ffn_router_b1", (RH,), F32),
        ("L0_ffn_router_w2", (RH, EXPERTS), F32), ("L0_ffn_router_b2", (EXPERTS,), F32)]
_INS += [(f"L0_ffn_expert_w{i}", (EXPERTS, FEAT, FEAT), F32) for i in (1, 2, 3)]
_INS += [(f"L0_ffn_expert_b{i}", (EXPERTS, FEAT), F32) for i in (1, 2, 3)]


def kernel(**inputs):
    import concourse.bacc as bacc
    from concourse.bass_utils import run_bass_kernel_spmd as run

    nc = bacc.Bacc("TRN2", target_bir_lowering=False, num_devices=1)
    arrays, args = {}, {}
    for name, shape, dt in _INS:
        v = np.asarray(inputs["adj"]).T if name == "adjT" else inputs[name]
        arrays[name] = np.ascontiguousarray(v).reshape(shape)
        args[name] = nc.dram_tensor(name, shape, dt, kind="ExternalInput").ap()
    out = nc.dram_tensor("out", (OUT_ROWS, FEAT), F32, kind="ExternalOutput").ap()
    tokens = "(n u p) f -> n p u f"
    A = {
        "x": args["x"].rearrange(tokens, u=GT, p=P),
        "x_blocks": args["x"].rearrange("(k g p) f -> k p g f", g=XG * GT, p=P),
        "adjT": args["adjT"].rearrange("(k p) i -> k p i", p=P),
        "W": args["L0_gnn_W"], "a": args["L0_gnn_a"], "out": out,
        "x1": out[0:TOKENS, :].rearrange(tokens, u=GT, p=P),
        "out_pad": out[TOKENS:OUT_ROWS, :].rearrange("(i u p) f -> i p u f", u=GT, p=P),
        "router_w1": args["L0_ffn_router_w1"], "router_b1": args["L0_ffn_router_b1"],
        "router_w2": args["L0_ffn_router_w2"], "router_b2": args["L0_ffn_router_b2"],
        "w": [args[f"L0_ffn_expert_w{i}"] for i in (1, 2, 3)], "b1": args["L0_ffn_expert_b1"],
        "b2": args["L0_ffn_expert_b2"], "b3": args["L0_ffn_expert_b3"],
        "lists": nc.dram_tensor("lists", (LIST_ROWS, ROW), F32, kind="Internal").ap(),
        "h": nc.dram_tensor("h", (GROUPS, P, GT, FEAT), F32, kind="Internal").ap(),
    }
    s1 = nc.dram_tensor("s1_rows", (TOKENS,), F32, kind="Internal").ap()
    A["s1_save"] = s1.rearrange("(t p) -> t p", p=P)
    A["s1_rows"] = s1.rearrange("(n one i) -> n one i", one=1, i=GW)
    A["hmean_rows"] = nc.dram_tensor("hmean_rows", (BATCH, 1, FEAT), F32, kind="Internal").ap()
    build(nc, A)
    r = run(nc, [arrays], core_ids=[0])
    return r.results[0]["out"][:TOKENS].reshape(BATCH, NODES, FEAT)
```
